# Optimizing a Trainium2 kernel written in Bass

```python
import numpy as np
import jax
import jax.numpy as jnp

def _softmax(x, axis=-1):
    return jax.nn.softmax(x, axis=axis)

def _gelu(x):
    return jax.nn.gelu(x, approximate=True)

def _silu(x):
    return jax.nn.silu(x)

def _sigmoid(x):
    return jax.nn.sigmoid(x)

def _layernorm(x, axis=-1, eps=1e-05):
    m = jnp.mean(x, axis=axis, keepdims=True)
    v = jnp.var(x, axis=axis, keepdims=True)
    return (x - m) / jnp.sqrt(v + eps)

def _scatter_add(tgt, idx, src, axis=0):
    return tgt.at[idx].add(src)

def _segment_sum(src, seg, n):
    return jax.ops.segment_sum(src, seg, n)
kernel_name = 'mk_sandwich_d1_jaxref_r8_c51f67'

def setup_inputs(seed: int=0):
    np.random.seed(seed)
    _w = jnp.asarray

    def _L0_attn_setup():
        import jax, jax.numpy as jnp
        import numpy as np
        HID = 256
        H = 16
        D_NOPE = 128
        D_ROPE = 64
        D_Q = D_NOPE + D_ROPE
        D_V = 128
        QR = 192
        KVR = 64
        PH = 16
        PD = HID // PH
        THETA = 10000.0
        EPS = 1e-06

        def rmsnorm(x, w):
            var = jnp.mean(jnp.square(x), axis=-1, keepdims=True)
            return x * jax.lax.rsqrt(var + EPS) * w

        def rope_cos_sin(seq_len):
            inv_freq = 1.0 / THETA ** (jnp.arange(0, D_ROPE, 2, dtype=jnp.float32) / D_ROPE)
            t = jnp.arange(seq_len, dtype=jnp.float32)
            freqs = jnp.outer(t, inv_freq)
            emb = jnp.concatenate([freqs, freqs], -1)
            return (jnp.cos(emb), jnp.sin(emb))

        def rotate_half(x):
            x1, x2 = jnp.split(x, 2, axis=-1)
            return jnp.concatenate([-x2, x1], axis=-1)

        def apply_rope(x, cos, sin):
            return x * cos[None, None] + rotate_half(x) * sin[None, None]
        key = jax.random.key(seed)
        ks = jax.random.split(key, 12)

        def w(k, shape):
            return (jax.random.normal(k, shape, jnp.float32) / np.sqrt(shape[-1])).astype(jnp.float32)
        B, S = (2, 128)
        return {'hidden_states': jax.random.normal(ks[0], (B, S, HID), jnp.float32), 'q_a_w': w(ks[1], (QR, HID)), 'q_a_ln_w': jnp.ones((QR,), jnp.float32), 'q_b_w': w(ks[2], (H * D_Q, QR)), 'kv_a_w': w(ks[3], (KVR + H * D_ROPE, HID)), 'kv_a_ln_w': jnp.ones((KVR,), jnp.float32), 'kv_b_w': w(ks[4], (H * (D_NOPE + D_V), KVR)), 'o_w': w(ks[5], (HID, H * D_V)), 'sp_q_w': w(ks[6], (HID, HID)), 'sp_k_w': w(ks[7], (HID, HID)), 'sp_v_w': w(ks[8], (HID, HID)), 'sp_o_w': w(ks[9], (HID, HID)), 'gate_w': w(ks[10], (2, HID)), 'gate_b': jnp.zeros((2,), jnp.float32)}
    _L0_attn_in = _L0_attn_setup()

    def _L0_ffn_setup():
        import jax, jax.numpy as jnp
        import numpy as np
        BLOCK_SIZE = 32
        FP4_GRID = jnp.array([0.0, 0.5, 1.0, 1.5, 2.0, 3.0, 4.0, 6.0], dtype=jnp.float32)
        FP4_MIDS = jnp.array([0.25, 0.75, 1.25, 1.75, 2.5, 3.5, 5.0], dtype=jnp.float32)

        def quantize_to_mxfp4(w, block_size=BLOCK_SIZE):
            K, N = w.shape
            wb = w.reshape(K // block_size, block_size, N)
            amax = jnp.max(jnp.abs(wb), axis=1, keepdims=True)
            exp = jnp.floor(jnp.log2(jnp.maximum(amax, 1e-30))) - 2.0
            scales = jnp.exp2(exp)
            x = wb / scales
            idx = jnp.digitize(jnp.abs(x), FP4_MIDS)
            q = jnp.sign(x) * FP4_GRID[idx]
            return (q, scales)

        def mxfp4_matmul(inputs, q, scales, block_size=BLOCK_SIZE):
            K = inputs.shape[-1]
            N = q.shape[-1]
            w = (q * scales).reshape(K, N)
            return inputs @ w
        key = jax.random.key(seed)
        ks = jax.random.split(key, 3)
        B, S, D, F = (4, 256, 256, 1024)
        inputs = jax.random.normal(ks[0], (B, S, D), dtype=jnp.float32)
        up_kernel = jax.random.normal(ks[1], (D, F), dtype=jnp.float32) * (1.0 / np.sqrt(D))
        down_kernel = jax.random.normal(ks[2], (F, D), dtype=jnp.float32) * (1.0 / np.sqrt(F))
        up_bias = jnp.zeros((F,), dtype=jnp.float32)
        down_bias = jnp.zeros((D,), dtype=jnp.float32)
        return {'inputs': inputs, 'up_kernel': up_kernel, 'up_bias': up_bias, 'down_kernel': down_kernel, 'down_bias': down_bias}
    _L0_ffn_in = _L0_ffn_setup()
    _d = {'L0_attn_hidden_states': _L0_attn_in['hidden_states'], 'L0_attn_q_a_w': _L0_attn_in['q_a_w'], 'L0_attn_q_a_ln_w': _L0_attn_in['q_a_ln_w'], 'L0_attn_q_b_w': _L0_attn_in['q_b_w'], 'L0_attn_kv_a_w': _L0_attn_in['kv_a_w'], 'L0_attn_kv_a_ln_w': _L0_attn_in['kv_a_ln_w'], 'L0_attn_kv_b_w': _L0_attn_in['kv_b_w'], 'L0_attn_o_w': _L0_attn_in['o_w'], 'L0_attn_sp_q_w': _L0_attn_in['sp_q_w'], 'L0_attn_sp_k_w': _L0_attn_in['sp_k_w'], 'L0_attn_sp_v_w': _L0_attn_in['sp_v_w'], 'L0_attn_sp_o_w': _L0_attn_in['sp_o_w'], 'L0_attn_gate_w': _L0_attn_in['gate_w'], 'L0_attn_gate_b': _L0_attn_in['gate_b'], 'L0_ffn_up_kernel': _L0_ffn_in['up_kernel'], 'L0_ffn_up_bias': _L0_ffn_in['up_bias'], 'L0_ffn_down_kernel': _L0_ffn_in['down_kernel'], 'L0_ffn_down_bias': _L0_ffn_in['down_bias']}
    _x0 = _d['L0_attn_hidden_states']
    _d['L0_attn_hidden_states'] = jax.random.normal(jax.random.fold_in(jax.random.key(seed), 1), (1, 1024, 256), dtype=_x0.dtype)
    del _x0
    return _d

def reference(L0_attn_hidden_states, L0_attn_q_a_w, L0_attn_q_a_ln_w, L0_attn_q_b_w, L0_attn_kv_a_w, L0_attn_kv_a_ln_w, L0_attn_kv_b_w, L0_attn_o_w, L0_attn_sp_q_w, L0_attn_sp_k_w, L0_attn_sp_v_w, L0_attn_sp_o_w, L0_attn_gate_w, L0_attn_gate_b, L0_ffn_up_kernel, L0_ffn_up_bias, L0_ffn_down_kernel, L0_ffn_down_bias):

    def _L0_attn_ref(hidden_states, q_a_w, q_a_ln_w, q_b_w, kv_a_w, kv_a_ln_w, kv_b_w, o_w, sp_q_w, sp_k_w, sp_v_w, sp_o_w, gate_w, gate_b):
        import jax, jax.numpy as jnp
        import numpy as np
        HID = 256
        H = 16
        D_NOPE = 128
        D_ROPE = 64
        D_Q = D_NOPE + D_ROPE
        D_V = 128
        QR = 192
        KVR = 64
        PH = 16
        PD = HID // PH
        THETA = 10000.0
        EPS = 1e-06

        def rmsnorm(x, w):
            var = jnp.mean(jnp.square(x), axis=-1, keepdims=True)
            return x * jax.lax.rsqrt(var + EPS) * w

        def rope_cos_sin(seq_len):
            inv_freq = 1.0 / THETA ** (jnp.arange(0, D_ROPE, 2, dtype=jnp.float32) / D_ROPE)
            t = jnp.arange(seq_len, dtype=jnp.float32)
            freqs = jnp.outer(t, inv_freq)
            emb = jnp.concatenate([freqs, freqs], -1)
            return (jnp.cos(emb), jnp.sin(emb))

        def rotate_half(x):
            x1, x2 = jnp.split(x, 2, axis=-1)
            return jnp.concatenate([-x2, x1], axis=-1)

        def apply_rope(x, cos, sin):
            return x * cos[None, None] + rotate_half(x) * sin[None, None]
        b, s, _ = hidden_states.shape
        dt = hidden_states.dtype
        q_mid = rmsnorm(hidden_states @ q_a_w.T, q_a_ln_w)
        q = (q_mid @ q_b_w.T).reshape(b, s, H, D_Q).transpose(0, 2, 1, 3)
        q_nope, q_pe = (q[..., :D_NOPE], q[..., D_NOPE:])
        kv_a = hidden_states @ kv_a_w.T
        kv_lora, k_pe_flat = (kv_a[..., :KVR], kv_a[..., KVR:])
        k_pe = k_pe_flat.reshape(b, s, H, D_ROPE).transpose(0, 2, 1, 3)
        kv = rmsnorm(kv_lora, kv_a_ln_w) @ kv_b_w.T
        kv = kv.reshape(b, s, H, D_NOPE + D_V).transpose(0, 2, 1, 3)
        k_nope, v = (kv[..., :D_NOPE], kv[..., D_NOPE:])
        cos, sin = rope_cos_sin(s)
        q_pe = apply_rope(q_pe, cos, sin)
        k_pe = apply_rope(k_pe, cos, sin)
        qf = jnp.concatenate([q_nope, q_pe], -1)
        kf = jnp.concatenate([k_nope, k_pe], -1)
        scale = D_Q ** (-0.5)
        scores = jnp.einsum('bhqd,bhkd->bhqk', qf, kf) * scale
        probs = jax.nn.softmax(scores.astype(jnp.float32), axis=-1).astype(dt)
        ctx = jnp.einsum('bhqk,bhkd->bhqd', probs, v)
        main_out = ctx.transpose(0, 2, 1, 3).reshape(b, s, H * D_V) @ o_w.T

        def split_heads(x):
            return x.reshape(b, s, PH, PD).transpose(0, 2, 1, 3)
        pq = split_heads(hidden_states @ sp_q_w.T)
        pk = split_heads(hidden_states @ sp_k_w.T)
        pv = split_heads(hidden_states @ sp_v_w.T)
        p_scores = jnp.einsum('bhqd,bhkd->bhqk', pq, pk) * PD ** (-0.5)
        p_probs = jax.nn.softmax(p_scores.astype(jnp.float32), axis=-1).astype(dt)
        p_ctx = jnp.einsum('bhqk,bhkd->bhqd', p_probs, pv)
        pattern_out = p_ctx.transpose(0, 2, 1, 3).reshape(b, s, HID) @ sp_o_w.T
        gates = jax.nn.softmax(hidden_states @ gate_w.T + gate_b, axis=-1)
        return gates[..., 0:1] * main_out + gates[..., 1:2] * pattern_out

    def _L0_ffn_ref(inputs, up_kernel, up_bias, down_kernel, down_bias):
        import jax, jax.numpy as jnp
        import numpy as np
        BLOCK_SIZE = 32
        FP4_GRID = jnp.array([0.0, 0.5, 1.0, 1.5, 2.0, 3.0, 4.0, 6.0], dtype=jnp.float32)
        FP4_MIDS = jnp.array([0.25, 0.75, 1.25, 1.75, 2.5, 3.5, 5.0], dtype=jnp.float32)

        def quantize_to_mxfp4(w, block_size=BLOCK_SIZE):
            K, N = w.shape
            wb = w.reshape(K // block_size, block_size, N)
            amax = jnp.max(jnp.abs(wb), axis=1, keepdims=True)
            exp = jnp.floor(jnp.log2(jnp.maximum(amax, 1e-30))) - 2.0
            scales = jnp.exp2(exp)
            x = wb / scales
            idx = jnp.digitize(jnp.abs(x), FP4_MIDS)
            q = jnp.sign(x) * FP4_GRID[idx]
            return (q, scales)

        def mxfp4_matmul(inputs, q, scales, block_size=BLOCK_SIZE):
            K = inputs.shape[-1]
            N = q.shape[-1]
            w = (q * scales).reshape(K, N)
            return inputs @ w
        q_up, s_up = quantize_to_mxfp4(up_kernel, BLOCK_SIZE)
        x = mxfp4_matmul(inputs, q_up, s_up, BLOCK_SIZE) + up_bias
        x = jax.nn.gelu(x)
        q_dn, s_dn = quantize_to_mxfp4(down_kernel, BLOCK_SIZE)
        x = mxfp4_matmul(x, q_dn, s_dn, BLOCK_SIZE) + down_bias
        return x
    x = L0_attn_hidden_states
    x = x + _layernorm(_L0_attn_ref(_layernorm(x, axis=-1), L0_attn_q_a_w, L0_attn_q_a_ln_w, L0_attn_q_b_w, L0_attn_kv_a_w, L0_attn_kv_a_ln_w, L0_attn_kv_b_w, L0_attn_o_w, L0_attn_sp_q_w, L0_attn_sp_k_w, L0_attn_sp_v_w, L0_attn_sp_o_w, L0_attn_gate_w, L0_attn_gate_b), axis=-1)
    x = x + _layernorm(_L0_ffn_ref(_layernorm(x, axis=-1), L0_ffn_up_kernel, L0_ffn_up_bias, L0_ffn_down_kernel, L0_ffn_down_bias), axis=-1)
    return x

_drawn_inputs = setup_inputs


def setup_inputs(seed=0):
    import zlib

    import numpy as np

    out = dict(_drawn_inputs(seed))
    spreads = {'L0_attn_q_a_ln_w': (1.0, 0.2),
     'L0_attn_kv_a_ln_w': (1.0, 0.2),
     'L0_attn_gate_b': (0.0, 0.539),
     'L0_ffn_up_bias': (0.0, 0.1),
     'L0_ffn_down_bias': (0.0, 0.1)}
    factors = {}
    for name, (base, spread) in spreads.items():
        noise = np.random.default_rng([zlib.crc32(name.encode()), seed]).standard_normal(out[name].shape)
        drawn = base * np.exp(spread * noise) if base else spread * noise
        out[name] = jnp.asarray(drawn.astype(out[name].dtype))
    for name, factor in factors.items():
        out[name] = (out[name] * factor).astype(out[name].dtype)
    return out
```

```python
from contextlib import ExitStack
from itertools import islice

import numpy as np

import concourse.bass as bass
from concourse import mybir

F32 = mybir.dt.float32
F32R = mybir.dt.float32r
I32 = mybir.dt.int32
ALU = mybir.AluOpType
ACT = mybir.ActivationFunctionType
AX = mybir.AxisListType.X

P = 128
S, HID = 1024, 256
H, NOPE, ROPE, DV = 16, 128, 64, 128
DQ = NOPE + ROPE
QR, LAT = 192, 64
PH, PD = 16, 16
F = 1024
NT = S // P
NK = HID // P
NP = H // 2
HALF = 512
W1 = QR + LAT + 2
MAIN_SCALE = float(DQ) ** -0.5
PAT_SCALE = float(PD) ** -0.5
NW = 12



def prologue(nc, a, d, g):
    jobs = [("xT", k, q) for k in range(NK) for q in range(2)]
    jobs += [("w1T", k) for k in range(NK)]
    jobs += [("proj1", t) for t in range(NT)]
    jobs += [("spT", w) for w in range(3)]
    jobs += [("kpT", k, q) for k in range(NK) for q in range(2)]
    jobs += [("pe0T", q) for q in range(2)] + [("pe1T", q) for q in range(2)]
    jobs += [("lat0", q) for q in range(2)] + [("lat1", q) for q in range(2)]
    jobs += [("spqk", w, m, h) for w in range(2) for m in range(2) for h in range(2)]
    jobs += [("spv", q) for q in range(NT // 2)]
    jobs += [("qm0T", q) for q in range(2)] + [("qm1T", q) for q in range(2)]
    jobs += [("cT", q) for q in range(2)]
    split = ("spqk", "qm0T", "qm1T")
    by_act = [j[0] not in split and j[0] != "cT" and n % 2 == 0 for n, j in enumerate(jobs)]
    index = {j: n for n, j in enumerate(jobs)}

    first_spqk = index[("spqk", 0, 0, 0)]

    def last(kind):
        return max(n for n, j in enumerate(jobs) if j[0] == kind)

    with ExitStack() as ctx:
        def sb(name, shape, dt=F32):
            return ctx.enter_context(nc.sbuf_tensor(name, shape, dt))

        def sem(name):
            return ctx.enter_context(nc.semaphore(name))

        bank = [ctx.enter_context(nc.psum_tensor(f"a_bank{i}", [P, HALF], F32)) for i in range(8)]
        xn = sb("xn", [P, NT, HID])
        xT = sb("xT", [P, NK, S])
        qa_nat = sb("qa_nat", [96, 2, HID])
        lora_nat = sb("lora_nat", [LAT, HID])
        gate_nat = sb("gate_nat", [2, HID])
        sp_nat = sb("sp_nat", [P, 3, 2, HID])
        kpe_nat = sb("kpe_nat", [P, NP, HID])
        wqn = sb("wqn", [P, H, QR])
        wpe = sb("wpe", [P, NP, 256])
        wk = sb("wk", [P, H, LAT])
        w1T = sb("w1T", [P, NK, W1])
        spT = sb("spT", [P, 3, NK, HID])
        kpT = sb("kpT", [P, NK, S])
        aq = [sb("aq0", [P, NP, 256]), sb("aq1", [P, NP, 256])]
        split_hi = sb("split_hi", [P, S], F32R)
        split_lo = sb("split_lo", [P, S], F32R)
        m1 = sb("m1", [P, NT, W1])
        cT = sb("cT", [P, S])
        sp_hi = sb("sp_hi", [P, 2, HALF], F32R)
        sp_lo = sb("sp_lo", [P, 2, HALF], F32R)
        vf = sb("vf", [P, NT, HID])
        lnq = sb("lnq", [P, QR])
        lnkv = sb("lnkv", [P, LAT])
        gate_b = sb("gate_b", [P, 2])
        stats = sb("stats", [P, NT, 6])
        mv = sb("mv", [P, NT, 2])
        rstd = sb("rstd", [P, NT])
        junk = sb("junk", [P, QR])
        ssq = sb("ssq", [P, 2, NT])
        rms = sb("rms", [P, 2, NT])
        gl = sb("gl", [P, NT, 2])
        gmax = sb("gmax", [P, NT])
        gsum = sb("gsum", [P, NT])
        ident, cdup, gates = g["ident"], g["cdup"], g["gates"]

        s_x, s_const, s_w1, s_sp, s_kpe, s_wq, s_ln = (
            sem(n) for n in ("x_in", "const_in", "w1_in", "sp_in", "kpe_in", "wq_in", "ln_in"))
        stat = sem("stat")
        rstd_ready = sem("rstd_ready")
        xn_ready = sem("xn_ready")
        pe_job = sem("pe_job")
        ev_act = sem("ev_act")
        ev_dve = sem("ev_dve")
        hi_ready = sem("hi_ready")
        ssq_ready = sem("ssq_ready")
        rms_ready = sem("rms_ready")
        norm_ready = sem("norm_ready")
        wsplit_hi = sem("wsplit_hi")
        wsplit_lo = sem("wsplit_lo")
        wstored = sem("wstored")
        spstored = [sem(f"spstored{i}") for i in range(2)]
        vstored = sem("vstored")
        dve_own = sem("dve_own")
        pool_own = sem("pool_own")
        logits = sem("logits")
        gexp = sem("gexp")

        def evacuated(eng, n):
            for s, flag in ((ev_act, True), (ev_dve, False)):
                count = sum(b == flag for b in by_act[:n + 1])
                if count:
                    eng.wait_ge(s, count)

        block = ctx.enter_context(nc.Block())

        @block.sync
        def _(sp):
            x = a["x"].rearrange("b (t p) n -> p (b t) n", p=P)
            sp.dma_start(xn[:, 0:4, :], x[:, 0:4, :]).then_inc(s_x, 16)
            sp.dma_start(xn[:, 4:8, :], x[:, 4:8, :]).then_inc(s_x, 16)
            sp.dma_start(ident[:, :], a["consts"][:, 0:P]).then_inc(s_const, 16)
            sp.dma_start(g["sel_f"][0:64, :], a["consts"][0:64, P:P + 256]).then_inc(s_const, 16)
            sp.dma_start(qa_nat[:, :, :], a["q_a_w"].rearrange("(m p) n -> p m n", p=96)).then_inc(s_w1, 16)
            sp.dma_start(lora_nat[:, :], a["kv_a_w"][0:LAT, :]).then_inc(s_w1, 16)
            sp.dma_start(gate_nat[:, :], a["gate_w"]).then_inc(s_w1, 16)
            for w, name in enumerate(("sp_q_w", "sp_k_w", "sp_v_w")):
                sp.dma_start(sp_nat[:, w, :, :], a[name].rearrange("(m p) n -> p m n", p=P)).then_inc(s_sp, 16)
            sp.dma_start(kpe_nat[:, :, :],
                         a["kv_a_w"][LAT:LAT + H * ROPE, :].rearrange("(n p) k -> p n k", p=P)).then_inc(s_kpe, 16)
            heads = a["q_b_w"].rearrange("(h d) r -> d h r", d=DQ)
            for h in range(2):
                rows = heads[NOPE:DQ].rearrange("d (n two) r -> d n two r", two=2)[:, :, h, :]
                at = slice(64 * h, 64 * h + 64)
                sp.dma_start(wpe[at, :, 0:QR], rows).then_inc(s_wq, 16)
                sp.dma_start(wpe[at, :, QR:256], rows[:, :, P:QR]).then_inc(s_wq, 16)
            sp.dma_start(wqn[:, :, :], heads[0:NOPE]).then_inc(s_wq, 16)
            sp.dma_start(wk[:, :, :], a["kv_b_w"].rearrange("(h d) l -> d h l", d=NOPE + DV)[0:NOPE]).then_inc(s_wq, 16)
            sp.dma_start(lnq[:, :], a["q_a_ln_w"].rearrange("(a n) -> a n", a=1).broadcast_to((P, QR))).then_inc(s_ln, 16)
            sp.dma_start(lnkv[:, :], a["kv_a_ln_w"].rearrange("(a n) -> a n", a=1).broadcast_to((P, LAT))).then_inc(s_ln, 16)
            sp.dma_start(gate_b[:, :], a["gate_b"].rearrange("(a n) -> a n", a=1).broadcast_to((P, 2))).then_inc(s_ln, 16)
            sp.dma_start(g["cos"][:, :], a["rope"][0]).then_inc(s_const, 16)
            sp.dma_start(g["sin"][:, :], a["rope"][1]).then_inc(s_const, 16)
            stage = d["wst"].rearrange("n p (c j) -> p n c j", j=P)

            def store_weights(c):
                sp.wait_ge(wsplit_hi, c + 1)
                sp.wait_ge(wsplit_lo, c + 1)
                for lo, t in enumerate((split_hi, split_lo)):
                    if c < 2:
                        sp.dma_start(stage[:, :, 8 + 2 * c + lo, :],
                                     t[:, :].bitcast(F32).rearrange("p (n j) -> p n j", j=P)).then_inc(wstored, 16)
                    else:
                        kind, q = (c - 2) // 2, (c - 2) % 2
                        v = t[:, :].bitcast(F32).rearrange("p (n b j) -> p n b j", b=2, j=P)
                        for b in range(2):
                            sp.dma_start(stage[:, 4 * q:4 * q + 4, 4 * b + 2 * kind + lo, :],
                                         v[:, :, b, :]).then_inc(wstored, 16)

            store_weights(0)
            store_weights(1)
            for i in range(8):
                w, m, h = jobs[first_spqk + i][1:]
                sp.wait_ge(ev_dve, sum(not b for b in by_act[:first_spqk + i + 1]))
                for lo, t in enumerate((sp_hi, sp_lo)):
                    sp.dma_start(d["spqk"][w, lo, m * P:(m + 1) * P, h * HALF:(h + 1) * HALF],
                                 t[:, i % 2, :].bitcast(F32)).then_inc(spstored[i % 2], 16)
                if i % 2:
                    store_weights(2 + i // 2)
            evacuated(sp, last("spv"))
            sp.dma_start(d["vp"], vf[:, :, :].rearrange("p t n -> p (t n)")).then_inc(vstored, 16)
            sp.wait_ge(vstored, 16)
            sp.wait_ge(wstored, 16 * (2 * 2 + 4 * 4))
            for s in spstored:
                sp.wait_ge(s, 16 * 8)
            sp.wait_ge(s_const, 64)

        @block.gpsimd
        def _(pool):
            pool.memset(g["mhalf"][:, :], -0.5).then_inc(pool_own, 1)
            pool.wait_ge(stat, 2 * NT)
            pool.tensor_scalar(rstd[:, :], mv[:, :, 1], 1e-5, None, ALU.add).then_inc(pool_own, 1)
            pool.wait_ge(pool_own, 2)
            pool.tensor_tensor(rstd[:, :], rstd[:, :], g["mhalf"][:, 0:NT], ALU.pow).then_inc(rstd_ready, 1)
            pool.wait_ge(ssq_ready, 2 * NT)
            pool.tensor_scalar(rms[:, :, :], ssq[:, :, :], 1e-6, None, ALU.add).then_inc(pool_own, 1)
            pool.wait_ge(pool_own, 3)
            pool.tensor_tensor(rms[:, :, :], rms[:, :, :], g["mhalf"][:, 0:2 * NT].rearrange("p (a b) -> p a b", a=2),
                               ALU.pow).then_inc(rms_ready, 1)

        @block.tensor
        def _(pe):
            def transposes(n, blocks):
                at = 0
                for src in blocks:
                    k, m = src.shape[0], src.shape[1]
                    mm = pe.transpose(bank[n % 8][0:m, at:at + k], src, ident[0:k, 0:k])
                    at += k
                mm.then_inc(pe_job, 1)

            pe.wait_ge(s_const, 64)
            for n, job in enumerate(jobs):
                kind, out = job[0], bank[n % 8]
                if n >= 8:
                    evacuated(pe, n - 8)
                if kind == "xT":
                    k, q = job[1:]
                    pe.wait_ge(xn_ready, 4 * q + 4)
                    transposes(n, [xn[:, 4 * q + j, k * P:(k + 1) * P] for j in range(4)])
                elif kind == "w1T":
                    k = slice(job[1] * P, (job[1] + 1) * P)
                    pe.wait_ge(s_w1, 48)
                    transposes(n, [qa_nat[:, 0, k], qa_nat[:, 1, k], lora_nat[:, k], gate_nat[:, k]])
                elif kind == "proj1":
                    t = slice(job[1] * P, (job[1] + 1) * P)
                    evacuated(pe, last("w1T"))
                    for k in range(NK):
                        mm = pe.matmul(out[:, 0:W1], xT[:, k, t], w1T[:, k, :], start=(k == 0), stop=(k == NK - 1))
                    mm.then_inc(pe_job, 1)
                elif kind == "spT":
                    pe.wait_ge(s_sp, 48)
                    transposes(n, [sp_nat[:, job[1], m, k * P:(k + 1) * P] for k in range(NK) for m in range(2)])
                elif kind == "kpT":
                    k, q = job[1:]
                    pe.wait_ge(s_kpe, 16)
                    transposes(n, [kpe_nat[:, 4 * q + j, k * P:(k + 1) * P] for j in range(4)])
                elif kind in ("pe0T", "pe1T"):
                    r = slice(0, P) if kind == "pe0T" else slice(P, 256)
                    pe.wait_ge(s_wq, 96)
                    transposes(n, [wpe[:, 4 * job[1] + j, r] for j in range(4)])
                elif kind == "lat0":
                    for j in range(8):
                        h = 8 * job[1] + j
                        mm = pe.matmul(out[:, 64 * j:64 * j + 64], wqn[:, h, 0:P], wk[:, h, :], start=True, stop=True)
                    mm.then_inc(pe_job, 1)
                elif kind == "lat1":
                    for j in range(8):
                        h = 8 * job[1] + j
                        for r in (0, 64):
                            mm = pe.matmul(out[r:r + 64, 64 * j:64 * j + 64], wqn[:, h, P:QR], wk[:, h, :],
                                           start=True, stop=True)
                    mm.then_inc(pe_job, 1)
                elif kind == "spqk":
                    w, m, h = job[1:]
                    evacuated(pe, last("spT"))
                    for k in range(NK):
                        mm = pe.matmul(out[:, :], spT[:, w, k, m * P:(m + 1) * P], xT[:, k, h * HALF:(h + 1) * HALF],
                                       start=(k == 0), stop=(k == NK - 1))
                    mm.then_inc(pe_job, 1)
                elif kind == "spv":
                    for j in range(2):
                        t = 2 * job[1] + j
                        for k in range(NK):
                            mm = pe.matmul(out[:, j * HID:(j + 1) * HID], xT[:, k, t * P:(t + 1) * P], spT[:, 2, k, :],
                                           start=(k == 0), stop=(k == NK - 1))
                    mm.then_inc(pe_job, 1)
                elif kind in ("qm0T", "qm1T"):
                    r = slice(0, P) if kind == "qm0T" else slice(P, 256)
                    pe.wait_ge(norm_ready, 1)
                    transposes(n, [m1[:, 4 * job[1] + j, r] for j in range(4)])
                elif kind == "cT":
                    transposes(n, [cdup[:, 4 * job[1] + j, :] for j in range(4)])

        def plain(n):
            job = jobs[n]
            kind, out = job[0], bank[n % 8]
            if kind == "xT":
                return xT[:, job[1], job[2] * HALF:(job[2] + 1) * HALF], out[:, :]
            if kind == "w1T":
                return w1T[:, job[1], :], out[:, 0:W1]
            if kind == "proj1":
                return m1[:, job[1], :], out[:, 0:W1]
            if kind == "spT":
                return spT[:, job[1], :, :].rearrange("p k n -> p (k n)"), out[:, :]
            if kind == "kpT":
                return kpT[:, job[1], job[2] * HALF:(job[2] + 1) * HALF], out[:, :]
            if kind in ("pe0T", "pe1T"):
                to = aq[kind == "pe1T"][:, 4 * job[1]:4 * job[1] + 4, :]
                return (to.rearrange("p n (b j) -> p n b j", j=64)[:, :, 0:4:3, :],
                        out[:, :].rearrange("p (n b j) -> p n b j", b=2, j=64))
            if kind in ("lat0", "lat1"):
                to = aq[kind == "lat1"][:, 4 * job[1]:4 * job[1] + 4, 64:192]
                return to, out[:, :].rearrange("p (n j) -> p n j", j=P)
            if kind == "spv":
                return vf[:, 2 * job[1]:2 * job[1] + 2, :].rearrange("p t n -> p (t n)"), out[:, :]
            if kind == "cT":
                return cT[:, job[1] * HALF:(job[1] + 1) * HALF], out[:, :]
            return None

        def hi_of(n):
            job = jobs[n]
            if job[0] == "spqk":
                return sp_hi[:, (n - first_spqk) % 2, :]
            cols = slice(job[1] * HALF, (job[1] + 1) * HALF)
            return (g["qm0h"] if job[0] == "qm0T" else g["qm1"])[:, cols]

        chunks = [kpT[:, 0, :], kpT[:, 1, :]] + [
            aq[kind][:, 4 * q:4 * q + 4, :].rearrange("p n j -> p (n j)") for kind in range(2) for q in range(2)]
        chunk_jobs = [last("kpT")] * 2 + [last("lat0")] * 2 + [last("lat1")] * 2

        @block.scalar
        def _(act):
            def weight_hi(c):
                evacuated(act, chunk_jobs[c])
                if c:
                    act.wait_ge(wstored, 16 * (2 * c if c < 3 else 4 + 4 * (c - 2)))
                act.activation(split_hi[:, :], chunks[c], ACT.Copy).then_inc(wsplit_hi, 1)

            for n, job in enumerate(jobs):
                if job[0] in split:
                    act.wait_ge(pe_job, n + 1)
                    if job[0] == "spqk" and n - first_spqk >= 2:
                        i = n - first_spqk
                        act.wait_ge(spstored[i % 2], 32 * (i // 2))
                    act.activation(hi_of(n), bank[n % 8][:, :], ACT.Copy).then_inc(hi_ready, 1)
                elif by_act[n]:
                    act.wait_ge(pe_job, n + 1)
                    act.activation(*plain(n), ACT.Copy).then_inc(ev_act, 1)
                if n == last("xT") + 2:
                    evacuated(act, last("xT"))
                    act.activation(g["xh"][:, :, :], xT[:, :, :], ACT.Copy).then_inc(hi_ready, 1)
                if n == last("spT"):
                    evacuated(act, last("proj1"))
                    for t in range(NT):
                        act.activation(junk[:, :], m1[:, t, 0:QR], ACT.Square, scale=float(QR) ** -0.5,
                                       accum_out=ssq[:, 0, t:t + 1]).then_inc(ssq_ready, 1)
                        act.wait_ge(ssq_ready, 2 * t + 1)
                        act.activation(junk[:, 0:LAT], m1[:, t, QR:QR + LAT], ACT.Square, scale=float(LAT) ** -0.5,
                                       accum_out=ssq[:, 1, t:t + 1]).then_inc(ssq_ready, 1)
                        act.wait_ge(ssq_ready, 2 * t + 2)
                if n == last("kpT") + 2:
                    weight_hi(0)
                if n == last("kpT") + 4:
                    weight_hi(1)
                if job[0] == "spqk" and (n - first_spqk) % 2:
                    weight_hi(2 + (n - first_spqk) // 2)
            act.wait_ge(logits, 1)
            act.activation(gl[:, :, :], gl[:, :, :], ACT.Exp).then_inc(gexp, 1)
            evacuated(act, last("cT"))
            for b in range(4):
                rows = slice(64, P) if b % 2 == 0 else slice(0, 64)
                act.activation(g["kh"][rows, b, :], cT[rows, :], ACT.Copy).then_inc(hi_ready, 1)
            act.activation(g["sel"][0:64, :], g["sel_f"][0:64, :], ACT.Copy).then_inc(hi_ready, 1)

        @block.vector
        def _(dve):
            own = [0]

            def link(ins):
                own[0] += 1
                ins.then_inc(dve_own, 1)
                dve.wait_ge(dve_own, own[0])

            his = [0]

            def weight_lo(c):
                dve.wait_ge(wsplit_hi, c + 1)
                dve.tensor_tensor(split_lo[:, :], chunks[c], split_hi[:, :].bitcast(F32),
                                  ALU.subtract).then_inc(wsplit_lo, 1)

            for q in range(2):
                dve.wait_ge(s_x, 32)
                for t in range(4 * q, 4 * q + 4):
                    dve.bn_stats(stats[:, t, :], xn[:, t, :]).then_inc(stat, 1)
            dve.wait_ge(stat, NT)
            for t in range(NT):
                dve.bn_aggr(mv[:, t, :], stats[:, t, :]).then_inc(stat, 1)
            dve.wait_ge(rstd_ready, 1)
            for t in range(NT):
                dve.tensor_scalar(xn[:, t, :], xn[:, t, :], mv[:, t, 0:1], rstd[:, t:t + 1],
                                  ALU.subtract, ALU.mult).then_inc(xn_ready, 1)
            for n, job in enumerate(jobs):
                kind = job[0]
                if kind in split:
                    his[0] += 1
                    dve.wait_ge(hi_ready, 1 + his[0])
                    src, hi = bank[n % 8], hi_of(n)
                    if kind == "spqk":
                        lo = sp_lo[:, (n - first_spqk) % 2, :]
                        dve.tensor_tensor(lo, src[:, :], hi.bitcast(F32), ALU.subtract).then_inc(ev_dve, 1)
                    elif kind == "qm0T":
                        lo = g["qm0l"][:, job[1] * HALF:(job[1] + 1) * HALF]
                        dve.tensor_tensor(lo, src[:, :], hi.bitcast(F32), ALU.subtract).then_inc(ev_dve, 1)
                    else:
                        dve.tensor_tensor(hi[64:P, :], src[64:P, :], hi[64:P, :].bitcast(F32),
                                          ALU.subtract).then_inc(ev_dve, 1)
                elif not by_act[n]:
                    dve.wait_ge(pe_job, n + 1)
                    dve.tensor_copy(*plain(n)).then_inc(ev_dve, 1)
                if n == last("xT") + 4:
                    dve.wait_ge(hi_ready, 1)
                    link(dve.tensor_tensor(g["xl"][:, :, :], xT[:, :, :], g["xh"][:, :, :].bitcast(F32), ALU.subtract))
                if n == last("kpT") + 2:
                    dve.wait_ge(rms_ready, 1)
                    dve.wait_ge(s_ln, 48)
                    for t in range(NT):
                        for r in (0, 64):
                            ins = dve.scalar_tensor_tensor(cdup[:, t, r:r + 64], m1[:, t, QR:QR + LAT],
                                                           rms[:, 1, t:t + 1], lnkv[:, :], ALU.mult, ALU.mult)
                    link(ins)
                    for t in range(NT):
                        ins = dve.scalar_tensor_tensor(m1[:, t, 0:QR], m1[:, t, 0:QR], rms[:, 0, t:t + 1],
                                                       lnq[:, :], ALU.mult, ALU.mult)
                    link(ins)
                    link(dve.tensor_copy(m1[:, :, QR:256], m1[:, :, P:QR]))
                    dve.tensor_tensor(gl[:, :, :], m1[:, :, 256:258],
                                      gate_b[:, :].unsqueeze(1).broadcast_to((P, NT, 2)), ALU.add).then_inc(norm_ready, 1)
                    dve.wait_ge(norm_ready, 1)
                    link(dve.tensor_reduce(gmax[:, :], gl[:, :, :], AX, ALU.max))
                    dve.tensor_tensor(gl[:, :, :], gl[:, :, :], gmax[:, :].unsqueeze(2).broadcast_to((P, NT, 2)),
                                      ALU.subtract).then_inc(logits, 1)
                if n == last("kpT") + 3:
                    weight_lo(0)
                if n == last("kpT") + 5:
                    weight_lo(1)
                if kind == "spqk" and (n - first_spqk) % 2:
                    weight_lo(2 + (n - first_spqk) // 2)
            dve.wait_ge(gexp, 1)
            link(dve.tensor_reduce(gsum[:, :], gl[:, :, :], AX, ALU.add))
            link(dve.reciprocal(gsum[:, :], gsum[:, :]))
            link(dve.tensor_tensor(gates[:, :, :], gl[:, :, :], gsum[:, :].unsqueeze(2).broadcast_to((P, NT, 2)),
                                   ALU.mult))
            for b in range(4):
                dve.wait_ge(hi_ready, 2 + his[0] + b)
                rows = slice(64, P) if b % 2 == 0 else slice(0, 64)
                ins = dve.tensor_tensor(g["kl"][rows, b, :], cT[rows, :], g["kh"][rows, b, :].bitcast(F32), ALU.subtract)
            link(ins)



X_STEPS = [
    [("mm", 3), ("P", 0)],
    [("S", 1), ("mm", 3), ("P", 1)],
    [("mm", 3), ("P", 2)],
    [("mm", 3), ("P", 3)],
    [("pm", 3), ("P", 4)],
    [("pm", 3), ("P", 5)],
    [("mT", 1), ("pm", 4)],
    [("pm", 5)],
    [("pm", 5)],
    [("S", 0), ("pm", 4)],
    [("pm", 4)],
    [("pm", 4)],
    [("pT", 0), ("pT", 1), ("mm", 4)],
    [("mm", 6)],
    [("mm", 6)],
    [("mT", 0), ("mm", 4)],
]
MM_LATE = 20
BY_ACT = ("mT", "pT", "S")


def x_steps(v):
    count = {"pm": 0, "mm": MM_LATE}
    steps = []
    for tiles in X_STEPS:
        step = []
        for kind, n in tiles:
            numbers = [n]
            if kind in count:
                numbers = [(count[kind] + i) % 32 for i in range(n)]
                count[kind] += n
            for i in numbers:
                if (kind, i) == ("mT", 1) or kind == "mm" and i >= MM_LATE:
                    here = 1 <= v <= NP
                elif kind == "S":
                    here = v >= 2 if i else 1 <= v <= NP
                else:
                    here = v < NP
                if here:
                    step.append((kind, i))
        steps.append(step)
    return steps


def attention(nc, a, d, g):
    NS = 16
    slots = range(NP + 2)
    xs = [x_steps(v) for v in slots]
    x_index = {}
    for v in slots:
        for step in xs[v]:
            for tile in step:
                x_index[(v, *tile)] = len(x_index)

    x_tiles = [(t[0], t[1:]) for t in x_index]

    with ExitStack() as ctx:
        def sb(name, shape, dt=F32):
            return ctx.enter_context(nc.sbuf_tensor(name, shape, dt))

        def ps(name):
            return ctx.enter_context(nc.psum_tensor(name, [P, HALF], F32))

        def sem(name):
            return ctx.enter_context(nc.semaphore(name))

        st = [ps(f"st{i}") for i in range(4)]
        xb = [ps(f"xb{i}") for i in range(2)]
        pvm = ps("pvm")
        pvp = ps("pvp")
        kh, kl = g["kh"], g["kl"]
        qh = sb("qh", [P, 4, S], F32R)
        ql = sb("ql", [P, 4, S], F32R)
        wst = sb("wst", [P, 2, NW, P], F32R)
        raw = sb("raw", [P, 2, HALF])
        rot = sb("rot", [P, 2, HALF])
        rc = sb("rc", [P, 2, HALF])
        em = sb("em", [P, 8, HALF])
        ep = sb("ep", [P, 8, HALF])
        acc = sb("acc", [P, 2, HALF])
        pq = sb("pq", [P, 2, 2, HALF], F32R)
        pk = sb("pk", [P, 2, 2, S], F32R)
        vp = sb("vp", [P, 2, NT, 4, 32])
        ones = sb("ones", [P, 64])
        mr = sb("mr", [64, S], F32R)
        mrp = sb("mrp", [4, HALF], F32R)
        m2 = sb("m2", [P, 2, 2, 4, 2])
        ms = sb("ms", [P, 2, 4, 2])
        m2p = sb("m2p", [P, 4, 4, 2])
        msp = sb("msp", [P, 4, 4])
        ctxr = sb("ctxr", [P, HALF])
        sums = sb("sums", [P, HALF])
        rec = sb("rec", [P, HALF])
        pvr = sb("pvr", [P, HALF])
        prec = sb("prec", [P, HALF])
        ident, sel, cdup = g["ident"], g["sel"], g["cdup"]

        init = sem("init")
        x_ready = sem("x_ready")
        x_dve = sem("x_dve")
        x_act = sem("x_act")
        st_ready = sem("st_ready")
        e_ready = sem("e_ready")
        pvm_done = sem("pvm_done")
        pvp_done = sem("pvp_done")
        added = sem("added")
        raw_ready = sem("raw_ready")
        lat_hi = sem("lat_hi")
        cos_done = sem("cos_done")
        turned = [sem(f"turned{i}") for i in range(2)]
        sin_done = sem("sin_done")
        roped = sem("roped")
        rope_hi = sem("rope_hi")
        rope_lo = sem("rope_lo")
        mm_part = sem("mm_part")
        mm_ready = sem("mm_ready")
        pm_part = sem("pm_part")
        pm_ready = sem("pm_ready")
        mrow_in = sem("mrow_in")
        wst_in = [sem(f"wst_in{i}") for i in range(2)]
        stack_in = [sem(f"stack_in{i}") for i in range(2)]
        vp_in = [sem(f"vp_in{i}") for i in range(2)]
        ctx_out = sem("ctx_out")
        rec_part = sem("rec_part")
        ctx_ready = sem("ctx_ready")
        ctx_stored = sem("ctx_stored")
        pat_out = sem("pat_out")
        pat_part = sem("pat_part")
        pat_ready = sem("pat_ready")
        pat_stored = sem("pat_stored")

        block = ctx.enter_context(nc.Block())

        def x_bank(v, tile):
            return xb[x_index[(v, *tile)] % 2]

        def x_wait(eng, v, tile):
            eng.wait_ge(x_ready, x_index[(v, *tile)] + 1)

        def x_emptied(eng, v, tile):
            kind = tile[0] in BY_ACT
            n = sum((t[1] in BY_ACT) == kind and i <= x_index[(v, *tile)] for t, i in x_index.items())
            eng.wait_ge(x_act if kind else x_dve, n)

        def adds(it, q, kt, h):
            return 28 * it + 14 * q + 2 * (max(kt, 1) - 1) + h + 1

        NSTACK = 12
        UNIT = [(0, 1), (2, 3), (4,), (5,)]
        FIN = {3: 0, 5: 1, 6: 2, 7: 3}

        @block.sync
        def _(sp):
            def load_stacks(v):
                quad, half, b = v // 2, v % 2, v % 2
                for w, to, cols in ((0, pq, slice(half * HALF, (half + 1) * HALF)), (1, pk, slice(0, S))):
                    for j in range(2):
                        for slot in range(3):
                            lo = int(slot == (2 if w == 0 else 1))
                            src = d["spqk"][w, lo, 64 * quad:64 * quad + 64, cols].rearrange(
                                "(t j p) n -> j p t n", j=2, p=PD)[j]
                            at = 64 * j + PD * slot
                            sp.dma_start(to[at:at + PD, b, :, :].bitcast(F32), src).then_inc(stack_in[v % 2], 16)

            def load_vp(v):
                src = d["vp"].rearrange("p (t n e) -> p t n e", t=NT, e=PD)[:, :, 4 * (v // 2):4 * (v // 2) + 4, :]
                for t in range(NT):
                    sp.dma_start(vp[:, v % 2, t, :, 0:PD], src[:, t]).then_inc(vp_in[v % 2], 16)

            def load_weights(v):
                sp.dma_start(wst[:, v % 2, :, :].rearrange("p c j -> p (c j)").bitcast(F32), d["wst"][v]).then_inc(wst_in[v % 2], 16)

            def turn(v, u):
                n = 4 * v + u
                sp.wait_ge(raw_ready, 6 * v + UNIT[u][-1] + 1)
                if n >= 2:
                    sp.wait_ge(roped, n - 1)
                for b in range(4):
                    o = b ^ 1
                    sp.dma_start(rot[32 * b:32 * b + 32, n % 2, :], raw[32 * o:32 * o + 32, n % 2, :]).then_inc(turned[n % 2], 16)

            sp.wait_ge(init, 4)
            load_weights(0)
            for v in slots:
                if v < NP:
                    if v >= 2:
                        sp.wait_ge(st_ready, 64 * (v - 1))
                    load_stacks(v)
                    if v + 1 < NP:
                        if v >= 1:
                            x_wait(sp, v - 1, ("P", 5))
                        load_weights(v + 1)
                    turn(v, 0)
                if v >= 2:
                    sp.wait_ge(ctx_ready, 2 * (v - 2) + 2)
                    sp.dma_start(d["ctx"][v - 2, :, HALF:S], rec[:, :]).then_inc(ctx_stored, 16)
                if v < NP:
                    if v >= 2:
                        sp.wait_ge(pvp_done, NT * (v - 1))
                    load_vp(v)
                    turn(v, 1)
                if v >= 2:
                    sp.wait_ge(pat_ready, v - 1)
                    sp.dma_start(d["pat"][v - 2], prec[:, :]).then_inc(pat_stored, 16)
                if v < NP:
                    for u in (2, 3):
                        turn(v, u)
                if 1 <= v <= NP:
                    sp.wait_ge(ctx_ready, 2 * (v - 1) + 1)
                    sp.dma_start(d["ctx"][v - 1, :, 0:HALF], rec[:, :]).then_inc(ctx_stored, 16)
                if v < NP:
                    x_emptied(sp, v, ("pT", 1))
                    for hh in range(4):
                        at = 64 * (hh % 2) + 3 * PD
                        sp.dma_start(pq[at:at + 1, v % 2, hh // 2, :].bitcast(F32),
                                     mrp[hh:hh + 1, :].bitcast(F32)).then_inc(mrow_in, 16)
            sp.wait_ge(ctx_stored, 16 * 2 * NP)
            sp.wait_ge(pat_stored, 16 * NP)

        @block.gpsimd
        def _(pool):
            pool.memset(vp[:, :, :, :, PD:32], 1.0).then_inc(init, 1)
            pool.memset(ones[:, :], 1.0).then_inc(init, 1)

            def turn_sin(v, u):
                n = 4 * v + u
                half = slice((u % 2) * HALF, (u % 2 + 1) * HALF)
                pool.wait_ge(turned[n % 2], 64 * (n // 2 + 1))
                pool.tensor_tensor(rot[:, n % 2, :], rot[:, n % 2, :], g["sin"][:, half], ALU.mult).then_inc(sin_done, 1)

            def rope(v, u):
                n = 4 * v + u
                pool.wait_ge(sin_done, n + 1)
                if u < 2:
                    pool.wait_ge(cos_done, 4 * v + 2 * u + 2)
                else:
                    x_emptied(pool, v, ("P", UNIT[u][0]))
                pool.tensor_tensor(rc[:, n % 2, :], rc[:, n % 2, :], rot[:, n % 2, :], ALU.add).then_inc(roped, 1)

            def rope_lo_of(v, u, s):
                n = 4 * v + u
                if v:
                    it, t = (v - 1, s - 1)
                    pool.wait_ge(added, adds(it, t // NT, t % NT, 1))
                half = slice((u % 2) * HALF, (u % 2 + 1) * HALF)
                hi, lo = (qh, ql) if u < 2 else (kh, kl)
                for h in range(2):
                    rows = slice(64 * h, 64 * h + 64)
                    pool.wait_ge(rope_hi, 2 * n + h + 1)
                    pool.tensor_tensor(lo[rows, 2 * (v % 2) + h, half], rc[rows, n % 2, :],
                                       hi[rows, 2 * (v % 2) + h, half].bitcast(F32),
                                       ALU.subtract).then_inc(rope_lo, 1)
                pool.wait_ge(rope_lo, 2 * n + 2)

            def add(it, q, kt):
                for h in range(2):
                    j = 2 * (NT * q + kt) + h
                    pool.wait_ge(e_ready, 64 * it + 4 * (NT * q + kt) + 2 * h + 1)
                    if kt == 1:
                        if q == 1:
                            x_wait(pool, it + 1, ("S", 0))
                        elif it >= 1:
                            x_wait(pool, it + 1, ("S", 1))
                        first = em[:, (j - 2) % 8, :]
                    else:
                        pool.wait_ge(added, adds(it, q, kt - 1, h))
                        first = acc[:, h, :]
                    pool.tensor_tensor(acc[:, h, :], first, em[:, j % 8, :], ALU.add).then_inc(added, 1)

            for v in slots:
                for s in range(NS):
                    if v < NP and s - 1 in FIN:
                        rope_lo_of(v, FIN[s - 1], s)
                    if v < NP and s in FIN:
                        turn_sin(v, FIN[s])
                        rope(v, FIN[s])
                    if 1 <= v <= NP and s % NT:
                        add(v - 1, s // NT, s % NT)

        @block.scalar
        def _(act):
            def produce(v, i):
                tile, n = x_bank(v, ("P", i)), 6 * v + i
                x_wait(act, v, ("P", i))
                u = next(u for u in range(4) if i in UNIT[u])
                un = 4 * v + u
                if i == UNIT[u][0] and un >= 2:
                    act.wait_ge(turned[un % 2], 64 * (un // 2))
                if i < 4:
                    h, half = i % 2, slice((i // 2) * HALF, (i // 2 + 1) * HALF)
                    pe_rows = slice(64 * h, 64 * h + 64)
                    lat_rows = slice(64 - 64 * h, P - 64 * h)
                    act.activation(raw[pe_rows, un % 2, :], tile[pe_rows, :], ACT.Copy).then_inc(raw_ready, 1)
                    act.activation(qh[lat_rows, 2 * (v % 2) + h, half], tile[lat_rows, :],
                                   ACT.Copy).then_inc(lat_hi, 1)
                else:
                    act.activation(raw[:, un % 2, :], tile[:, :], ACT.Copy).then_inc(raw_ready, 1)

            def x_tile(v, tile):
                kind, i = tile
                if kind == "P":
                    produce(v, i)
                if kind not in BY_ACT:
                    return
                x_wait(act, v, tile)
                src = x_bank(v, tile)
                if kind == "mT":
                    at = 32 * ((v - i) % 2)
                    act.activation(mr[at:at + 2, i * HALF:(i + 1) * HALF], src[0:2, :], ACT.Copy).then_inc(x_act, 1)
                elif kind == "pT":
                    if v:
                        act.wait_ge(mrow_in, 64 * v)
                    act.activation(mrp[:, 256 * i:256 * i + 256], src[0:4, 0:256], ACT.Copy).then_inc(x_act, 1)
                elif kind == "S":
                    n = 2 * (v - 2) + 1 if i else 2 * (v - 1)
                    if n:
                        act.wait_ge(rec_part, 4 * n)
                    act.activation(sums[:, :], src[:, :], ACT.Copy).then_inc(x_act, 1)

            def rope_hi_of(v, u):
                n = 4 * v + u
                half = slice((u % 2) * HALF, (u % 2 + 1) * HALF)
                act.wait_ge(roped, n + 1)
                for h in range(2):
                    rows = slice(64 * h, 64 * h + 64)
                    to = (qh if u < 2 else kh)[rows, 2 * (v % 2) + h, half]
                    act.activation(to, rc[rows, n % 2, :], ACT.Copy).then_inc(rope_hi, 1)

            for v in slots:
                it = v - 1
                for s in range(NS):
                    if s == 1 and v >= 2 or s == 9 and 1 <= v <= NP:
                        n = 2 * (v - 2) + 1 if s == 1 else 2 * it
                        act.wait_ge(pvm_done, 16 * (n + 1))
                        if n:
                            act.wait_ge(ctx_ready, n)
                        act.activation(ctxr[:, :], pvm[:, :], ACT.Copy).then_inc(ctx_out, 1)
                    if s == 2 and v >= 2:
                        act.wait_ge(pvp_done, NT * (v - 1))
                        if v > 2:
                            act.wait_ge(pat_ready, v - 2)
                        act.activation(pvr[:, :], pvp[:, :], ACT.Copy).then_inc(pat_out, 1)
                    tiles = iter(xs[v][s])
                    if 0 <= it < NP:
                        for x in range(4):
                            n = 64 * it + 4 * s + x
                            j = 32 * it + 2 * s + x // 2
                            act.wait_ge(st_ready, n + 1)
                            if j >= 8:
                                if x % 2 == 0:
                                    act.wait_ge(pvm_done, j - 7)
                                    o = j - 8
                                    act.wait_ge(added, adds(o // 32, o % 32 // 16, o % 16 // 2, o % 2))
                                else:
                                    act.wait_ge(pvp_done, (j - 8) // 4 + 1)
                            if x % 2 == 0:
                                act.activation(em[:, j % 8, :], st[n % 4][:, :], ACT.Exp,
                                               scale=MAIN_SCALE).then_inc(e_ready, 1)
                            else:
                                act.activation(ep[:, j % 8, :], st[n % 4][:, :], ACT.Exp,
                                               scale=PAT_SCALE).then_inc(e_ready, 1)
                            for tile in islice(tiles, 1):
                                x_tile(v, tile)
                    for tile in tiles:
                        x_tile(v, tile)
                    if v < NP and s in FIN:
                        rope_hi_of(v, FIN[s])

        @block.vector
        def _(dve):
            dve.memset(pk[:, :, :, :].bitcast(F32), -1.0).then_inc(init, 1)
            dve.memset(pq[:, :, :, :].bitcast(F32), 0.0).then_inc(init, 1)

            def produce(v, i):
                tile, n = x_bank(v, ("P", i)), 6 * v + i
                u = next(u for u in range(4) if i in UNIT[u])
                half = slice((u % 2) * HALF, (u % 2 + 1) * HALF)
                un = 4 * v + u
                if un >= 2:
                    dve.wait_ge(rope_lo, 2 * (un - 1))
                if i < 4:
                    h = i % 2
                    pe_rows = slice(64 * h, 64 * h + 64)
                    lat_rows = slice(64 - 64 * h, P - 64 * h)
                    dve.wait_ge(raw_ready, n + 1)
                    dve.tensor_tensor(rc[pe_rows, un % 2, :], tile[pe_rows, :], g["cos"][pe_rows, half],
                                      ALU.mult).then_inc(cos_done, 1)
                    dve.wait_ge(lat_hi, 4 * v + i + 1)
                    dve.tensor_tensor(ql[lat_rows, 2 * (v % 2) + h, half], tile[lat_rows, :],
                                      qh[lat_rows, 2 * (v % 2) + h, half].bitcast(F32),
                                      ALU.subtract).then_inc(x_dve, 1)
                else:
                    dve.wait_ge(raw_ready, n + 1)
                    dve.tensor_tensor(rc[:, un % 2, :], tile[:, :], g["cos"][:, half], ALU.mult).then_inc(x_dve, 1)

            def x_tile(v, tile):
                kind, i = tile
                if kind == "P":
                    produce(v, i)
                if kind not in ("pm", "mm"):
                    return
                x_wait(dve, v, tile)
                src = x_bank(v, tile)
                if kind == "pm":
                    dve.tensor_reduce(m2p[:, i // 8, i % 4, i // 4 % 2:i // 4 % 2 + 1], src[:, :], AX,
                                      ALU.max).then_inc(x_dve, 1)
                    if i == 31:
                        x_emptied(dve, v, tile)
                        if v:
                            x_wait(dve, v - 1, ("pT", 1))
                        dve.tensor_reduce(msp[:, :, :], m2p[:, :, :, :], AX, ALU.max).then_inc(pm_ready, 1)
                elif kind == "mm":
                    q, h, t, kt = i // 16, i // 8 % 2, i // 2 % 4, i % 2
                    dve.tensor_reduce(m2[:, q, h, t, kt:kt + 1], src[:, :], AX, ALU.max).then_inc(x_dve, 1)
                    if i % 16 == 15:
                        x_emptied(dve, v, tile)
                        dve.tensor_reduce(ms[:, q, :, :].rearrange("p t h -> p h t"), m2[:, q, :, :, :], AX,
                                          ALU.max).then_inc(mm_ready, 1)

            QUARTER = HALF // 4

            def main_reciprocal(v, i, j):
                n = 2 * (v - 2) + 1 if i else 2 * (v - 1)
                cols = slice(j * QUARTER, (j + 1) * QUARTER)
                if j == 0:
                    x_emptied(dve, v, ("S", i))
                    if n:
                        dve.wait_ge(ctx_stored, 16 * n)
                dve.reciprocal(rec[:, cols], sums[:, cols]).then_inc(rec_part, 1)
                if j == 3:
                    dve.wait_ge(rec_part, 4 * (n + 1))
                    dve.wait_ge(ctx_out, n + 1)
                    dve.tensor_tensor(rec[:, :], ctxr[:, :], rec[:, :], ALU.mult).then_inc(ctx_ready, 1)

            def pattern_reciprocal(it, j):
                cols = slice(j * QUARTER, (j + 1) * QUARTER)
                if j == 0:
                    dve.wait_ge(pat_out, it + 1)
                    if it:
                        dve.wait_ge(pat_stored, 16 * it)
                    dve.stream_shuffle(prec[:, :], pvr[:, :], [i | 16 for i in range(32)]).then_inc(pat_part, 1)
                    dve.wait_ge(pat_part, 5 * it + 1)
                dve.reciprocal(prec[:, cols], prec[:, cols]).then_inc(pat_part, 1)
                if j == 3:
                    dve.wait_ge(pat_part, 5 * it + 5)
                    dve.tensor_tensor(prec[:, :], pvr[:, :], prec[:, :], ALU.mult).then_inc(pat_ready, 1)

            def between(v, s, j):
                if v >= 2 and s in (2, 3):
                    main_reciprocal(v, 1, 2 * (s - 2) + j)
                if v >= 2 and s in (4, 5):
                    pattern_reciprocal(v - 2, 2 * (s - 4) + j)
                if 1 <= v <= NP and s in (10, 11):
                    main_reciprocal(v, 0, 2 * (s - 10) + j)

            for v in slots:
                for s in range(NS):
                    tiles = iter(xs[v][s])
                    for j in range(2):
                        for tile in islice(tiles, 2):
                            x_tile(v, tile)
                        between(v, s, j)
                    for tile in tiles:
                        x_tile(v, tile)

        @block.tensor
        def _(pe):
            pe.wait_ge(init, 4)

            def passes(out, pairs, sem_):
                for n, (w, x) in enumerate(pairs):
                    mm = pe.matmul(out, w, x, start=(n == 0), stop=(n == len(pairs) - 1))
                mm.then_inc(sem_, 1)

            def main_scores(it, s, h):
                n = 64 * it + 4 * s + 2 * h
                q, kt, b = s // NT, s % NT, 2 * (it % 2) + h
                if n >= 4:
                    pe.wait_ge(e_ready, n - 3)
                keys, queries = slice(kt * P, (kt + 1) * P), slice(q * HALF, (q + 1) * HALF)
                at = 32 * (it % 2)
                passes(st[n % 4][:, :], [
                    (kh[:, b, keys], qh[:, b, queries]), (kh[:, b, keys], ql[:, b, queries]),
                    (kl[:, b, keys], qh[:, b, queries]), (sel[at:at + 2, h * P:(h + 1) * P], mr[at:at + 2, queries]),
                ], st_ready)

            def pattern_scores(it, s, x):
                n = 64 * it + 4 * s + 2 * x + 1
                if n >= 4:
                    pe.wait_ge(e_ready, n - 3)
                hh, kt = 2 * (s % 2) + x, s // 2
                rows = slice(64 * x, 64 * x + 3 * PD + 1)
                passes(st[n % 4][:, :], [(pk[rows, it % 2, hh // 2, kt * P:(kt + 1) * P],
                                          pq[rows, it % 2, hh // 2, :])], st_ready)

            def main_values(it, s):
                q, kt = s // NT, s % NT
                if kt == 0 and (it or q):
                    pe.wait_ge(ctx_out, 2 * it + q)
                for h in range(2):
                    pe.wait_ge(e_ready, 64 * it + 4 * s + 2 * h + 1)
                    pe.matmul(pvm[64 * h:64 * h + 64, :], cdup[:, kt, 0:LAT], em[:, (2 * s + h) % 8, :],
                              start=(kt == 0), stop=(kt == NT - 1)).then_inc(pvm_done, 1)

            def pattern_values(it, kt):
                if kt == 0:
                    pe.wait_ge(vp_in[it % 2], 16 * NT * (it // 2 + 1))
                    if it:
                        pe.wait_ge(pat_out, it)
                pe.wait_ge(e_ready, 64 * it + 4 * (2 * kt + 1) + 4)
                for hh in range(4):
                    mm = pe.matmul(pvp[32 * hh:32 * hh + 32, :], vp[:, it % 2, kt, hh, :], ep[:, (4 * kt + hh) % 8, :],
                                   start=(kt == 0), stop=(kt == NT - 1))
                mm.then_inc(pvp_done, 1)

            def x_tile(v, tile):
                kind, i = tile
                n = x_index[(v, *tile)]
                out, b = xb[n % 2], v % 2
                if n >= 2:
                    x_emptied(pe, *x_tiles[n - 2])
                if kind == "P":
                    if i == 0:
                        pe.wait_ge(wst_in[v % 2], 16 * (v // 2 + 1))
                    w = [wst[:, b, c, :] for c in range(NW)]
                    if i < 4:
                        half = slice((i // 2) * HALF, (i // 2 + 1) * HALF)
                        o = 4 * (i % 2)
                        qm0h, qm0l, qm1 = g["qm0h"][:, half], g["qm0l"][:, half], g["qm1"]
                        passes(out[:, :], [(w[o], qm0h), (w[o + 1], qm0h), (w[o], qm0l), (w[o + 2], qm1[:, half]),
                                           (w[o + 3][0:64, :], qm1[0:64, half])], x_ready)
                    else:
                        half = slice((i - 4) * HALF, (i - 3) * HALF)
                        pairs = []
                        for k in range(NK):
                            xh, xl = g["xh"][:, k, half], g["xl"][:, k, half]
                            pairs += [(w[8 + 2 * k], xh), (w[9 + 2 * k], xh), (w[8 + 2 * k], xl)]
                        passes(out[:, :], pairs, x_ready)
                elif kind == "pm":
                    if i == 0:
                        pe.wait_ge(stack_in[v % 2], 16 * NSTACK * (v // 2 + 1))
                    hh, kt, t = i % 4, i // 4 % 2, i // 8
                    rows = slice(64 * (hh % 2), 64 * (hh % 2) + 3 * PD)
                    passes(out[:, :], [(pq[rows, b, hh // 2, t * P:(t + 1) * P],
                                        pk[rows, b, hh // 2, kt * HALF:(kt + 1) * HALF])], x_ready)
                elif kind == "mm":
                    if i == 0:
                        pe.wait_ge(rope_hi, 8 * (v + 1))
                    q, h, t, kt = i // 16, i // 8 % 2, i // 2 % 4, i % 2
                    at = (4 * q + t) * P
                    b = (v - (i >= MM_LATE)) % 2
                    passes(out[:, :], [(qh[:, 2 * b + h, at:at + P],
                                        kh[:, 2 * b + h, kt * HALF:(kt + 1) * HALF])], x_ready)
                elif kind == "mT":
                    pair = v - 1 if i else v
                    pe.wait_ge(mm_ready, 2 * pair + i + 1)
                    for t in range(4):
                        mm = pe.matmul(out[0:2, t * P:(t + 1) * P], ms[:, i, t, :], ident[:, :], start=True, stop=True)
                    mm.then_inc(x_ready, 1)
                elif kind == "pT":
                    pe.wait_ge(pm_ready, v + 1)
                    for t in range(2):
                        mm = pe.matmul(out[0:4, t * P:(t + 1) * P], msp[:, 2 * i + t, :], ident[:, :],
                                       start=True, stop=True)
                    mm.then_inc(x_ready, 1)
                elif kind == "S":
                    it = v - 2 if i else v - 1
                    for h in range(2):
                        pe.wait_ge(added, adds(it, i, NT - 1, h))
                        mm = pe.matmul(out[64 * h:64 * h + 64, :], ones[:, :], acc[:, h, :], start=True, stop=True)
                    mm.then_inc(x_ready, 1)

            for v in slots:
                it = v - 1
                for s in range(NS):
                    tiles = iter(xs[v][s])
                    if 0 <= it < NP:
                        if s == 0:
                            pe.wait_ge(rope_lo, 8 * (it + 1))
                            x_emptied(pe, it, ("mT", 0))
                            pe.wait_ge(mrow_in, 64 * (it + 1))
                        if s == NT:
                            x_emptied(pe, v, ("mT", 1))
                        for x in range(2):
                            for scores in (main_scores, pattern_scores):
                                scores(it, s, x)
                                for tile in islice(tiles, 1):
                                    x_tile(v, tile)
                        if s:
                            main_values(it, s - 1)
                        if s >= 3 and s % 2:
                            pattern_values(it, (s - 3) // 2)
                    if v >= 2:
                        if s == 0:
                            main_values(v - 2, NS - 1)
                        if s == 1:
                            pattern_values(v - 2, NT - 1)
                    for tile in tiles:
                        x_tile(v, tile)



def epilogue(nc, a, d, g, out):
    order = [(kind, t) for t in range(NT) for kind in range(2)] + [(2, t) for t in range(NT)]
    jobs = [("oT", j) for j in range(8)] + [("spoT", j) for j in range(2)]
    jobs += [("vo", j) for j in range(4)]
    jobs += [("o", t) for t in range(NT)]
    jobs += [("xT", k, q) for q in range(2) for k in range(NK)]
    for q in range(2):
        jobs += [("up", q, m) for m in range(8)] + [("down", q, m) for m in range(2)]
        jobs += [("yT", 2 * q + j) for j in range(2)]
    index = {j: n for n, j in enumerate(jobs)}
    by_act = [j[0] in ("oT", "spoT", "vo", "up", "down") for j in jobs]

    def last(kind):
        return max(n for n, j in enumerate(jobs) if j[0] == kind)

    with ExitStack() as ctx:
        def sb(name, shape, dt=F32):
            return ctx.enter_context(nc.sbuf_tensor(name, shape, dt))

        def sem(name):
            return ctx.enter_context(nc.semaphore(name))

        bank = [ctx.enter_context(nc.psum_tensor(f"c_bank{i}", [P, HALF], F32)) for i in range(8)]
        ctx_all = sb("ctx_all", [P, NP, S])
        pat_all = sb("pat_all", [P, 4, S])
        o_nat = sb("o_nat", [P, 2, H * DV])
        oT = sb("oT", [P, H, HID])
        spo_nat = sb("spo_nat", [P, 2, 4, 4, 32])
        spoT = sb("spoT", [P, 4, HID])
        wv = sb("wv", [P, H, LAT])
        vo = sb("vo", [P, NP, HID])
        res = sb("res", [P, NT, HID])
        wtmp = sb("wtmp", [P, 2048])
        wabs = sb("wabs", [P, 2048])
        wcode = sb("wcode", [P, 2048])
        amax = sb("amax", [P, 64])
        inv = sb("inv", [P, 64])
        wup = sb("wup", [P, NK, F], F32R)
        wdn = sb("wdn", [P, 8, HID], F32R)
        x2h = sb("x2h", [P, NK, S], F32R)
        x2l = sb("x2l", [P, NK, S], F32R)
        hf = sb("hf", [P, 2, HALF])
        hhi = sb("hhi", [P, 8, HALF], F32R)
        hlo = sb("hlo", [P, 8, HALF], F32R)
        yT = sb("yT", [P, 2, HALF])
        y = sb("y", [P, 2, HID])
        x2 = sb("x2", [P, NT, HID])
        ub = sb("ub", [P, 8])
        db = sb("db", [P, 2])
        stats = sb("c_stats", [P, NT, 6])
        mv = sb("c_mv", [P, 4, NT, 2])
        rstd = sb("c_rstd", [P, 4, NT])
        ident, gates = g["ident"], g["gates"]

        w_in = sem("c_w_in")
        ctx_in = sem("ctx_in")
        up_in = sem("up_in")
        dn_in = sem("dn_in")
        dn_free = sem("dn_free")
        bias_in = sem("bias_in")
        zeroed = sem("zeroed")
        spo_in = sem("spo_in")
        pe_job = sem("c_pe_job")
        ev_act = sem("c_ev_act")
        ev_dve = sem("c_ev_dve")
        own = sem("c_own")
        var_ready = sem("var_ready")
        rstd_ready = sem("c_rstd_ready")
        x2_ready = sem("x2_ready")
        pool_own = sem("c_pool_own")
        x2_hi = sem("x2_hi")
        quant = sem("quant")
        h_hi = sem("h_hi")
        h_full = sem("h_full")
        h_lo = sem("h_lo")
        y_ready = sem("y_ready")
        stored = sem("stored")

        def evacuated(eng, n):
            for s, flag in ((ev_act, True), (ev_dve, False)):
                count = sum(b == flag for b in by_act[:n + 1])
                if count:
                    eng.wait_ge(s, count)

        block = ctx.enter_context(nc.Block())

        @block.sync
        def _(sp):
            sp.dma_start(wtmp[:, :], a["ffn_up"].rearrange("(k p) n -> p k n", p=P)).then_inc(up_in, 16)
            sp.dma_start(o_nat[:, :, :], a["o_w"].rearrange("(m p) n -> p m n", p=P)).then_inc(w_in, 16)
            sp.dma_start(wv[:, :, :], a["kv_b_w"].rearrange("(h d) l -> d h l", d=NOPE + DV)[NOPE:NOPE + DV]).then_inc(w_in, 16)
            sp.wait_ge(zeroed, 1)
            for m in range(2):
                for q in range(4):
                    sp.dma_start(spo_nat[:, m, q, :, 0:PD],
                                 a["sp_o_w"][m * P:(m + 1) * P, 64 * q:64 * q + 64].rearrange("p (h e) -> p h e", e=PD)
                                 ).then_inc(spo_in, 16)
            for n in range(NP):
                sp.dma_start(ctx_all[:, n, :], d["ctx"][n]).then_inc(ctx_in, 16)
                sp.dma_start(pat_all[:, n // 2, (n % 2) * HALF:(n % 2 + 1) * HALF], d["pat"][n]).then_inc(ctx_in, 16)
            sp.dma_start(res[:, :, :], a["x"].rearrange("b (t p) n -> p (b t) n", p=P)).then_inc(bias_in, 16)
            sp.dma_start(ub[:, :], a["up_bias"]).then_inc(bias_in, 16)
            sp.dma_start(db[:, :], a["down_bias"]).then_inc(bias_in, 16)
            sp.wait_ge(dn_free, 1)
            sp.dma_start(wtmp[:, :], a["ffn_down"].rearrange("(k p) n -> p k n", p=P)).then_inc(dn_in, 16)
            o = out.rearrange("b (t p) n -> p (b t) n", p=P)
            for t in range(NT):
                sp.wait_ge(y_ready, t + 1)
                sp.dma_start(o[:, t, :], x2[:, t, :]).then_inc(stored, 16)
            sp.wait_ge(stored, 16 * NT)

        @block.gpsimd
        def _(pool):
            pool.memset(spo_nat[:, :, :, :, :], 0.0).then_inc(zeroed, 1)
            for n, (kind, t) in enumerate(order):
                pool.wait_ge(var_ready, n + 1)
                pool.tensor_scalar(rstd[:, kind, t:t + 1], mv[:, kind, t, 1:2], 1e-5, None, ALU.add).then_inc(pool_own, 1)
                pool.wait_ge(pool_own, n + 1)
                pool.tensor_tensor(rstd[:, kind, t:t + 1], rstd[:, kind, t:t + 1], g["mhalf"][:, 0:1],
                                   ALU.pow).then_inc(rstd_ready, 1)

        @block.tensor
        def _(pe):
            def transposes(n, blocks):
                for j, src in enumerate(blocks):
                    mm = pe.transpose(bank[n % 8][:, j * P:(j + 1) * P], src, ident[:, :])
                mm.then_inc(pe_job, 1)

            for n, job in enumerate(jobs):
                kind, o = job[0], bank[n % 8]
                if n >= 8:
                    evacuated(pe, n - 8)
                if kind == "oT":
                    pe.wait_ge(w_in, 32)
                    transposes(n, [o_nat[:, m, (2 * job[1] + h) * DV:(2 * job[1] + h + 1) * DV]
                                   for h in range(2) for m in range(2)])
                elif kind == "spoT":
                    pe.wait_ge(spo_in, 128)
                    transposes(n, [spo_nat[:, m, 2 * job[1] + q, :, :].rearrange("p h e -> p (h e)")
                                   for q in range(2) for m in range(2)])
                elif kind == "vo":
                    evacuated(pe, last("oT"))
                    for j in range(2):
                        for h in range(2):
                            hd = 2 * (2 * job[1] + j) + h
                            mm = pe.matmul(o[64 * h:64 * h + 64, j * HID:(j + 1) * HID], wv[:, hd, :], oT[:, hd, :],
                                           start=True, stop=True)
                    mm.then_inc(pe_job, 1)
                elif kind == "o":
                    t = slice(job[1] * P, (job[1] + 1) * P)
                    evacuated(pe, last("vo"))
                    pe.wait_ge(ctx_in, 256)
                    for j in range(NP):
                        pe.matmul(o[:, 0:HID], ctx_all[:, j, t], vo[:, j, :], start=(j == 0), stop=(j == NP - 1))
                    for j in range(4):
                        mm = pe.matmul(o[:, HID:2 * HID], pat_all[:, j, t], spoT[:, j, :], start=(j == 0), stop=(j == 3))
                    mm.then_inc(pe_job, 1)
                elif kind == "xT":
                    k, q = job[1:]
                    pe.wait_ge(x2_ready, 4 * q + 4)
                    transposes(n, [x2[:, 4 * q + j, k * P:(k + 1) * P] for j in range(4)])
                elif kind == "up":
                    q, m = job[1:]
                    half = slice(q * HALF, (q + 1) * HALF)
                    pe.wait_ge(quant, 1)
                    evacuated(pe, index[("xT", 1, q)])
                    for i, (k, x) in enumerate([(k, x) for k in range(NK) for x in (x2h, x2l)]):
                        mm = pe.matmul(o[:, :], wup[:, k, m * P:(m + 1) * P], x[:, k, half], start=(i == 0), stop=(i == 3))
                    mm.then_inc(pe_job, 1)
                elif kind == "down":
                    q, m = job[1:]
                    pe.wait_ge(quant, 2)
                    pe.wait_ge(h_lo, 8 * q + 8)
                    for i, (k, x) in enumerate([(k, x) for k in range(8) for x in (hhi, hlo)]):
                        mm = pe.matmul(o[:, :], wdn[:, k, m * P:(m + 1) * P], x[:, k, :], start=(i == 0), stop=(i == 15))
                    mm.then_inc(pe_job, 1)
                elif kind == "yT":
                    q, j = divmod(job[1], 2)
                    evacuated(pe, index[("down", q, 1)])
                    transposes(n, [yT[:, m, (2 * j + t) * P:(2 * j + t + 1) * P] for t in range(2) for m in range(2)])

        @block.scalar
        def _(act):
            ups = 0
            for n, job in enumerate(jobs):
                kind, o = job[0], bank[n % 8]
                if not by_act[n]:
                    if kind == "xT":
                        k, q = job[1:]
                        act.wait_ge(pe_job, n + 1)
                        act.activation(x2h[:, k, q * HALF:(q + 1) * HALF], o[:, :], ACT.Copy).then_inc(x2_hi, 1)
                    continue
                act.wait_ge(pe_job, n + 1)
                if kind == "oT":
                    act.activation(oT[:, 2 * job[1]:2 * job[1] + 2, :].rearrange("p h n -> p (h n)"), o[:, :],
                                   ACT.Copy).then_inc(ev_act, 1)
                elif kind == "spoT":
                    act.activation(spoT[:, 2 * job[1]:2 * job[1] + 2, :].rearrange("p h n -> p (h n)"), o[:, :],
                                   ACT.Copy).then_inc(ev_act, 1)
                elif kind == "vo":
                    act.activation(vo[:, 2 * job[1]:2 * job[1] + 2, :].rearrange("p h n -> p (h n)"), o[:, :],
                                   ACT.Copy).then_inc(ev_act, 1)
                elif kind == "up":
                    q, m = job[1:]
                    if ups == 0:
                        act.wait_ge(bias_in, 48)
                    if q:
                        act.wait_ge(pe_job, index[("down", 0, 1)] + 1)
                    if ups >= 2:
                        act.wait_ge(h_lo, ups - 1)
                    act.activation(hf[:, m % 2, :], o[:, :], ACT.Gelu_apprx_tanh, bias=ub[:, m:m + 1]).then_inc(h_full, 1)
                    act.activation(hhi[:, m, :], o[:, :], ACT.Gelu_apprx_tanh, bias=ub[:, m:m + 1]).then_inc(ev_act, 1)
                    ups += 1
                elif kind == "down":
                    q, m = job[1:]
                    if q:
                        act.wait_ge(pe_job, index[("yT", 1)] + 1)
                    act.activation(yT[:, m, :], o[:, :], ACT.Identity, bias=db[:, m:m + 1]).then_inc(ev_act, 1)

        @block.vector
        def _(dve):
            count = [0]

            def link(ins):
                count[0] += 1
                ins.then_inc(own, 1)
                dve.wait_ge(own, count[0])

            def quantize(natural, result, loaded, done):
                dve.wait_ge(loaded, 16)
                link(dve.transpose(wcode[:, :], natural))
                if done is not None:
                    dve.engine_nop().then_inc(done, 1)
                blocks = wcode[:, :].rearrange("p (b j) -> p b j", j=32)
                spread = lambda t: t[:, :].unsqueeze(2).broadcast_to((P, 64, 32))
                link(dve.tensor_reduce(amax[:, :], blocks, AX, ALU.max, apply_absolute_value=True))
                link(dve.tensor_scalar(amax[:, :], amax[:, :], 1e-30, None, ALU.max))
                link(dve.tensor_scalar(amax[:, :].bitcast(I32), amax[:, :].bitcast(I32), 0x7F800000, None, ALU.bitwise_and))
                link(dve.reciprocal(inv[:, :], amax[:, :]))
                link(dve.tensor_scalar(inv[:, :], inv[:, :], 4.0, None, ALU.mult))
                link(dve.tensor_scalar(amax[:, :], amax[:, :], 0.125, None, ALU.mult))
                ab = wabs[:, :].rearrange("p (b j) -> p b j", j=32)
                link(dve.tensor_scalar(wabs[:, :].bitcast(I32), wcode[:, :].bitcast(I32), 0x7FFFFFFF, None, ALU.bitwise_and))
                link(dve.tensor_tensor(ab, ab, spread(inv), ALU.mult))
                return blocks, spread

            def codes(result, blocks, spread, tmp):
                link(dve.tensor_scalar(tmp, wabs[:, :], 5.0, 2.0, ALU.is_ge, ALU.mult))
                for mid in (3.5, 2.5):
                    link(dve.scalar_tensor_tensor(tmp, wabs[:, :], mid, tmp, ALU.is_ge, ALU.add))
                link(dve.tensor_scalar(tmp, tmp, 2.0, None, ALU.mult))
                for mid in (1.75, 1.25, 0.75, 0.25):
                    link(dve.scalar_tensor_tensor(tmp, wabs[:, :], mid, tmp, ALU.is_ge, ALU.add))
                link(dve.tensor_scalar(wcode[:, :].bitcast(I32), wcode[:, :].bitcast(I32), -2147483648, None, ALU.bitwise_and))
                link(dve.tensor_tensor(tmp.bitcast(I32), tmp.bitcast(I32), wcode[:, :].bitcast(I32), ALU.bitwise_or))
                tb = tmp.rearrange("p (b j) -> p b j", j=32)
                link(dve.tensor_tensor(tb, tb, spread(amax), ALU.mult))
                link(dve.transpose(wabs[:, :], tmp))
                dve.tensor_copy(result, wabs[:, :]).then_inc(quant, 1)

            stat_n, norm_n = [0], [0]

            def statistics(kind, t, src):
                link(dve.bn_stats(stats[:, t, :], src))
                dve.bn_aggr(mv[:, kind, t, :], stats[:, t, :]).then_inc(var_ready, 1)
                stat_n[0] += 1

            def normalise(kind, t, dst, src):
                dve.wait_ge(rstd_ready, order.index((kind, t)) + 1)
                return dve.tensor_scalar(dst, src, mv[:, kind, t, 0:1], rstd[:, kind, t:t + 1], ALU.subtract, ALU.mult)

            blocks, spread = quantize(wtmp[:, :], wup, up_in, None)
            codes(wup[:, :, :].rearrange("p k n -> p (k n)"), blocks, spread, wtmp[:, :])
            dve.engine_nop().then_inc(dn_free, 1)
            for t in range(NT):
                n = index[("o", t)]
                o = bank[n % 8]
                dve.wait_ge(pe_job, n + 1)
                if t == 0:
                    dve.wait_ge(bias_in, 48)
                link(dve.tensor_scalar(y[:, t % 2, :], o[:, HID:2 * HID], gates[:, t, 1:2], None, ALU.mult))
                dve.scalar_tensor_tensor(y[:, t % 2, :], o[:, 0:HID], gates[:, t, 0:1], y[:, t % 2, :],
                                         ALU.mult, ALU.add).then_inc(ev_dve, 1)
                evacuated(dve, n)
                statistics(0, t, y[:, t % 2, :])
                link(normalise(0, t, y[:, t % 2, :], y[:, t % 2, :]))
                link(dve.tensor_tensor(res[:, t, :], res[:, t, :], y[:, t % 2, :], ALU.add))
                statistics(1, t, res[:, t, :])
                normalise(1, t, x2[:, t, :], res[:, t, :]).then_inc(x2_ready, 1)
            for q in range(2):
                for k in range(NK):
                    n = index[("xT", k, q)]
                    half = slice(q * HALF, (q + 1) * HALF)
                    dve.wait_ge(x2_hi, 2 * q + k + 1)
                    dve.tensor_tensor(x2l[:, k, half], bank[n % 8][:, :], x2h[:, k, half].bitcast(F32),
                                      ALU.subtract).then_inc(ev_dve, 1)
            blocks, spread = quantize(wtmp[:, :], wdn, dn_in, None)
            codes(wdn[:, :, :].rearrange("p k n -> p (k n)"), blocks, spread, wtmp[:, :])
            for q in range(2):
                for m in range(8):
                    i = 8 * q + m
                    dve.wait_ge(h_full, i + 1)
                    dve.wait_ge(ev_act, sum(by_act[:index[("up", q, m)] + 1]))
                    dve.tensor_tensor(hlo[:, m, :], hf[:, m % 2, :], hhi[:, m, :].bitcast(F32),
                                      ALU.subtract).then_inc(h_lo, 1)
                for j in (2 * q, 2 * q + 1):
                    n = index[("yT", j)]
                    dve.wait_ge(pe_job, n + 1)
                    for t in range(2):
                        tt = 2 * j + t
                        ins = dve.tensor_copy(y[:, t, :], bank[n % 8][:, t * HID:(t + 1) * HID])
                        if t:
                            ins.then_inc(ev_dve, 1)
                            evacuated(dve, n)
                        else:
                            link(ins)
                    for t in range(2):
                        tt = 2 * j + t
                        statistics(2, tt, y[:, t, :])
                        link(normalise(2, tt, y[:, t, :], y[:, t, :]))
                        dve.tensor_tensor(x2[:, tt, :], res[:, tt, :], y[:, t, :], ALU.add).then_inc(y_ready, 1)


NAMES = {
    "x": "L0_attn_hidden_states", "q_a_w": "L0_attn_q_a_w", "q_a_ln_w": "L0_attn_q_a_ln_w",
    "q_b_w": "L0_attn_q_b_w", "kv_a_w": "L0_attn_kv_a_w", "kv_a_ln_w": "L0_attn_kv_a_ln_w",
    "kv_b_w": "L0_attn_kv_b_w", "o_w": "L0_attn_o_w", "sp_q_w": "L0_attn_sp_q_w",
    "sp_k_w": "L0_attn_sp_k_w", "sp_v_w": "L0_attn_sp_v_w", "sp_o_w": "L0_attn_sp_o_w",
    "gate_w": "L0_attn_gate_w", "gate_b": "L0_attn_gate_b", "ffn_up": "L0_ffn_up_kernel",
    "up_bias": "L0_ffn_up_bias", "ffn_down": "L0_ffn_down_kernel", "down_bias": "L0_ffn_down_bias",
}


def build(nc, a, out):
    def scratch(name, shape, dt=F32):
        return nc.dram_tensor(name, shape, dt, kind="Internal").ap()

    d = {
        "wst": scratch("wst_d", (NP, P, NW * P)),
        "spqk": scratch("spqk_d", (2, 2, HID, S)),
        "vp": scratch("vp_d", (P, NT * HID)),
        "ctx": scratch("ctx_d", (NP, P, S)),
        "pat": scratch("pat_d", (NP, P, HALF)),
    }
    with ExitStack() as ctx:
        def sb(name, shape, dt=F32):
            return ctx.enter_context(nc.sbuf_tensor(name, shape, dt))

        g = {"ident": sb("ident", [P, P]), "gates": sb("gates", [P, NT, 2]), "mhalf": sb("mhalf", [P, 2 * NT])}
        with ExitStack() as inner:
            def sbi(name, shape, dt=F32):
                return inner.enter_context(nc.sbuf_tensor(name, shape, dt))

            g |= {
                "sel_f": sbi("sel_f", [64, 256]), "sel": sbi("sel", [64, 256], F32R),
                "cos": sbi("cos", [P, S]), "sin": sbi("sin", [P, S]),
                "cdup": sbi("cdup", [P, NT, P]),
                "xh": sbi("xh", [P, NK, S], F32R), "xl": sbi("xl", [P, NK, S], F32R),
                "qm0h": sbi("qm0h", [P, S], F32R), "qm0l": sbi("qm0l", [P, S], F32R), "qm1": sbi("qm1", [P, S], F32R),
                "kh": sbi("kh", [P, 4, S], F32R), "kl": sbi("kl", [P, 4, S], F32R),
            }
            prologue(nc, a, d, g)
            attention(nc, a, d, g)
        epilogue(nc, a, d, g, out)



def constants():
    consts = np.zeros((P, P + 256), np.float32)
    consts[:, 0:P] = np.eye(P, dtype=np.float32)
    for b in (0, 32):
        for h in range(2):
            consts[b + h, P + h * P:P + (h + 1) * P] = -1.0
    f32 = np.float32
    inv_freq = f32(1.0) / np.power(f32(10000.0), np.arange(0, ROPE, 2, dtype=f32) / f32(ROPE))
    angle = np.outer(inv_freq, np.arange(S, dtype=f32)).astype(f32)
    c, s = np.cos(angle), np.sin(angle)
    rope = np.stack([np.concatenate([c] * 4), np.concatenate([-s, s] * 2)]).astype(f32)
    return consts, rope


def kernel(**inputs):
    import concourse.bacc as bacc
    from concourse.bass_utils import run_bass_kernel_spmd

    nc = bacc.Bacc("TRN2", target_bir_lowering=False, num_devices=1, dynamic_dma_scratch_size=1024)
    arrays, aps = {}, {}
    for short, name in NAMES.items():
        v = np.ascontiguousarray(inputs[name])
        if short in ("up_bias", "down_bias"):
            v = np.ascontiguousarray(v.reshape(-1, P).T)
        arrays[f"in_{short}"] = v
    arrays["in_consts"], arrays["in_rope"] = constants()
    for key, v in arrays.items():
        aps[key[3:]] = nc.dram_tensor(key, v.shape, F32, kind="ExternalInput").ap()
    out = nc.dram_tensor("out_0", (1, S, HID), F32, kind="ExternalOutput").ap()
    build(nc, aps, out)
    r = run_bass_kernel_spmd(nc, [arrays], core_ids=[0])
    return r.results[0]["out_0"]
```

```python
from contextlib import ExitStack
from itertools import islice

import numpy as np

import concourse.bass as bass
from concourse import mybir

F32 = mybir.dt.float32
F32R = mybir.dt.float32r
I32 = mybir.dt.int32
ALU = mybir.AluOpType
ACT = mybir.ActivationFunctionType
AX = mybir.AxisListType.X

P = 128
S, HID = 1024, 256
H, NOPE, ROPE, DV = 16, 128, 64, 128
DQ = NOPE + ROPE
QR, LAT = 192, 64
PH, PD = 16, 16
F = 1024
NT = S // P
NK = HID // P
NP = H // 2
HALF = 512
W1 = QR + LAT + 2
MAIN_SCALE = float(DQ) ** -0.5
PAT_SCALE = float(PD) ** -0.5
NW = 12



def prologue(nc, a, d, g):
    jobs = [("xT", k, q) for k in range(NK) for q in range(2)]
    jobs += [("w1T", k) for k in range(NK)]
    jobs += [("proj1", t) for t in range(NT)]
    jobs += [("spT", w) for w in range(3)]
    jobs += [("kpT", k, q) for k in range(NK) for q in range(2)]
    jobs += [("pe0T", q) for q in range(2)] + [("pe1T", q) for q in range(2)]
    jobs += [("lat0", q) for q in range(2)] + [("lat1", q) for q in range(2)]
    jobs += [("spqk", w, m, h) for w in range(2) for m in range(2) for h in range(2)]
    jobs += [("spv", q) for q in range(NT // 2)]
    jobs += [("qm0T", q) for q in range(2)] + [("qm1T", q) for q in range(2)]
    jobs += [("cT", q) for q in range(2)]
    split = ("spqk", "qm0T", "qm1T")
    by_act = [j[0] not in split and j[0] != "cT" and n % 2 == 0 for n, j in enumerate(jobs)]
    index = {j: n for n, j in enumerate(jobs)}

    first_spqk = index[("spqk", 0, 0, 0)]

    def last(kind):
        return max(n for n, j in enumerate(jobs) if j[0] == kind)

    with ExitStack() as ctx:
        def sb(name, shape, dt=F32):
            return ctx.enter_context(nc.sbuf_tensor(name, shape, dt))

        def sem(name):
            return ctx.enter_context(nc.semaphore(name))

        bank = [ctx.enter_context(nc.psum_tensor(f"a_bank{i}", [P, HALF], F32)) for i in range(8)]
        xn = sb("xn", [P, NT, HID])
        xT = sb("xT", [P, NK, S])
        qa_nat = sb("qa_nat", [96, 2, HID])
        lora_nat = sb("lora_nat", [LAT, HID])
        gate_nat = sb("gate_nat", [2, HID])
        sp_nat = sb("sp_nat", [P, 3, 2, HID])
        kpe_nat = sb("kpe_nat", [P, NP, HID])
        wqn = sb("wqn", [P, H, QR])
        wpe = sb("wpe", [P, NP, 256])
        wk = sb("wk", [P, H, LAT])
        w1T = sb("w1T", [P, NK, W1])
        spT = sb("spT", [P, 3, NK, HID])
        kpT = sb("kpT", [P, NK, S])
        aq = [sb("aq0", [P, NP, 256]), sb("aq1", [P, NP, 256])]
        split_hi = sb("split_hi", [P, 2, S], F32R)
        split_lo = sb("split_lo", [P, 2, S], F32R)
        m1 = sb("m1", [P, NT, W1])
        cT = sb("cT", [P, S])
        sp_hi = sb("sp_hi", [P, 2, HALF], F32R)
        sp_lo = sb("sp_lo", [P, 2, HALF], F32R)
        vf = sb("vf", [P, NT, HID])
        lnq = sb("lnq", [P, QR])
        lnkv = sb("lnkv", [P, LAT])
        gate_b = sb("gate_b", [P, 2])
        stats = sb("stats", [P, NT, 6])
        mv = sb("mv", [P, NT, 2])
        rstd = sb("rstd", [P, NT])
        junk = sb("junk", [P, QR])
        ssq = sb("ssq", [P, 2, NT])
        rms = sb("rms", [P, 2, NT])
        gl = sb("gl", [P, NT, 2])
        gmax = sb("gmax", [P, NT])
        gsum = sb("gsum", [P, NT])
        ident, cdup, gates = g["ident"], g["cdup"], g["gates"]

        s_x = [sem(f"x_in{i}") for i in range(2)]
        s_ident, s_const, s_w1, s_sp, s_kpe, s_wq, s_ln = (
            sem(n) for n in ("ident_in", "const_in", "w1_in", "sp_in", "kpe_in", "wq_in", "ln_in"))
        stat = sem("stat")
        rstd_ready = sem("rstd_ready")
        xn_ready = sem("xn_ready")
        pe_job = sem("pe_job")
        ev_act = sem("ev_act")
        ev_dve = sem("ev_dve")
        hi_ready = sem("hi_ready")
        ssq_ready = sem("ssq_ready")
        rms_ready = sem("rms_ready")
        norm_ready = sem("norm_ready")
        wsplit_hi = sem("wsplit_hi")
        wsplit_lo = sem("wsplit_lo")
        wstored = [sem(f"wstored{i}") for i in range(2)]
        spstored = [sem(f"spstored{i}") for i in range(2)]
        vstored = sem("vstored")
        dve_own = sem("dve_own")
        pool_own = sem("pool_own")
        logits = sem("logits")
        gexp = sem("gexp")

        def evacuated(eng, n):
            for s, flag in ((ev_act, True), (ev_dve, False)):
                count = sum(b == flag for b in by_act[:n + 1])
                if count:
                    eng.wait_ge(s, count)

        block = ctx.enter_context(nc.Block())

        @block.sync
        def _(sp):
            x = a["x"].rearrange("b (t p) n -> p (b t) n", p=P)
            sp.dma_start(xn[:, 0:4, :], x[:, 0:4, :]).then_inc(s_x[0], 16)
            sp.dma_start(xn[:, 4:8, :], x[:, 4:8, :]).then_inc(s_x[1], 16)
            sp.dma_start(ident[:, :], a["consts"][:, 0:P]).then_inc(s_ident, 16)
            sp.dma_start(g["sel_f"][0:64, :], a["consts"][0:64, P:P + 256]).then_inc(s_const, 16)
            sp.dma_start(qa_nat[:, :, :], a["q_a_w"].rearrange("(m p) n -> p m n", p=96)).then_inc(s_w1, 16)
            sp.dma_start(lora_nat[:, :], a["kv_a_w"][0:LAT, :]).then_inc(s_w1, 16)
            sp.dma_start(gate_nat[:, :], a["gate_w"]).then_inc(s_w1, 16)
            for w, name in enumerate(("sp_q_w", "sp_k_w", "sp_v_w")):
                sp.dma_start(sp_nat[:, w, :, :], a[name].rearrange("(m p) n -> p m n", p=P)).then_inc(s_sp, 16)
            sp.dma_start(kpe_nat[:, :, :],
                         a["kv_a_w"][LAT:LAT + H * ROPE, :].rearrange("(n p) k -> p n k", p=P)).then_inc(s_kpe, 16)
            heads = a["q_b_w"].rearrange("(h d) r -> d h r", d=DQ)
            for h in range(2):
                rows = heads[NOPE:DQ].rearrange("d (n two) r -> d n two r", two=2)[:, :, h, :]
                at = slice(64 * h, 64 * h + 64)
                sp.dma_start(wpe[at, :, 0:QR], rows).then_inc(s_wq, 16)
                sp.dma_start(wpe[at, :, QR:256], rows[:, :, P:QR]).then_inc(s_wq, 16)
            sp.dma_start(wqn[:, :, :], heads[0:NOPE]).then_inc(s_wq, 16)
            sp.dma_start(wk[:, :, :], a["kv_b_w"].rearrange("(h d) l -> d h l", d=NOPE + DV)[0:NOPE]).then_inc(s_wq, 16)
            sp.dma_start(lnq[:, :], a["q_a_ln_w"].rearrange("(a n) -> a n", a=1).broadcast_to((P, QR))).then_inc(s_ln, 16)
            sp.dma_start(lnkv[:, :], a["kv_a_ln_w"].rearrange("(a n) -> a n", a=1).broadcast_to((P, LAT))).then_inc(s_ln, 16)
            sp.dma_start(gate_b[:, :], a["gate_b"].rearrange("(a n) -> a n", a=1).broadcast_to((P, 2))).then_inc(s_ln, 16)
            sp.dma_start(g["cos"][:, :], a["rope"][0]).then_inc(s_const, 16)
            sp.dma_start(g["sin"][:, :], a["rope"][1]).then_inc(s_const, 16)
            stage = d["wst"].rearrange("n p (c j) -> p n c j", j=P)

            def store_weights(c):
                sp.wait_ge(wsplit_hi, c + 1)
                sp.wait_ge(wsplit_lo, c + 1)
                for lo, t in enumerate((split_hi, split_lo)):
                    t = t[:, c % 2, :].bitcast(F32)
                    if c < 2:
                        sp.dma_start(stage[:, :, 8 + 2 * c + lo, :],
                                     t.rearrange("p (n j) -> p n j", j=P)).then_inc(wstored[c % 2], 16)
                    else:
                        kind, q = (c - 2) // 2, (c - 2) % 2
                        v = t.rearrange("p (n b j) -> p n b j", b=2, j=P)
                        for b in range(2):
                            sp.dma_start(stage[:, 4 * q:4 * q + 4, 4 * b + 2 * kind + lo, :],
                                         v[:, :, b, :]).then_inc(wstored[c % 2], 16)

            store_weights(0)
            store_weights(1)
            for i in range(8):
                w, m, h = jobs[first_spqk + i][1:]
                sp.wait_ge(ev_dve, sum(not b for b in by_act[:first_spqk + i + 1]))
                for lo, t in enumerate((sp_hi, sp_lo)):
                    sp.dma_start(d["spqk"][w, lo, m * P:(m + 1) * P, h * HALF:(h + 1) * HALF],
                                 t[:, i % 2, :].bitcast(F32)).then_inc(spstored[i % 2], 16)
                if i % 2:
                    store_weights(2 + i // 2)
            evacuated(sp, last("spv"))
            sp.dma_start(d["vp"], vf[:, :, :].rearrange("p t n -> p (t n)")).then_inc(vstored, 16)
            sp.wait_ge(vstored, 16)
            for s in wstored:
                sp.wait_ge(s, 16 * (2 + 2 * 4))
            for s in spstored:
                sp.wait_ge(s, 16 * 8)
            sp.wait_ge(s_const, 48)

        @block.gpsimd
        def _(pool):
            pool.memset(g["mhalf"][:, :], -0.5).then_inc(pool_own, 1)
            pool.wait_ge(stat, 2 * NT)
            pool.tensor_scalar(rstd[:, :], mv[:, :, 1], 1e-5, None, ALU.add).then_inc(pool_own, 1)
            pool.wait_ge(pool_own, 2)
            pool.tensor_tensor(rstd[:, :], rstd[:, :], g["mhalf"][:, 0:NT], ALU.pow).then_inc(rstd_ready, 1)
            pool.wait_ge(ssq_ready, 2 * NT)
            pool.tensor_scalar(rms[:, :, :], ssq[:, :, :], 1e-6, None, ALU.add).then_inc(pool_own, 1)
            pool.wait_ge(pool_own, 3)
            pool.tensor_tensor(rms[:, :, :], rms[:, :, :], g["mhalf"][:, 0:2 * NT].rearrange("p (a b) -> p a b", a=2),
                               ALU.pow).then_inc(rms_ready, 1)

        @block.tensor
        def _(pe):
            def transposes(n, blocks):
                at = 0
                for src in blocks:
                    k, m = src.shape[0], src.shape[1]
                    mm = pe.transpose(bank[n % 8][0:m, at:at + k], src, ident[0:k, 0:k])
                    at += k
                mm.then_inc(pe_job, 1)

            pe.wait_ge(s_ident, 16)
            for n, job in enumerate(jobs):
                kind, out = job[0], bank[n % 8]
                if n >= 8:
                    evacuated(pe, n - 8)
                if kind == "xT":
                    k, q = job[1:]
                    pe.wait_ge(xn_ready, 4 * q + 4)
                    transposes(n, [xn[:, 4 * q + j, k * P:(k + 1) * P] for j in range(4)])
                elif kind == "w1T":
                    k = slice(job[1] * P, (job[1] + 1) * P)
                    pe.wait_ge(s_w1, 48)
                    transposes(n, [qa_nat[:, 0, k], qa_nat[:, 1, k], lora_nat[:, k], gate_nat[:, k]])
                elif kind == "proj1":
                    t = slice(job[1] * P, (job[1] + 1) * P)
                    evacuated(pe, last("w1T"))
                    for k in range(NK):
                        mm = pe.matmul(out[:, 0:W1], xT[:, k, t], w1T[:, k, :], start=(k == 0), stop=(k == NK - 1))
                    mm.then_inc(pe_job, 1)
                elif kind == "spT":
                    pe.wait_ge(s_sp, 48)
                    transposes(n, [sp_nat[:, job[1], m, k * P:(k + 1) * P] for k in range(NK) for m in range(2)])
                elif kind == "kpT":
                    k, q = job[1:]
                    pe.wait_ge(s_kpe, 16)
                    transposes(n, [kpe_nat[:, 4 * q + j, k * P:(k + 1) * P] for j in range(4)])
                elif kind in ("pe0T", "pe1T"):
                    r = slice(0, P) if kind == "pe0T" else slice(P, 256)
                    pe.wait_ge(s_wq, 96)
                    transposes(n, [wpe[:, 4 * job[1] + j, r] for j in range(4)])
                elif kind == "lat0":
                    for j in range(8):
                        h = 8 * job[1] + j
                        mm = pe.matmul(out[:, 64 * j:64 * j + 64], wqn[:, h, 0:P], wk[:, h, :], start=True, stop=True)
                    mm.then_inc(pe_job, 1)
                elif kind == "lat1":
                    for j in range(8):
                        h = 8 * job[1] + j
                        for r in (0, 64):
                            mm = pe.matmul(out[r:r + 64, 64 * j:64 * j + 64], wqn[:, h, P:QR], wk[:, h, :],
                                           start=True, stop=True)
                    mm.then_inc(pe_job, 1)
                elif kind == "spqk":
                    w, m, h = job[1:]
                    evacuated(pe, last("spT"))
                    for k in range(NK):
                        mm = pe.matmul(out[:, :], spT[:, w, k, m * P:(m + 1) * P], xT[:, k, h * HALF:(h + 1) * HALF],
                                       start=(k == 0), stop=(k == NK - 1))
                    mm.then_inc(pe_job, 1)
                elif kind == "spv":
                    for j in range(2):
                        t = 2 * job[1] + j
                        for k in range(NK):
                            mm = pe.matmul(out[:, j * HID:(j + 1) * HID], xT[:, k, t * P:(t + 1) * P], spT[:, 2, k, :],
                                           start=(k == 0), stop=(k == NK - 1))
                    mm.then_inc(pe_job, 1)
                elif kind in ("qm0T", "qm1T"):
                    r = slice(0, P) if kind == "qm0T" else slice(P, 256)
                    pe.wait_ge(norm_ready, 1)
                    transposes(n, [m1[:, 4 * job[1] + j, r] for j in range(4)])
                elif kind == "cT":
                    transposes(n, [cdup[:, 4 * job[1] + j, :] for j in range(4)])

        def plain(n):
            job = jobs[n]
            kind, out = job[0], bank[n % 8]
            if kind == "xT":
                return xT[:, job[1], job[2] * HALF:(job[2] + 1) * HALF], out[:, :]
            if kind == "w1T":
                return w1T[:, job[1], :], out[:, 0:W1]
            if kind == "proj1":
                return m1[:, job[1], :], out[:, 0:W1]
            if kind == "spT":
                return spT[:, job[1], :, :].rearrange("p k n -> p (k n)"), out[:, :]
            if kind == "kpT":
                return kpT[:, job[1], job[2] * HALF:(job[2] + 1) * HALF], out[:, :]
            if kind in ("pe0T", "pe1T"):
                to = aq[kind == "pe1T"][:, 4 * job[1]:4 * job[1] + 4, :]
                return (to.rearrange("p n (b j) -> p n b j", j=64)[:, :, 0:4:3, :],
                        out[:, :].rearrange("p (n b j) -> p n b j", b=2, j=64))
            if kind in ("lat0", "lat1"):
                to = aq[kind == "lat1"][:, 4 * job[1]:4 * job[1] + 4, 64:192]
                return to, out[:, :].rearrange("p (n j) -> p n j", j=P)
            if kind == "spv":
                return vf[:, 2 * job[1]:2 * job[1] + 2, :].rearrange("p t n -> p (t n)"), out[:, :]
            if kind == "cT":
                return cT[:, job[1] * HALF:(job[1] + 1) * HALF], out[:, :]
            return None

        def hi_of(n):
            job = jobs[n]
            if job[0] == "spqk":
                return sp_hi[:, (n - first_spqk) % 2, :]
            cols = slice(job[1] * HALF, (job[1] + 1) * HALF)
            return (g["qm0h"] if job[0] == "qm0T" else g["qm1"])[:, cols]

        chunks = [kpT[:, 0, :], kpT[:, 1, :]] + [
            aq[kind][:, 4 * q:4 * q + 4, :].rearrange("p n j -> p (n j)") for kind in range(2) for q in range(2)]
        chunk_jobs = [last("kpT")] * 2 + [last("lat0")] * 2 + [last("lat1")] * 2

        @block.scalar
        def _(act):
            def weight_hi(c):
                evacuated(act, chunk_jobs[c])
                if c >= 2:
                    act.wait_ge(wstored[c % 2], 32 if c < 4 else 96)
                act.activation(split_hi[:, c % 2, :], chunks[c], ACT.Copy).then_inc(wsplit_hi, 1)

            for n, job in enumerate(jobs):
                if job[0] in split:
                    act.wait_ge(pe_job, n + 1)
                    if job[0] == "spqk" and n - first_spqk >= 2:
                        i = n - first_spqk
                        act.wait_ge(spstored[i % 2], 32 * (i // 2))
                    act.activation(hi_of(n), bank[n % 8][:, :], ACT.Copy).then_inc(hi_ready, 1)
                elif by_act[n]:
                    act.wait_ge(pe_job, n + 1)
                    act.activation(*plain(n), ACT.Copy).then_inc(ev_act, 1)
                if n == last("xT") + 2:
                    evacuated(act, last("xT"))
                    act.activation(g["xh"][:, :, :], xT[:, :, :], ACT.Copy).then_inc(hi_ready, 1)
                if n == last("spT"):
                    evacuated(act, last("proj1"))
                    for t in range(NT):
                        act.activation(junk[:, :], m1[:, t, 0:QR], ACT.Square, scale=float(QR) ** -0.5,
                                       accum_out=ssq[:, 0, t:t + 1]).then_inc(ssq_ready, 1)
                        act.wait_ge(ssq_ready, 2 * t + 1)
                        act.activation(junk[:, 0:LAT], m1[:, t, QR:QR + LAT], ACT.Square, scale=float(LAT) ** -0.5,
                                       accum_out=ssq[:, 1, t:t + 1]).then_inc(ssq_ready, 1)
                        act.wait_ge(ssq_ready, 2 * t + 2)
                if n == last("kpT") + 2:
                    weight_hi(0)
                if n == last("kpT") + 4:
                    weight_hi(1)
                if job[0] == "spqk" and (n - first_spqk) % 2:
                    weight_hi(2 + (n - first_spqk) // 2)
            act.wait_ge(logits, 1)
            act.activation(gl[:, :, :], gl[:, :, :], ACT.Exp).then_inc(gexp, 1)
            evacuated(act, last("cT"))
            for b in range(4):
                rows = slice(64, P) if b % 2 == 0 else slice(0, 64)
                act.activation(g["kh"][rows, b, :], cT[rows, :], ACT.Copy).then_inc(hi_ready, 1)
            act.wait_ge(s_const, 48)
            act.activation(g["sel"][0:64, :], g["sel_f"][0:64, :], ACT.Copy).then_inc(hi_ready, 1)

        @block.vector
        def _(dve):
            own = [0]

            def link(ins):
                own[0] += 1
                ins.then_inc(dve_own, 1)
                dve.wait_ge(dve_own, own[0])

            his = [0]

            def weight_lo(c):
                dve.wait_ge(wsplit_hi, c + 1)
                dve.tensor_tensor(split_lo[:, c % 2, :], chunks[c], split_hi[:, c % 2, :].bitcast(F32),
                                  ALU.subtract).then_inc(wsplit_lo, 1)

            for q in range(2):
                dve.wait_ge(s_x[q], 16)
                for t in range(4 * q, 4 * q + 4):
                    dve.bn_stats(stats[:, t, :], xn[:, t, :]).then_inc(stat, 1)
            dve.wait_ge(stat, NT)
            for t in range(NT):
                dve.bn_aggr(mv[:, t, :], stats[:, t, :]).then_inc(stat, 1)
            dve.wait_ge(rstd_ready, 1)
            for t in range(NT):
                dve.tensor_scalar(xn[:, t, :], xn[:, t, :], mv[:, t, 0:1], rstd[:, t:t + 1],
                                  ALU.subtract, ALU.mult).then_inc(xn_ready, 1)
            for n, job in enumerate(jobs):
                kind = job[0]
                if kind in split:
                    his[0] += 1
                    dve.wait_ge(hi_ready, 1 + his[0])
                    src, hi = bank[n % 8], hi_of(n)
                    if kind == "spqk":
                        lo = sp_lo[:, (n - first_spqk) % 2, :]
                        dve.tensor_tensor(lo, src[:, :], hi.bitcast(F32), ALU.subtract).then_inc(ev_dve, 1)
                    elif kind == "qm0T":
                        lo = g["qm0l"][:, job[1] * HALF:(job[1] + 1) * HALF]
                        dve.tensor_tensor(lo, src[:, :], hi.bitcast(F32), ALU.subtract).then_inc(ev_dve, 1)
                    else:
                        dve.tensor_tensor(hi[64:P, :], src[64:P, :], hi[64:P, :].bitcast(F32),
                                          ALU.subtract).then_inc(ev_dve, 1)
                elif not by_act[n]:
                    dve.wait_ge(pe_job, n + 1)
                    dve.tensor_copy(*plain(n)).then_inc(ev_dve, 1)
                if n == last("xT") + 4:
                    dve.wait_ge(hi_ready, 1)
                    link(dve.tensor_tensor(g["xl"][:, :, :], xT[:, :, :], g["xh"][:, :, :].bitcast(F32), ALU.subtract))
                if n == last("kpT") + 2:
                    dve.wait_ge(rms_ready, 1)
                    dve.wait_ge(s_ln, 48)
                    for t in range(NT):
                        for r in (0, 64):
                            ins = dve.scalar_tensor_tensor(cdup[:, t, r:r + 64], m1[:, t, QR:QR + LAT],
                                                           rms[:, 1, t:t + 1], lnkv[:, :], ALU.mult, ALU.mult)
                    link(ins)
                    for t in range(NT):
                        ins = dve.scalar_tensor_tensor(m1[:, t, 0:QR], m1[:, t, 0:QR], rms[:, 0, t:t + 1],
                                                       lnq[:, :], ALU.mult, ALU.mult)
                    link(ins)
                    link(dve.tensor_copy(m1[:, :, QR:256], m1[:, :, P:QR]))
                    dve.tensor_tensor(gl[:, :, :], m1[:, :, 256:258],
                                      gate_b[:, :].unsqueeze(1).broadcast_to((P, NT, 2)), ALU.add).then_inc(norm_ready, 1)
                    dve.wait_ge(norm_ready, 1)
                    link(dve.tensor_reduce(gmax[:, :], gl[:, :, :], AX, ALU.max))
                    dve.tensor_tensor(gl[:, :, :], gl[:, :, :], gmax[:, :].unsqueeze(2).broadcast_to((P, NT, 2)),
                                      ALU.subtract).then_inc(logits, 1)
                if n == last("kpT") + 3:
                    weight_lo(0)
                if n == last("kpT") + 5:
                    weight_lo(1)
                if kind == "spqk" and (n - first_spqk) % 2:
                    weight_lo(2 + (n - first_spqk) // 2)
            dve.wait_ge(gexp, 1)
            link(dve.tensor_reduce(gsum[:, :], gl[:, :, :], AX, ALU.add))
            link(dve.reciprocal(gsum[:, :], gsum[:, :]))
            link(dve.tensor_tensor(gates[:, :, :], gl[:, :, :], gsum[:, :].unsqueeze(2).broadcast_to((P, NT, 2)),
                                   ALU.mult))
            for b in range(4):
                dve.wait_ge(hi_ready, 2 + his[0] + b)
                rows = slice(64, P) if b % 2 == 0 else slice(0, 64)
                ins = dve.tensor_tensor(g["kl"][rows, b, :], cT[rows, :], g["kh"][rows, b, :].bitcast(F32), ALU.subtract)
            link(ins)



X_STEPS = [
    [("mm", 3), ("P", 0)],
    [("S", 1), ("mm", 3), ("P", 1)],
    [("o", 1), ("mm", 3), ("P", 2)],
    [("o", 1), ("mm", 3), ("P", 3)],
    [("o", 1), ("pm", 4)],
    [("o", 1), ("pm", 3), ("P", 4)],
    [("mT", 1), ("pm", 4)],
    [("pm", 4), ("P", 5)],
    [("pm", 5)],
    [("S", 0), ("pm", 4)],
    [("pm", 4)],
    [("pm", 4)],
    [("pT", 0), ("pT", 1), ("mm", 4)],
    [("mm", 6)],
    [("mm", 6)],
    [("mT", 0), ("mm", 4)],
]
X_FIRST = [
    [("P", 0), ("P", 1)],
    [("P", 2), ("P", 3)],
    [("pm", 4)],
    [("pm", 4)],
    [("oT", 1), ("pm", 2), ("oT", 1), ("pm", 2)],
    [("oT", 1), ("pm", 2), ("oT", 1), ("pm", 2)],
    [("oT", 1), ("pm", 2), ("oT", 1), ("pm", 1)],
    [("P", 4), ("oT", 1), ("pm", 2)],
    [("P", 5), ("oT", 1), ("pm", 2)],
    [("oT", 1), ("pm", 2), ("oT", 1), ("pm", 1)],
    [("vo", 1), ("pm", 2), ("vo", 1), ("pm", 1)],
    [("vo", 1), ("pm", 2), ("vo", 1), ("pm", 1)],
    [("pT", 0), ("pT", 1), ("mm", 4)],
    [("mm", 6)],
    [("mm", 6)],
    [("mT", 0), ("mm", 4)],
]
MM_LATE = 20
BY_ACT = ("mT", "pT", "S", "oT", "vo", "o")


def x_steps(v):
    count = {"pm": 0, "mm": MM_LATE if v else 0, "oT": 0, "vo": 0, "o": 0}
    steps = []
    for tiles in X_STEPS if v else X_FIRST:
        step = []
        for kind, n in tiles:
            numbers = [n]
            if kind in count:
                numbers = [(count[kind] + i) % 32 for i in range(n)]
                count[kind] += n
            for i in numbers:
                if (kind, i) == ("mT", 1) or kind == "mm" and i >= MM_LATE:
                    here = 1 <= v <= NP
                elif kind == "o":
                    here = v == NP + 1
                elif kind == "S":
                    here = v >= 2 if i else 1 <= v <= NP
                else:
                    here = v < NP
                if here:
                    step.append((kind, i))
        steps.append(step)
    return steps


def attention(nc, a, d, g):
    NS = 16
    slots = range(NP + 2)
    xs = [x_steps(v) for v in slots]
    x_index = {}
    for v in slots:
        for step in xs[v]:
            for tile in step:
                x_index[(v, *tile)] = len(x_index)

    x_tiles = [(t[0], t[1:]) for t in x_index]

    with ExitStack() as ctx:
        def sb(name, shape, dt=F32):
            return ctx.enter_context(nc.sbuf_tensor(name, shape, dt))

        def ps(name):
            return ctx.enter_context(nc.psum_tensor(name, [P, HALF], F32))

        def sem(name):
            return ctx.enter_context(nc.semaphore(name))

        st = [ps(f"st{i}") for i in range(4)]
        xb = [ps(f"xb{i}") for i in range(2)]
        pvm = ps("pvm")
        pvp = ps("pvp")
        kh, kl = g["kh"], g["kl"]
        qh, ql, wst = g["qh"], g["ql"], g["wst"]
        raw, rot, rc = g["raw"], g["rot"], g["rc"]
        em = g["em"]
        ep = sb("ep", [P, 8, HALF])
        acc = sb("acc", [P, 2, HALF])
        pq = sb("pq", [P, 2, 2, HALF], F32R)
        pk = sb("pk", [P, 2, 2, S], F32R)
        vp = sb("vp", [P, 2, NT, 4, 32])
        ones = sb("ones", [P, 64])
        mr = sb("mr", [64, S], F32R)
        mrp = sb("mrp", [4, HALF], F32R)
        m2 = sb("m2", [P, 2, 2, 4, 2])
        ms = sb("ms", [P, 2, 4, 2])
        m2p = sb("m2p", [P, 4, 4, 2])
        msp = sb("msp", [P, 4, 4])
        ctxr = sb("ctxr", [P, HALF])
        sums = sb("sums", [P, HALF])
        rec = sb("rec", [P, HALF])
        pvr = sb("pvr", [P, HALF])
        prec = sb("prec", [P, HALF])
        amax = sb("amax", [P, 32])
        inv = sb("inv", [P, 32])
        ident, sel, cdup = g["ident"], g["sel"], g["cdup"]
        o_nat = em[:, :, :].rearrange("p a b -> p (a b)").rearrange("p (m n) -> p m n", m=2)
        oT = ep[:, :, :].rearrange("p a b -> p (a b)").rearrange("p (h n) -> p h n", n=HID)
        wv = acc[:, :, :].rearrange("p a b -> p (a b)").rearrange("p (h l) -> p h l", l=LAT)
        spo_nat = [t[:, :].rearrange("p (q h e) -> p q h e", q=4, h=4) for t in (ctxr, sums)]
        vo_out = [ctxr, sums, pvr, prec]
        natural = [g["cos"], g["sin"]]
        code, absolute, sign = (g[n + "_f"][:, :] for n in ("qm0h", "qm0l", "qm1"))

        init = sem("init")
        x_ready = sem("x_ready")
        x_dve = sem("x_dve")
        x_act = sem("x_act")
        st_ready = sem("st_ready")
        e_ready = sem("e_ready")
        pvm_done = sem("pvm_done")
        pvp_done = sem("pvp_done")
        added = sem("added")
        raw_ready = sem("raw_ready")
        lat_hi = sem("lat_hi")
        cos_done = sem("cos_done")
        turned = [sem(f"turned{i}") for i in range(2)]
        sin_done = sem("sin_done")
        roped = sem("roped")
        rope_hi = sem("rope_hi")
        rope_lo = sem("rope_lo")
        mm_part = sem("mm_part")
        mm_ready = sem("mm_ready")
        pm_part = sem("pm_part")
        pm_ready = sem("pm_ready")
        mrow_in = sem("mrow_in")
        wst_in = [sem(f"wst_in{i}") for i in range(2)]
        stack_in = [sem(f"stack_in{i}") for i in range(2)]
        vp_in = [sem(f"vp_in{i}") for i in range(2)]
        ctx_out = sem("ctx_out")
        rec_part = sem("rec_part")
        ctx_ready = sem("ctx_ready")
        ctx_stored = sem("ctx_stored")
        pat_out = sem("pat_out")
        pat_part = sem("pat_part")
        pat_ready = sem("pat_ready")
        pat_stored = sem("pat_stored")

        ow_in = sem("ow_in")
        spo_in = sem("spo_in")
        vo_stored = sem("vo_stored")
        ffn_in = [sem(f"ffn_in{i}") for i in range(2)]
        transposed = sem("transposed")
        q_own = sem("q_own")
        ctx_back = sem("ctx_back")

        block = ctx.enter_context(nc.Block())

        DIRECT = 2 * NP - 3
        PDIRECT = NP - 2

        def x_bank(v, tile):
            return xb[x_index[(v, *tile)] % 2]

        def x_wait(eng, v, tile):
            eng.wait_ge(x_ready, x_index[(v, *tile)] + 1)

        def x_emptied(eng, v, tile):
            kind = tile[0] in BY_ACT
            n = sum((t[1] in BY_ACT) == kind and i <= x_index[(v, *tile)] for t, i in x_index.items())
            eng.wait_ge(x_act if kind else x_dve, n)

        def adds(it, q, kt, h):
            return 28 * it + 14 * q + 2 * (max(kt, 1) - 1) + h + 1

        NSTACK = 12
        UNIT = [(0, 1), (2, 3), (4,), (5,)]

        def unit_at(v, s):
            return ({3: 0, 5: 1, 7: 2, 9: 3} if v else {5: 0, 6: 1, 8: 2, 10: 3}).get(s) if v < NP else None


        @block.sync
        def _(sp):
            def load_stacks(v):
                quad, half, b = v // 2, v % 2, v % 2
                for w, to, cols in ((0, pq, slice(half * HALF, (half + 1) * HALF)), (1, pk, slice(0, S))):
                    for j in range(2):
                        for slot in range(3):
                            lo = int(slot == (2 if w == 0 else 1))
                            src = d["spqk"][w, lo, 64 * quad:64 * quad + 64, cols].rearrange(
                                "(t j p) n -> j p t n", j=2, p=PD)[j]
                            at = 64 * j + PD * slot
                            sp.dma_start(to[at:at + PD, b, :, :].bitcast(F32), src).then_inc(stack_in[v % 2], 16)

            def load_vp(v):
                src = d["vp"].rearrange("p (t n e) -> p t n e", t=NT, e=PD)[:, :, 4 * (v // 2):4 * (v // 2) + 4, :]
                for t in range(NT):
                    sp.dma_start(vp[:, v % 2, t, :, 0:PD], src[:, t]).then_inc(vp_in[v % 2], 16)

            def load_weights(v):
                sp.dma_start(wst[:, v % 2, :, :].rearrange("p c j -> p (c j)").bitcast(F32), d["wst"][v]).then_inc(wst_in[v % 2], 16)

            def turn(v, u):
                n = 4 * v + u
                sp.wait_ge(raw_ready, 6 * v + UNIT[u][-1] + 1)
                if n >= 2:
                    sp.wait_ge(roped, n - 1)
                for b in range(4):
                    o = b ^ 1
                    sp.dma_start(rot[32 * b:32 * b + 32, n % 2, :], raw[32 * o:32 * o + 32, n % 2, :]).then_inc(turned[n % 2], 16)

            def load_ffn(c):
                src = (a["ffn_up"][c * P:(c + 1) * P, :] if c < 2 else
                       a["ffn_down"].rearrange("(k p) n -> p k n", p=P)[:, 4 * (c - 2):4 * (c - 1), :])
                to = natural[c % 2][:, :]
                if c >= 2:
                    to = to.rearrange("p (k n) -> p k n", n=HID)
                sp.dma_start(to, src).then_inc(ffn_in[c % 2], 16)

            def load_epilogue():
                sp.wait_ge(rope_lo, 8 * NP)
                sp.wait_ge(sin_done, 4 * NP)
                x_emptied(sp, NP - 1, ("P", 5))
                load_ffn(0)
                load_ffn(1)
                for j in range(4):
                    sp.dma_start((rot if j < 2 else rc)[:, j % 2, :], d["vo"][j]).then_inc(ctx_back, 16)
                sp.wait_ge(pat_stored, 16 * PDIRECT)
                for n in range(PDIRECT):
                    sp.dma_start(pattern_tile(g, n), d["pat"][n]).then_inc(ctx_back, 16)
                sp.wait_ge(st_ready, 64 * (NP - 1))
                sp.wait_ge(ctx_stored, 16 * DIRECT)
                for n in range(DIRECT):
                    half = slice(n % 2 * HALF, (n % 2 + 1) * HALF)
                    sp.dma_start(context_tile(g, n // 2)[:, half], d["ctx"][n // 2, :, half]).then_inc(ctx_back, 16)
                for c in (2, 3):
                    sp.wait_ge(transposed, c - 1)
                    load_ffn(c)
                sp.wait_ge(ctx_back, 16 * (4 + PDIRECT + DIRECT))

            load_weights(0)
            for v in slots:
                if v < NP:
                    if v >= 2:
                        sp.wait_ge(st_ready, 64 * (v - 1))
                    if v == 0:
                        sp.wait_ge(init, 6)
                    load_stacks(v)
                    if v == 0:
                        sp.dma_start(o_nat, a["o_w"].rearrange("(m p) n -> p m n", p=P)).then_inc(ow_in, 16)
                        sp.dma_start(wv, a["kv_b_w"].rearrange("(h d) l -> d h l", d=NOPE + DV)[NOPE:NOPE + DV]
                                     ).then_inc(ow_in, 16)
                        for m in range(2):
                            for q in range(4):
                                sp.dma_start(spo_nat[m][:, q, :, 0:PD],
                                             a["sp_o_w"][m * P:(m + 1) * P, 64 * q:64 * q + 64].rearrange(
                                                 "p (h e) -> p h e", e=PD)).then_inc(spo_in, 16)
                    if v + 1 < NP:
                        if v >= 1:
                            x_wait(sp, v - 1, ("P", 5))
                        load_weights(v + 1)
                    turn(v, 0)
                if v == NP:
                    load_epilogue()
                if 2 <= v < NP:
                    sp.wait_ge(ctx_ready, 2 * (v - 2) + 2)
                    sp.dma_start(d["ctx"][v - 2, :, HALF:S], rec[:, :]).then_inc(ctx_stored, 16)
                if v < NP:
                    if v >= 2:
                        sp.wait_ge(pvp_done, NT * (v - 1))
                    load_vp(v)
                    turn(v, 1)
                if 2 <= v < NP:
                    sp.wait_ge(pat_ready, v - 1)
                    sp.dma_start(d["pat"][v - 2], prec[:, :]).then_inc(pat_stored, 16)
                if v < NP:
                    for u in (2, 3):
                        turn(v, u)
                if 1 <= v < NP:
                    sp.wait_ge(ctx_ready, 2 * (v - 1) + 1)
                    sp.dma_start(d["ctx"][v - 1, :, 0:HALF], rec[:, :]).then_inc(ctx_stored, 16)
                if v < NP:
                    x_emptied(sp, v, ("pT", 1))
                    for hh in range(4):
                        at = 64 * (hh % 2) + 3 * PD
                        sp.dma_start(pq[at:at + 1, v % 2, hh // 2, :].bitcast(F32),
                                     mrp[hh:hh + 1, :].bitcast(F32)).then_inc(mrow_in, 16)
                if v == 0:
                    for j in range(4):
                        x_emptied(sp, 0, ("vo", j))
                        sp.dma_start(d["vo"][j], vo_out[j][:, :]).then_inc(vo_stored, 16)

        @block.gpsimd
        def _(pool):
            pool.memset(pq[:, :, :, :].bitcast(F32), 0.0).then_inc(init, 1)
            pool.memset(vp[:, :, :, :, PD:32], 1.0).then_inc(init, 1)
            pool.memset(ones[:, :], 1.0).then_inc(init, 1)
            pool.memset(ctxr[:, :], 0.0).then_inc(init, 1)
            pool.memset(sums[:, :], 0.0).then_inc(init, 1)

            def turn_sin(v, u):
                n = 4 * v + u
                half = slice((u % 2) * HALF, (u % 2 + 1) * HALF)
                pool.wait_ge(turned[n % 2], 64 * (n // 2 + 1))
                pool.tensor_tensor(rot[:, n % 2, :], rot[:, n % 2, :], g["sin"][:, half], ALU.mult).then_inc(sin_done, 1)

            def rope(v, u):
                n = 4 * v + u
                pool.wait_ge(sin_done, n + 1)
                if u < 2:
                    pool.wait_ge(cos_done, 4 * v + 2 * u + 2)
                else:
                    x_emptied(pool, v, ("P", UNIT[u][0]))
                pool.tensor_tensor(rc[:, n % 2, :], rc[:, n % 2, :], rot[:, n % 2, :], ALU.add).then_inc(roped, 1)

            def rope_lo_of(v, u, s):
                n = 4 * v + u
                if v:
                    it, t = (v - 1, s - 1)
                    pool.wait_ge(added, 28 * it + 14 * (t // NT) + 2 * (t % NT))
                half = slice((u % 2) * HALF, (u % 2 + 1) * HALF)
                hi, lo = (qh, ql) if u < 2 else (kh, kl)
                for h in range(2):
                    rows = slice(64 * h, 64 * h + 64)
                    pool.wait_ge(rope_hi, 2 * n + h + 1)
                    pool.tensor_tensor(lo[rows, 2 * (v % 2) + h, half], rc[rows, n % 2, :],
                                       hi[rows, 2 * (v % 2) + h, half].bitcast(F32),
                                       ALU.subtract).then_inc(rope_lo, 1)
                pool.wait_ge(rope_lo, 2 * n + 2)

            def add(it, q, kt):
                for h in range(2):
                    j = 2 * (NT * q + kt) + h
                    pool.wait_ge(e_ready, 64 * it + 4 * (NT * q + kt) + 2 * h + 1)
                    if kt == 1:
                        if q == 1:
                            x_wait(pool, it + 1, ("S", 0))
                        elif it >= 1:
                            x_wait(pool, it + 1, ("S", 1))
                        else:
                            x_wait(pool, 0, ("vo", 3))
                        first = em[:, (j - 2) % 8, :]
                    else:
                        pool.wait_ge(added, adds(it, q, kt - 1, h))
                        first = acc[:, h, :]
                    pool.tensor_tensor(acc[:, h, :], first, em[:, j % 8, :], ALU.add).then_inc(added, 1)

            for v in slots:
                for s in range(NS):
                    if unit_at(v, s - 1) is not None:
                        rope_lo_of(v, unit_at(v, s - 1), s)
                    if unit_at(v, s) is not None:
                        turn_sin(v, unit_at(v, s))
                        rope(v, unit_at(v, s))
                    if 1 <= v <= NP and s % NT:
                        add(v - 1, s // NT, s % NT)

        @block.scalar
        def _(act):
            def produce(v, i):
                tile, n = x_bank(v, ("P", i)), 6 * v + i
                x_wait(act, v, ("P", i))
                u = next(u for u in range(4) if i in UNIT[u])
                un = 4 * v + u
                if i == UNIT[u][0] and un >= 2:
                    act.wait_ge(turned[un % 2], 64 * (un // 2))
                if i < 4:
                    h, half = i % 2, slice((i // 2) * HALF, (i // 2 + 1) * HALF)
                    pe_rows = slice(64 * h, 64 * h + 64)
                    lat_rows = slice(64 - 64 * h, P - 64 * h)
                    act.activation(raw[pe_rows, un % 2, :], tile[pe_rows, :], ACT.Copy).then_inc(raw_ready, 1)
                    act.activation(qh[lat_rows, 2 * (v % 2) + h, half], tile[lat_rows, :],
                                   ACT.Copy).then_inc(lat_hi, 1)
                else:
                    act.activation(raw[:, un % 2, :], tile[:, :], ACT.Copy).then_inc(raw_ready, 1)

            def x_tile(v, tile):
                kind, i = tile
                if kind == "P":
                    produce(v, i)
                if kind not in BY_ACT:
                    return
                x_wait(act, v, tile)
                src = x_bank(v, tile)
                if kind == "mT":
                    at = 32 * ((v - i) % 2)
                    act.activation(mr[at:at + 2, i * HALF:(i + 1) * HALF], src[0:2, :], ACT.Copy).then_inc(x_act, 1)
                elif kind == "pT":
                    if v:
                        act.wait_ge(mrow_in, 64 * v)
                    act.activation(mrp[:, 256 * i:256 * i + 256], src[0:4, 0:256], ACT.Copy).then_inc(x_act, 1)
                elif kind == "oT":
                    to = oT[:, 2 * i:2 * i + 2, :] if i < 8 else g["spoT"][:, 2 * (i - 8):2 * (i - 8) + 2, :]
                    act.activation(to.rearrange("p h n -> p (h n)"), src[:, :], ACT.Copy).then_inc(x_act, 1)
                elif kind == "o":
                    if i == 0:
                        act.wait_ge(pvm_done, 32 * NP)
                        act.wait_ge(added, 28 * NP)
                    act.activation(em[:, i, :], src[:, :], ACT.Copy).then_inc(x_act, 1)
                elif kind == "vo":
                    act.activation(vo_out[i][:, :], src[:, :], ACT.Copy).then_inc(x_act, 1)
                elif kind == "S":
                    n = 2 * (v - 2) + 1 if i else 2 * (v - 1)
                    if n:
                        act.wait_ge(rec_part, 4 * n)
                    act.activation(sums[:, :], src[:, :], ACT.Copy).then_inc(x_act, 1)

            def rope_hi_of(v, u):
                n = 4 * v + u
                half = slice((u % 2) * HALF, (u % 2 + 1) * HALF)
                act.wait_ge(roped, n + 1)
                for h in range(2):
                    rows = slice(64 * h, 64 * h + 64)
                    to = (qh if u < 2 else kh)[rows, 2 * (v % 2) + h, half]
                    act.activation(to, rc[rows, n % 2, :], ACT.Copy).then_inc(rope_hi, 1)

            for v in slots:
                it = v - 1
                for s in range(NS):
                    if s == 1 and v >= 2 or s == 9 and 1 <= v <= NP:
                        n = 2 * (v - 2) + 1 if s == 1 else 2 * it
                        act.wait_ge(pvm_done, 16 * (n + 1))
                        if n:
                            act.wait_ge(ctx_ready, n)
                        else:
                            act.wait_ge(vo_stored, 64)
                        act.activation(ctxr[:, :], pvm[:, :], ACT.Copy).then_inc(ctx_out, 1)
                    if s == 2 and v >= 2:
                        act.wait_ge(pvp_done, NT * (v - 1))
                        if v > 2:
                            act.wait_ge(pat_ready, v - 2)
                        act.activation(pvr[:, :], pvp[:, :], ACT.Copy).then_inc(pat_out, 1)
                    tiles = iter(xs[v][s])
                    if 0 <= it < NP:
                        for x in range(4):
                            n = 64 * it + 4 * s + x
                            j = 32 * it + 2 * s + x // 2
                            act.wait_ge(st_ready, n + 1)
                            if j >= 8:
                                if x % 2 == 0:
                                    act.wait_ge(pvm_done, j - 7)
                                    o = j - 8
                                    act.wait_ge(added, adds(o // 32, o % 32 // 16, o % 16 // 2, o % 2))
                                else:
                                    act.wait_ge(pvp_done, (j - 8) // 4 + 1)
                            if x % 2 == 0:
                                act.activation(em[:, j % 8, :], st[n % 4][:, :], ACT.Exp,
                                               scale=MAIN_SCALE).then_inc(e_ready, 1)
                            else:
                                act.activation(ep[:, j % 8, :], st[n % 4][:, :], ACT.Exp,
                                               scale=PAT_SCALE).then_inc(e_ready, 1)
                            for tile in islice(tiles, 1):
                                x_tile(v, tile)
                    for tile in tiles:
                        x_tile(v, tile)
                    if unit_at(v, s) is not None:
                        rope_hi_of(v, unit_at(v, s))

        @block.vector
        def _(dve):
            dve.memset(pk[:, :, :, :].bitcast(F32), -1.0).then_inc(init, 1)

            def produce(v, i):
                tile, n = x_bank(v, ("P", i)), 6 * v + i
                u = next(u for u in range(4) if i in UNIT[u])
                half = slice((u % 2) * HALF, (u % 2 + 1) * HALF)
                un = 4 * v + u
                if un >= 2:
                    dve.wait_ge(rope_lo, 2 * (un - 1))
                if i < 4:
                    h = i % 2
                    pe_rows = slice(64 * h, 64 * h + 64)
                    lat_rows = slice(64 - 64 * h, P - 64 * h)
                    dve.wait_ge(raw_ready, n + 1)
                    dve.tensor_tensor(rc[pe_rows, un % 2, :], tile[pe_rows, :], g["cos"][pe_rows, half],
                                      ALU.mult).then_inc(cos_done, 1)
                    dve.wait_ge(lat_hi, 4 * v + i + 1)
                    dve.tensor_tensor(ql[lat_rows, 2 * (v % 2) + h, half], tile[lat_rows, :],
                                      qh[lat_rows, 2 * (v % 2) + h, half].bitcast(F32),
                                      ALU.subtract).then_inc(x_dve, 1)
                else:
                    dve.wait_ge(raw_ready, n + 1)
                    dve.tensor_tensor(rc[:, un % 2, :], tile[:, :], g["cos"][:, half], ALU.mult).then_inc(x_dve, 1)

            def x_tile(v, tile):
                kind, i = tile
                if kind == "P":
                    produce(v, i)
                if kind not in ("pm", "mm"):
                    return
                x_wait(dve, v, tile)
                src = x_bank(v, tile)
                if kind == "pm":
                    dve.tensor_reduce(m2p[:, i // 8, i % 4, i // 4 % 2:i // 4 % 2 + 1], src[:, :], AX,
                                      ALU.max).then_inc(x_dve, 1)
                    if i == 31:
                        x_emptied(dve, v, tile)
                        if v:
                            x_wait(dve, v - 1, ("pT", 1))
                        dve.tensor_reduce(msp[:, :, :], m2p[:, :, :, :], AX, ALU.max).then_inc(pm_ready, 1)
                elif kind == "mm":
                    q, h, t, kt = i // 16, i // 8 % 2, i // 2 % 4, i % 2
                    dve.tensor_reduce(m2[:, q, h, t, kt:kt + 1], src[:, :], AX, ALU.max).then_inc(x_dve, 1)
                    if i % 16 == 15:
                        x_emptied(dve, v, tile)
                        dve.tensor_reduce(ms[:, q, :, :].rearrange("p t h -> p h t"), m2[:, q, :, :, :], AX,
                                          ALU.max).then_inc(mm_ready, 1)

            QUARTER = HALF // 4

            def main_reciprocal(v, i, j):
                n = 2 * (v - 2) + 1 if i else 2 * (v - 1)
                cols = slice(j * QUARTER, (j + 1) * QUARTER)
                if j == 0:
                    x_emptied(dve, v, ("S", i))
                    if n:
                        dve.wait_ge(ctx_ready, n)
                        dve.wait_ge(ctx_stored, 16 * min(n, DIRECT))
                    if n == DIRECT:
                        dve.wait_ge(st_ready, 64 * (NP - 1))
                dve.reciprocal(rec[:, cols], sums[:, cols]).then_inc(rec_part, 1)
                if j == 3:
                    dve.wait_ge(rec_part, 4 * (n + 1))
                    dve.wait_ge(ctx_out, n + 1)
                    to = rec[:, :]
                    if n >= DIRECT:
                        to = context_tile(g, n // 2)[:, n % 2 * HALF:(n % 2 + 1) * HALF]
                    dve.tensor_tensor(to, ctxr[:, :], rec[:, :], ALU.mult).then_inc(ctx_ready, 1)

            def pattern_reciprocal(it, j):
                cols = slice(j * QUARTER, (j + 1) * QUARTER)
                if j == 0:
                    dve.wait_ge(pat_out, it + 1)
                    if it:
                        dve.wait_ge(pat_ready, it)
                        dve.wait_ge(pat_stored, 16 * min(it, PDIRECT))
                    else:
                        dve.wait_ge(vo_stored, 64)
                    if it == PDIRECT:
                        for t in turned:
                            dve.wait_ge(t, 128 * NP)
                    dve.stream_shuffle(prec[:, :], pvr[:, :], [i | 16 for i in range(32)]).then_inc(pat_part, 1)
                    dve.wait_ge(pat_part, 5 * it + 1)
                dve.reciprocal(prec[:, cols], prec[:, cols]).then_inc(pat_part, 1)
                if j == 3:
                    dve.wait_ge(pat_part, 5 * it + 5)
                    to = prec[:, :] if it < PDIRECT else pattern_tile(g, it)
                    dve.tensor_tensor(to, pvr[:, :], prec[:, :], ALU.mult).then_inc(pat_ready, 1)

            def between(v, s, j):
                if v >= 2 and s in (2, 3):
                    main_reciprocal(v, 1, 2 * (s - 2) + j)
                if v >= 2 and s in (4, 5):
                    pattern_reciprocal(v - 2, 2 * (s - 4) + j)
                if 1 <= v <= NP and s in (10, 11):
                    main_reciprocal(v, 0, 2 * (s - 10) + j)

            own = [0]

            def link(ins):
                own[0] += 1
                ins.then_inc(q_own, 1)
                dve.wait_ge(q_own, own[0])

            STAGES = 7

            def quantize(c, stage):
                spread = lambda t: t[:, :].unsqueeze(2).broadcast_to((P, 32, 32))
                blocks = lambda t: t.rearrange("p (b j) -> p b j", j=32)

                def reach(mid):
                    link(dve.scalar_tensor_tensor(code, absolute, mid, code, ALU.is_ge, ALU.add))

                if stage == 0:
                    if c == 0:
                        x_wait(dve, NP - 1, ("P", 5))
                    dve.wait_ge(ffn_in[c % 2], 16 * (c // 2 + 1))
                    link(dve.transpose(sign, natural[c % 2][:, :]))
                    dve.engine_nop().then_inc(transposed, 1)
                    link(dve.tensor_reduce(amax[:, :], blocks(sign), AX, ALU.max, apply_absolute_value=True))
                    link(dve.tensor_scalar(amax[:, :], amax[:, :], 1e-30, None, ALU.max))
                elif stage == 1:
                    link(dve.tensor_scalar(amax[:, :].bitcast(I32), amax[:, :].bitcast(I32), 0x7F800000, None,
                                           ALU.bitwise_and))
                    link(dve.reciprocal(inv[:, :], amax[:, :]))
                    link(dve.tensor_scalar(absolute.bitcast(I32), sign.bitcast(I32), 0x7FFFFFFF, None, ALU.bitwise_and))
                elif stage == 2:
                    link(dve.scalar_tensor_tensor(blocks(absolute), blocks(absolute), 4.0, spread(inv), ALU.mult,
                                                  ALU.mult))
                    link(dve.tensor_scalar(code, absolute, 5.0, 2.0, ALU.is_ge, ALU.mult))
                    reach(3.5)
                elif stage == 3:
                    reach(2.5)
                    link(dve.tensor_scalar(code, code, 2.0, None, ALU.mult))
                    reach(1.75)
                elif stage == 4:
                    for mid in (1.25, 0.75, 0.25):
                        reach(mid)
                elif stage == 5:
                    link(dve.tensor_scalar(sign.bitcast(I32), sign.bitcast(I32), -2147483648, None, ALU.bitwise_and))
                    link(dve.tensor_tensor(code.bitcast(I32), code.bitcast(I32), sign.bitcast(I32), ALU.bitwise_or))
                    link(dve.scalar_tensor_tensor(blocks(code), blocks(code), 0.125, spread(amax), ALU.mult, ALU.mult))
                elif stage == 6:
                    to = g["xh"][:, c, :] if c < 2 else g["xl"][:, c - 2, :]
                    link(dve.transpose(absolute, code))
                    link(dve.tensor_copy(to, absolute))

            for v in slots:
                for s in range(NS):
                    tiles = iter(xs[v][s])
                    for j in range(2):
                        for tile in islice(tiles, 2):
                            x_tile(v, tile)
                        between(v, s, j)
                        if v == NP and s >= 4:
                            quantize(*divmod(2 * s + j - 4, STAGES))
                    for tile in tiles:
                        x_tile(v, tile)
                    if v == NP and s < 4:
                        quantize(*divmod(s, STAGES))

        @block.tensor
        def _(pe):

            def passes(out, pairs, sem_):
                for n, (w, x) in enumerate(pairs):
                    mm = pe.matmul(out, w, x, start=(n == 0), stop=(n == len(pairs) - 1))
                mm.then_inc(sem_, 1)

            def main_scores(it, s, h):
                n = 64 * it + 4 * s + 2 * h
                q, kt, b = s // NT, s % NT, 2 * (it % 2) + h
                if n >= 4:
                    pe.wait_ge(e_ready, n - 3)
                keys, queries = slice(kt * P, (kt + 1) * P), slice(q * HALF, (q + 1) * HALF)
                at = 32 * (it % 2)
                passes(st[n % 4][:, :], [
                    (kh[:, b, keys], qh[:, b, queries]), (kh[:, b, keys], ql[:, b, queries]),
                    (kl[:, b, keys], qh[:, b, queries]), (sel[at:at + 2, h * P:(h + 1) * P], mr[at:at + 2, queries]),
                ], st_ready)

            def pattern_scores(it, s, x):
                n = 64 * it + 4 * s + 2 * x + 1
                if n >= 4:
                    pe.wait_ge(e_ready, n - 3)
                hh, kt = 2 * (s % 2) + x, s // 2
                rows = slice(64 * x, 64 * x + 3 * PD + 1)
                passes(st[n % 4][:, :], [(pk[rows, it % 2, hh // 2, kt * P:(kt + 1) * P],
                                          pq[rows, it % 2, hh // 2, :])], st_ready)

            def main_values(it, s):
                q, kt = s // NT, s % NT
                if kt == 0 and (it or q):
                    pe.wait_ge(ctx_out, 2 * it + q)
                for h in range(2):
                    pe.wait_ge(e_ready, 64 * it + 4 * s + 2 * h + 1)
                    pe.matmul(pvm[64 * h:64 * h + 64, :], cdup[:, kt, 0:LAT], em[:, (2 * s + h) % 8, :],
                              start=(kt == 0), stop=(kt == NT - 1)).then_inc(pvm_done, 1)

            def pattern_values(it, kt):
                if kt == 0:
                    pe.wait_ge(vp_in[it % 2], 16 * NT * (it // 2 + 1))
                    if it:
                        pe.wait_ge(pat_out, it)
                pe.wait_ge(e_ready, 64 * it + 4 * (2 * kt + 1) + 4)
                for hh in range(4):
                    mm = pe.matmul(pvp[32 * hh:32 * hh + 32, :], vp[:, it % 2, kt, hh, :], ep[:, (4 * kt + hh) % 8, :],
                                   start=(kt == 0), stop=(kt == NT - 1))
                mm.then_inc(pvp_done, 1)

            def x_tile(v, tile):
                kind, i = tile
                n = x_index[(v, *tile)]
                out, b = xb[n % 2], v % 2
                if n >= 2:
                    x_emptied(pe, *x_tiles[n - 2])
                if kind == "P":
                    if i == 0:
                        pe.wait_ge(wst_in[v % 2], 16 * (v // 2 + 1))
                    w = [wst[:, b, c, :] for c in range(NW)]
                    if i < 4:
                        half = slice((i // 2) * HALF, (i // 2 + 1) * HALF)
                        o = 4 * (i % 2)
                        qm0h, qm0l, qm1 = g["qm0h"][:, half], g["qm0l"][:, half], g["qm1"]
                        passes(out[:, :], [(w[o], qm0h), (w[o + 1], qm0h), (w[o], qm0l), (w[o + 2], qm1[:, half]),
                                           (w[o + 3][0:64, :], qm1[0:64, half])], x_ready)
                    else:
                        half = slice((i - 4) * HALF, (i - 3) * HALF)
                        pairs = []
                        for k in range(NK):
                            xh, xl = g["xh"][:, k, half], g["xl"][:, k, half]
                            pairs += [(w[8 + 2 * k], xh), (w[9 + 2 * k], xh), (w[8 + 2 * k], xl)]
                        passes(out[:, :], pairs, x_ready)
                elif kind == "pm":
                    if i == 0:
                        if v == 0:
                            pe.wait_ge(init, 6)
                        pe.wait_ge(stack_in[v % 2], 16 * NSTACK * (v // 2 + 1))
                    hh, kt, t = i % 4, i // 4 % 2, i // 8
                    rows = slice(64 * (hh % 2), 64 * (hh % 2) + 3 * PD)
                    passes(out[:, :], [(pq[rows, b, hh // 2, t * P:(t + 1) * P],
                                        pk[rows, b, hh // 2, kt * HALF:(kt + 1) * HALF])], x_ready)
                elif kind == "mm":
                    if i == 0:
                        pe.wait_ge(rope_hi, 8 * (v + 1))
                    q, h, t, kt = i // 16, i // 8 % 2, i // 2 % 4, i % 2
                    at = (4 * q + t) * P
                    b = (v - (i >= MM_LATE)) % 2
                    passes(out[:, :], [(qh[:, 2 * b + h, at:at + P],
                                        kh[:, 2 * b + h, kt * HALF:(kt + 1) * HALF])], x_ready)
                elif kind == "oT":
                    pe.wait_ge(ow_in, 32)
                    pe.wait_ge(spo_in, 128)
                    for j in range(4):
                        r, m = 2 * i + j // 2, j % 2
                        if i < 8:
                            src = o_nat[:, m, r * DV:(r + 1) * DV]
                        else:
                            src = spo_nat[m][:, r - 16, :, :].rearrange("p h e -> p (h e)")
                        mm = pe.transpose(out[:, j * P:(j + 1) * P], src, ident[:, :])
                    mm.then_inc(x_ready, 1)
                elif kind == "o":
                    if i == 0:
                        pe.wait_ge(ctx_back, 16 * (4 + PDIRECT + DIRECT))
                        pe.wait_ge(ctx_ready, 2 * NP - 1)
                        pe.wait_ge(pat_ready, NP - 1)
                    output_projection(pe, g, out, i).then_inc(x_ready, 1)
                elif kind == "vo":
                    x_emptied(pe, 0, ("oT", 9))
                    for j in range(2):
                        for h in range(2):
                            hd = 2 * (2 * i + j) + h
                            mm = pe.matmul(out[64 * h:64 * h + 64, j * HID:(j + 1) * HID], wv[:, hd, :], oT[:, hd, :],
                                           start=True, stop=True)
                    mm.then_inc(x_ready, 1)
                elif kind == "mT":
                    pair = v - 1 if i else v
                    pe.wait_ge(mm_ready, 2 * pair + i + 1)
                    for t in range(4):
                        mm = pe.matmul(out[0:2, t * P:(t + 1) * P], ms[:, i, t, :], ident[:, :], start=True, stop=True)
                    mm.then_inc(x_ready, 1)
                elif kind == "pT":
                    pe.wait_ge(pm_ready, v + 1)
                    for t in range(2):
                        mm = pe.matmul(out[0:4, t * P:(t + 1) * P], msp[:, 2 * i + t, :], ident[:, :],
                                       start=True, stop=True)
                    mm.then_inc(x_ready, 1)
                elif kind == "S":
                    it = v - 2 if i else v - 1
                    for h in range(2):
                        pe.wait_ge(added, adds(it, i, NT - 1, h))
                        mm = pe.matmul(out[64 * h:64 * h + 64, :], ones[:, :], acc[:, h, :], start=True, stop=True)
                    mm.then_inc(x_ready, 1)

            for v in slots:
                it = v - 1
                for s in range(NS):
                    tiles = iter(xs[v][s])
                    if 0 <= it < NP:
                        if s == 0:
                            pe.wait_ge(rope_lo, 8 * (it + 1))
                            x_emptied(pe, it, ("mT", 0))
                            pe.wait_ge(mrow_in, 64 * (it + 1))
                        if s == NT:
                            x_emptied(pe, v, ("mT", 1))
                        for x in range(2):
                            for scores in (main_scores, pattern_scores):
                                scores(it, s, x)
                                for tile in islice(tiles, 1):
                                    x_tile(v, tile)
                        if s:
                            main_values(it, s - 1)
                        if s >= 3 and s % 2:
                            pattern_values(it, (s - 3) // 2)
                    if v >= 2:
                        if s == 0:
                            main_values(v - 2, NS - 1)
                        if s == 1:
                            pattern_values(v - 2, NT - 1)
                    for tile in tiles:
                        x_tile(v, tile)



def context_tile(g, pair):
    if pair >= 6:
        return g["ql_f"][:, pair % 2, :]
    return g[("kh", "kl", "qh")[pair // 2]][:, pair % 2, :].bitcast(F32)


def pattern_tile(g, n):
    if n < NP - 2:
        return g["wst"][:, n // 3, 4 * (n % 3):4 * (n % 3) + 4, :].rearrange("p c j -> p (c j)").bitcast(F32)
    return g["raw"][:, n - (NP - 2), :]


def output_projection(pe, g, out, t):
    half, tq = divmod(t, 4)
    for j in range(NP):
        vo = g["rot" if j < 4 else "rc"][:, j // 2 % 2, j % 2 * HID:(j % 2 + 1) * HID]
        pe.matmul(out[:, 0:HID], context_tile(g, j)[:, t * P:(t + 1) * P], vo, start=(j == 0), stop=(j == NP - 1))
    for j in range(4):
        mm = pe.matmul(out[:, HID:2 * HID], pattern_tile(g, 2 * j + half)[:, tq * P:(tq + 1) * P],
                       g["spoT"][:, j, :], start=(j == 0), stop=(j == 3))
    return mm


def epilogue(nc, a, d, g, out):
    order = [(0, 0), (1, 0), (0, 1), (1, 1), (2, 0), (2, 1)]
    jobs = [("o", t) for t in range(4, NT)]
    jobs += [("xT", k, 0) for k in range(NK)]
    jobs += [("up", 0, m) for m in range(8)] + [("down", 0, m) for m in range(2)]
    jobs += [("xT", k, 1) for k in range(NK)] + [("yT", j) for j in range(2)]
    jobs += [("up", 1, m) for m in range(8)] + [("down", 1, m) for m in range(2)]
    jobs += [("yT", 2 + j) for j in range(2)]
    index = {j: n for n, j in enumerate(jobs)}
    by_act = [j[0] in ("up", "down") for j in jobs]

    with ExitStack() as ctx:
        def sb(name, shape, dt=F32):
            return ctx.enter_context(nc.sbuf_tensor(name, shape, dt))

        def sem(name):
            return ctx.enter_context(nc.semaphore(name))

        bank = [ctx.enter_context(nc.psum_tensor(f"c_bank{i}", [P, HALF], F32)) for i in range(8)]
        wup, wdn = g["xh"], g["xl"][:, :, :].rearrange("p a b -> p (a b)").rearrange("p (k n) -> p k n", n=HID)
        hhi = [g[t][:, 2 + i, h * HALF:(h + 1) * HALF] for t in ("kh", "kl") for i in range(2) for h in range(2)]
        hlo = [g[t][:, 2 + i, h * HALF:(h + 1) * HALF] for t in ("qh", "ql") for i in range(2) for h in range(2)]
        res = sb("res", [P, NT, HID])
        x2h = sb("x2h", [P, NK, S], F32R)
        x2l = sb("x2l", [P, NK, S], F32R)
        hf = sb("hf", [P, 2, HALF])
        yT = sb("yT", [P, 2, HALF])
        ya = sb("ya", [P, 4, HID])
        yf = sb("yf", [P, 4, HID])
        x2 = sb("x2", [P, NT, HID])
        ub = sb("ub", [P, 8])
        db = sb("db", [P, 2])
        stats = sb("c_stats", [P, NT, 6])
        mv = sb("c_mv", [P, 3, NT, 2])
        rstd = sb("c_rstd", [P, 3, NT])
        ident, gates, stash = g["ident"], g["gates"], g["em"]

        res_in = sem("res_in")
        bias_in = sem("bias_in")
        pe_job = sem("c_pe_job")
        ev_act = sem("c_ev_act")
        ev_dve = sem("c_ev_dve")
        own = sem("c_own")
        var_ready = sem("var_ready")
        rstd_ready = sem("c_rstd_ready")
        x2_ready = sem("x2_ready")
        pool_own = sem("c_pool_own")
        x2_hi = sem("x2_hi")
        h_hi = sem("h_hi")
        h_full = sem("h_full")
        h_lo = sem("h_lo")
        y_ready = sem("y_ready")
        stored = sem("stored")

        def evacuated(eng, n):
            for s, flag in ((ev_act, True), (ev_dve, False)):
                count = sum(b == flag for b in by_act[:n + 1])
                if count:
                    eng.wait_ge(s, count)

        block = ctx.enter_context(nc.Block())

        @block.sync
        def _(sp):
            sp.dma_start(res[:, :, :], a["x"].rearrange("b (t p) n -> p (b t) n", p=P)).then_inc(res_in, 16)
            sp.dma_start(ub[:, :], a["up_bias"]).then_inc(bias_in, 16)
            sp.dma_start(db[:, :], a["down_bias"]).then_inc(bias_in, 16)
            o = out.rearrange("b (t p) n -> p (b t) n", p=P)
            for t in range(NT):
                sp.wait_ge(y_ready, t + 1)
                sp.dma_start(o[:, t, :], x2[:, t, :]).then_inc(stored, 16)
            sp.wait_ge(stored, 16 * NT)

        @block.gpsimd
        def _(pool):
            for n, (kind, q) in enumerate(order):
                four = rstd[:, kind, 4 * q:4 * q + 4]
                pool.wait_ge(var_ready, n + 1)
                pool.tensor_scalar(four, mv[:, kind, 4 * q:4 * q + 4, 1], 1e-5, None, ALU.add).then_inc(pool_own, 1)
                pool.wait_ge(pool_own, n + 1)
                pool.tensor_tensor(four, four, g["mhalf"][:, 0:4], ALU.pow).then_inc(rstd_ready, 1)

        @block.tensor
        def _(pe):
            def transposes(n, blocks):
                for j, src in enumerate(blocks):
                    mm = pe.transpose(bank[n % 8][:, j * P:(j + 1) * P], src, ident[:, :])
                mm.then_inc(pe_job, 1)

            for n, job in enumerate(jobs):
                kind, o = job[0], bank[n % 8]
                if n >= 8:
                    evacuated(pe, n - 8)
                if kind == "o":
                    output_projection(pe, g, o, job[1]).then_inc(pe_job, 1)
                elif kind == "xT":
                    k, q = job[1:]
                    pe.wait_ge(x2_ready, q + 1)
                    transposes(n, [x2[:, 4 * q + j, k * P:(k + 1) * P] for j in range(4)])
                elif kind == "up":
                    q, m = job[1:]
                    half = slice(q * HALF, (q + 1) * HALF)
                    evacuated(pe, index[("xT", 1, q)])
                    for i, (k, x) in enumerate([(k, x) for k in range(NK) for x in (x2h, x2l)]):
                        mm = pe.matmul(o[:, :], wup[:, k, m * P:(m + 1) * P], x[:, k, half], start=(i == 0), stop=(i == 3))
                    mm.then_inc(pe_job, 1)
                elif kind == "down":
                    q, m = job[1:]
                    for k in range(8):
                        if m == 0:
                            pe.wait_ge(h_lo, 8 * q + k + 1)
                        pe.matmul(o[:, :], wdn[:, k, m * P:(m + 1) * P], hhi[k], start=(k == 0), stop=False)
                        mm = pe.matmul(o[:, :], wdn[:, k, m * P:(m + 1) * P], hlo[k], start=False, stop=(k == 7))
                    mm.then_inc(pe_job, 1)
                elif kind == "yT":
                    q, j = divmod(job[1], 2)
                    pe.wait_ge(ev_act, sum(by_act[:index[("down", q, 1)] + 1]))
                    transposes(n, [yT[:, m, (2 * j + t) * P:(2 * j + t + 1) * P] for t in range(2) for m in range(2)])

        @block.scalar
        def _(act):
            ups = 0
            act.wait_ge(bias_in, 32)
            for n, job in enumerate(jobs):
                kind, o = job[0], bank[n % 8]
                if kind in ("o", "yT"):
                    continue
                act.wait_ge(pe_job, n + 1)
                if kind == "xT":
                    k, q = job[1:]
                    act.activation(x2h[:, k, q * HALF:(q + 1) * HALF], o[:, :], ACT.Copy).then_inc(x2_hi, 1)
                elif kind == "up":
                    q, m = job[1:]
                    if q:
                        act.wait_ge(pe_job, index[("down", 0, 1)] + 1)
                    if ups >= 2:
                        act.wait_ge(h_lo, ups - 1)
                    act.activation(hf[:, m % 2, :], o[:, :], ACT.Gelu_apprx_tanh, bias=ub[:, m:m + 1]).then_inc(h_full, 1)
                    act.activation(hhi[m], o[:, :], ACT.Gelu_apprx_tanh, bias=ub[:, m:m + 1]).then_inc(ev_act, 1)
                    ups += 1
                elif kind == "down":
                    q, m = job[1:]
                    if q:
                        act.wait_ge(pe_job, index[("yT", 1)] + 1)
                    act.activation(yT[:, m, :], o[:, :], ACT.Identity, bias=db[:, m:m + 1]).then_inc(ev_act, 1)

        @block.vector
        def _(dve):
            count = [0]

            def link(ins):
                count[0] += 1
                ins.then_inc(own, 1)
                dve.wait_ge(own, count[0])

            def statistics(kind, q, srcs):
                for t in range(4):
                    ins = dve.bn_stats(stats[:, 4 * q + t, :], srcs[t])
                link(ins)
                for t in range(4):
                    ins = dve.bn_aggr(mv[:, kind, 4 * q + t, :], stats[:, 4 * q + t, :])
                ins.then_inc(var_ready, 1)

            def normalise(kind, q, dsts, srcs):
                dve.wait_ge(rstd_ready, order.index((kind, q)) + 1)
                for t in range(4):
                    ins = dve.tensor_scalar(dsts[t], srcs[t], mv[:, kind, 4 * q + t, 0:1],
                                            rstd[:, kind, 4 * q + t:4 * q + t + 1], ALU.subtract, ALU.mult)
                return ins

            def tiles(t, q):
                return [t[:, 4 * q + i, :] for i in range(4)]

            def mix(q):
                for stage in range(2):
                    for t in range(4 * q, 4 * q + 4):
                        if q and stage == 0:
                            dve.wait_ge(pe_job, index[("o", t)] + 1)
                        o = bank[index[("o", t)] % 8] if q else stash[:, t, :]
                        if stage == 0:
                            ins = dve.tensor_scalar(ya[:, t % 4, :], o[:, HID:2 * HID], gates[:, t, 1:2], None, ALU.mult)
                            continue
                        ins = dve.scalar_tensor_tensor(ya[:, t % 4, :], o[:, 0:HID], gates[:, t, 0:1], ya[:, t % 4, :],
                                                       ALU.mult, ALU.add)
                        if q:
                            ins.then_inc(ev_dve, 1)
                    if stage == 0:
                        link(ins)
                if q:
                    dve.wait_ge(ev_dve, 4)
                else:
                    link(dve.engine_nop())

            def attention_norm(q, stage):
                if stage == 0:
                    statistics(0, q, tiles(ya, 0))
                elif stage == 1:
                    link(normalise(0, q, tiles(ya, 0), tiles(ya, 0)))
                elif stage == 2:
                    if q == 0:
                        dve.wait_ge(res_in, 16)
                    r = res[:, 4 * q:4 * q + 4, :]
                    link(dve.tensor_tensor(r, r, ya[:, :, :], ALU.add))
                elif stage == 3:
                    statistics(1, q, tiles(res, q))
                elif stage == 4:
                    normalise(1, q, tiles(x2, q), tiles(res, q)).then_inc(x2_ready, 1)

            def final_norm(q, stage):
                banks = [bank[index[("yT", 2 * q + j)] % 8] for j in range(2)]
                srcs = [banks[t // 2][:, t % 2 * HID:(t % 2 + 1) * HID] for t in range(4)]
                if stage == 0:
                    dve.wait_ge(pe_job, index[("yT", 2 * q + 1)] + 1)
                    statistics(2, q, srcs)
                elif stage == 1:
                    normalise(2, q, tiles(yf, 0), srcs).then_inc(ev_dve, 1)
                    evacuated(dve, index[("yT", 2 * q)])
                    dve.engine_nop().then_inc(ev_dve, 1)
                elif stage == 2:
                    for t in range(4):
                        dve.tensor_tensor(x2[:, 4 * q + t, :], res[:, 4 * q + t, :], yf[:, t, :],
                                          ALU.add).then_inc(y_ready, 1)

            def lo_of_input(q):
                for k in range(NK):
                    n = index[("xT", k, q)]
                    half = slice(q * HALF, (q + 1) * HALF)
                    dve.wait_ge(x2_hi, 2 * q + k + 1)
                    dve.tensor_tensor(x2l[:, k, half], bank[n % 8][:, :], x2h[:, k, half].bitcast(F32),
                                      ALU.subtract).then_inc(ev_dve, 1)

            def lo_of_gelu(q, m):
                dve.wait_ge(h_full, 8 * q + m + 1)
                dve.wait_ge(ev_act, sum(by_act[:index[("up", q, m)] + 1]))
                dve.tensor_tensor(hlo[m], hf[:, m % 2, :], hhi[m].bitcast(F32), ALU.subtract).then_inc(h_lo, 1)

            mix(0)
            for stage in range(5):
                attention_norm(0, stage)
            mix(1)
            lo_of_input(0)
            for m in range(8):
                lo_of_gelu(0, m)
                if 1 <= m <= 5:
                    attention_norm(1, m - 1)
            lo_of_input(1)
            for m in range(8):
                lo_of_gelu(1, m)
                if 1 <= m <= 3:
                    final_norm(0, m - 1)
            for stage in range(3):
                final_norm(1, stage)


NAMES = {
    "x": "L0_attn_hidden_states", "q_a_w": "L0_attn_q_a_w", "q_a_ln_w": "L0_attn_q_a_ln_w",
    "q_b_w": "L0_attn_q_b_w", "kv_a_w": "L0_attn_kv_a_w", "kv_a_ln_w": "L0_attn_kv_a_ln_w",
    "kv_b_w": "L0_attn_kv_b_w", "o_w": "L0_attn_o_w", "sp_q_w": "L0_attn_sp_q_w",
    "sp_k_w": "L0_attn_sp_k_w", "sp_v_w": "L0_attn_sp_v_w", "sp_o_w": "L0_attn_sp_o_w",
    "gate_w": "L0_attn_gate_w", "gate_b": "L0_attn_gate_b", "ffn_up": "L0_ffn_up_kernel",
    "up_bias": "L0_ffn_up_bias", "ffn_down": "L0_ffn_down_kernel", "down_bias": "L0_ffn_down_bias",
}


def build(nc, a, out):
    def scratch(name, shape, dt=F32):
        return nc.dram_tensor(name, shape, dt, kind="Internal").ap()

    d = {
        "wst": scratch("wst_d", (NP, P, NW * P)),
        "spqk": scratch("spqk_d", (2, 2, HID, S)),
        "vp": scratch("vp_d", (P, NT * HID)),
        "ctx": scratch("ctx_d", (NP, P, S)),
        "pat": scratch("pat_d", (NP, P, HALF)),
        "vo": scratch("vo_d", (4, P, HALF)),
    }
    with ExitStack() as ctx:
        def sb(name, shape, dt=F32):
            return ctx.enter_context(nc.sbuf_tensor(name, shape, dt))

        g = {"ident": sb("ident", [P, P]), "gates": sb("gates", [P, NT, 2]), "mhalf": sb("mhalf", [P, 2 * NT])}
        with ExitStack() as inner:
            def sbi(name, shape, dt=F32):
                return inner.enter_context(nc.sbuf_tensor(name, shape, dt))

            def two_types(shapes):
                with ExitStack() as before:
                    plain = {n + "_f": before.enter_context(nc.sbuf_tensor(n + "_f", shape, F32))
                             for n, shape in shapes.items()}
                return plain | {n: sbi(n, shape, F32R) for n, shape in shapes.items()}

            g |= two_types({"qm0h": [P, S], "qm0l": [P, S], "qm1": [P, S]})
            g |= {
                "sel_f": sbi("sel_f", [64, 256]), "sel": sbi("sel", [64, 256], F32R),
                "cos": sbi("cos", [P, S]), "sin": sbi("sin", [P, S]),
                "cdup": sbi("cdup", [P, NT, P]),
                "xh": sbi("xh", [P, NK, S], F32R), "xl": sbi("xl", [P, NK, S], F32R),
                "kh": sbi("kh", [P, 4, S], F32R), "kl": sbi("kl", [P, 4, S], F32R),
            }
            prologue(nc, a, d, g)
            g |= two_types({"ql": [P, 4, S]})
            g |= {
                "qh": sbi("qh", [P, 4, S], F32R), "wst": sbi("wst", [P, 2, NW, P], F32R),
                "raw": sbi("raw", [P, 2, HALF]), "rot": sbi("rot", [P, 2, HALF]), "rc": sbi("rc", [P, 2, HALF]),
                "em": sbi("em", [P, 8, HALF]), "spoT": sbi("spoT", [P, 4, HID]),
            }
            attention(nc, a, d, g)
            epilogue(nc, a, d, g, out)



def constants():
    consts = np.zeros((P, P + 256), np.float32)
    consts[:, 0:P] = np.eye(P, dtype=np.float32)
    for b in (0, 32):
        for h in range(2):
            consts[b + h, P + h * P:P + (h + 1) * P] = -1.0
    f32 = np.float32
    inv_freq = f32(1.0) / np.power(f32(10000.0), np.arange(0, ROPE, 2, dtype=f32) / f32(ROPE))
    angle = np.outer(inv_freq, np.arange(S, dtype=f32)).astype(f32)
    c, s = np.cos(angle), np.sin(angle)
    rope = np.stack([np.concatenate([c] * 4), np.concatenate([-s, s] * 2)]).astype(f32)
    return consts, rope


def kernel(**inputs):
    import concourse.bacc as bacc
    from concourse.bass_utils import run_bass_kernel_spmd

    nc = bacc.Bacc("TRN2", target_bir_lowering=False, num_devices=1, dynamic_dma_scratch_size=1024)
    arrays, aps = {}, {}
    for short, name in NAMES.items():
        v = np.ascontiguousarray(inputs[name])
        if short in ("up_bias", "down_bias"):
            v = np.ascontiguousarray(v.reshape(-1, P).T)
        arrays[f"in_{short}"] = v
    arrays["in_consts"], arrays["in_rope"] = constants()
    for key, v in arrays.items():
        aps[key[3:]] = nc.dram_tensor(key, v.shape, F32, kind="ExternalInput").ap()
    out = nc.dram_tensor("out_0", (1, S, HID), F32, kind="ExternalOutput").ap()
    build(nc, aps, out)
    r = run_bass_kernel_spmd(nc, [arrays], core_ids=[0])
    return r.results[0]["out_0"]
```

```python
from contextlib import ExitStack
from itertools import islice

import numpy as np

import concourse.bass as bass
from concourse import mybir

F32 = mybir.dt.float32
F32R = mybir.dt.float32r
I32 = mybir.dt.int32
ALU = mybir.AluOpType
ACT = mybir.ActivationFunctionType
AX = mybir.AxisListType.X

P = 128
S, HID = 1024, 256
H, NOPE, ROPE, DV = 16, 128, 64, 128
DQ = NOPE + ROPE
QR, LAT = 192, 64
PH, PD = 16, 16
F = 1024
NT = S // P
NK = HID // P
NP = H // 2
HALF = 512
W1 = QR + LAT + 2
MAIN_SCALE = float(DQ) ** -0.5
PAT_SCALE = float(PD) ** -0.5
NW = 12



def prologue(nc, a, d, g):
    jobs = [("xT", k, q) for k in range(NK) for q in range(2)]
    jobs += [("w1T", k) for k in range(NK)]
    jobs += [("kpT", k, q) for k in range(NK) for q in range(2)]
    jobs += [("proj1", t) for t in range(NT)]
    jobs += [("pe0T", q) for q in range(2)] + [("lat0", q) for q in range(2)]
    jobs += [("pe1T", q) for q in range(2)] + [("lat1", q) for q in range(2)]
    jobs += [("spT", w) for w in range(3)]
    jobs += [("spqk", w, m, h) for w in range(2) for m in range(2) for h in range(2)]
    jobs += [("spv", q) for q in range(NT // 2)]
    jobs += [("cT", q) for q in range(2)]
    jobs += [("qm0T", q) for q in range(2)] + [("qm1T", q) for q in range(2)]
    split = ("spqk", "qm0T", "qm1T")
    by_act = [j[0] not in split and j[0] != "cT" and n % 2 == 0 for n, j in enumerate(jobs)]
    index = {j: n for n, j in enumerate(jobs)}

    first_spqk = index[("spqk", 0, 0, 0)]

    def last(kind):
        return max(n for n, j in enumerate(jobs) if j[0] == kind)

    with ExitStack() as ctx:
        def sb(name, shape, dt=F32):
            return ctx.enter_context(nc.sbuf_tensor(name, shape, dt))

        def sem(name):
            return ctx.enter_context(nc.semaphore(name))

        bank = [ctx.enter_context(nc.psum_tensor(f"a_bank{i}", [P, HALF], F32)) for i in range(8)]
        NSP = 4
        xn = sb("xn", [P, NT, HID])
        xT = sb("xT", [P, NK, S])
        qa_nat = sb("qa_nat", [96, 2, HID])
        lora_nat = sb("lora_nat", [LAT, HID])
        gate_nat = sb("gate_nat", [2, HID])
        sp_nat = sb("sp_nat", [P, 3, 2, HID])
        kpe_nat = sb("kpe_nat", [P, NP, HID])
        wqn = sb("wqn", [P, H, QR])
        wpe = sb("wpe", [P, NP, 256])
        wk = sb("wk", [P, H, LAT])
        w1T = sb("w1T", [P, NK, W1])
        spT = sb("spT", [P, 3, NK, HID])
        kpT = sb("kpT", [P, NK, S])
        aq = [sb("aq0", [P, NP, 256]), sb("aq1", [P, NP, 256])]
        split_hi = sb("split_hi", [P, 2, S], F32R)
        split_lo = sb("split_lo", [P, 2, S], F32R)
        m1 = sb("m1", [P, NT, W1])
        cT = sb("cT", [P, S])
        sp_hi = sb("sp_hi", [P, NSP, HALF], F32R)
        sp_lo = sb("sp_lo", [P, NSP, HALF], F32R)
        vf = sb("vf", [P, NT, HID])
        lnq = sb("lnq", [P, QR])
        lnkv = sb("lnkv", [P, LAT])
        gate_b = sb("gate_b", [P, 2])
        stats = sb("stats", [P, NT, 6])
        mv = sb("mv", [P, NT, 2])
        rstd = sb("rstd", [P, NT])
        junk = sb("junk", [P, QR])
        ssq = sb("ssq", [P, 2, NT])
        rms = sb("rms", [P, 2, NT])
        gl = sb("gl", [P, NT, 2])
        gmax = sb("gmax", [P, NT])
        gsum = sb("gsum", [P, NT])
        ident, cdup, gates = g["ident"], g["cdup"], g["gates"]

        s_x = [sem(f"x_in{i}") for i in range(2)]
        s_ident, s_const, s_w1, s_sp, s_kpe, s_wq, s_ln = (
            sem(n) for n in ("ident_in", "const_in", "w1_in", "sp_in", "kpe_in", "wq_in", "ln_in"))
        stat = sem("stat")
        rstd_ready = sem("rstd_ready")
        xn_ready = sem("xn_ready")
        pe_job = sem("pe_job")
        ev_act = sem("ev_act")
        ev_dve = sem("ev_dve")
        kh_ready = sem("kh_ready")
        hi_ready = sem("hi_ready")
        ssq_ready = sem("ssq_ready")
        rms_ready = sem("rms_ready")
        norm_ready = sem("norm_ready")
        wsplit_hi = sem("wsplit_hi")
        wsplit_lo = sem("wsplit_lo")
        wstored = [sem(f"wstored{i}") for i in range(2)]
        spstored = [sem(f"spstored{i}") for i in range(NSP)]
        vstored = sem("vstored")
        dve_own = sem("dve_own")
        pool_own = sem("pool_own")
        logits = sem("logits")
        gexp = sem("gexp")

        def evacuated(eng, n):
            for s, flag in ((ev_act, True), (ev_dve, False)):
                count = sum(b == flag for b in by_act[:n + 1])
                if count:
                    eng.wait_ge(s, count)

        block = ctx.enter_context(nc.Block())

        chunk_after = [last("kpT") + 1, last("kpT") + 2, last("lat0") + 1, last("lat0") + 2,
                       last("lat1") + 1, last("lat1") + 2]

        @block.sync
        def _(sp):
            x = a["x"].rearrange("b (t p) n -> p (b t) n", p=P)
            sp.dma_start(xn[:, 0:4, :], x[:, 0:4, :]).then_inc(s_x[0], 16)
            sp.dma_start(xn[:, 4:8, :], x[:, 4:8, :]).then_inc(s_x[1], 16)
            sp.dma_start(ident[:, :], a["consts"][:, 0:P]).then_inc(s_ident, 16)
            sp.dma_start(qa_nat[:, :, :], a["q_a_w"].rearrange("(m p) n -> p m n", p=96)).then_inc(s_w1, 16)
            sp.dma_start(lora_nat[:, :], a["kv_a_w"][0:LAT, :]).then_inc(s_w1, 16)
            sp.dma_start(gate_nat[:, :], a["gate_w"]).then_inc(s_w1, 16)
            sp.dma_start(kpe_nat[:, :, :],
                         a["kv_a_w"][LAT:LAT + H * ROPE, :].rearrange("(n p) k -> p n k", p=P)).then_inc(s_kpe, 16)
            heads = a["q_b_w"].rearrange("(h d) r -> d h r", d=DQ)
            for h in range(2):
                rows = heads[NOPE:DQ].rearrange("d (n two) r -> d n two r", two=2)[:, :, h, :]
                at = slice(64 * h, 64 * h + 64)
                sp.dma_start(wpe[at, :, 0:QR], rows).then_inc(s_wq, 16)
                sp.dma_start(wpe[at, :, QR:256], rows[:, :, P:QR]).then_inc(s_wq, 16)
            sp.dma_start(wqn[:, :, :], heads[0:NOPE]).then_inc(s_wq, 16)
            sp.dma_start(wk[:, :, :], a["kv_b_w"].rearrange("(h d) l -> d h l", d=NOPE + DV)[0:NOPE]).then_inc(s_wq, 16)
            for w, name in enumerate(("sp_q_w", "sp_k_w", "sp_v_w")):
                sp.dma_start(sp_nat[:, w, :, :], a[name].rearrange("(m p) n -> p m n", p=P)).then_inc(s_sp, 16)
            sp.dma_start(lnq[:, :], a["q_a_ln_w"].rearrange("(a n) -> a n", a=1).broadcast_to((P, QR))).then_inc(s_ln, 16)
            sp.dma_start(lnkv[:, :], a["kv_a_ln_w"].rearrange("(a n) -> a n", a=1).broadcast_to((P, LAT))).then_inc(s_ln, 16)
            sp.dma_start(gate_b[:, :], a["gate_b"].rearrange("(a n) -> a n", a=1).broadcast_to((P, 2))).then_inc(s_ln, 16)
            sp.dma_start(g["sel_f"][0:64, :], a["consts"][0:64, P:P + 256]).then_inc(s_const, 16)
            sp.dma_start(g["cos"][:, :], a["rope"][0]).then_inc(s_const, 16)
            sp.dma_start(g["sin"][:, :], a["rope"][1]).then_inc(s_const, 16)
            stage = d["wst"].rearrange("n p (c j) -> p n c j", j=P)

            def store_weights(c):
                sp.wait_ge(wsplit_hi, c + 1)
                sp.wait_ge(wsplit_lo, c + 1)
                for lo, t in enumerate((split_hi, split_lo)):
                    t = t[:, c % 2, :].bitcast(F32)
                    if c < 2:
                        sp.dma_start(stage[:, :, 8 + 2 * c + lo, :],
                                     t.rearrange("p (n j) -> p n j", j=P)).then_inc(wstored[c % 2], 16)
                    else:
                        kind, q = (c - 2) // 2, (c - 2) % 2
                        v = t.rearrange("p (n b j) -> p n b j", b=2, j=P)
                        for b in range(2):
                            sp.dma_start(stage[:, 4 * q:4 * q + 4, 4 * b + 2 * kind + lo, :],
                                         v[:, :, b, :]).then_inc(wstored[c % 2], 16)

            for c in range(6):
                store_weights(c)
            for i in range(8):
                w, m, h = jobs[first_spqk + i][1:]
                sp.wait_ge(ev_dve, sum(not b for b in by_act[:first_spqk + i + 1]))
                for lo, t in enumerate((sp_hi, sp_lo)):
                    sp.dma_start(d["spqk"][w, lo, m * P:(m + 1) * P, h * HALF:(h + 1) * HALF],
                                 t[:, i % NSP, :].bitcast(F32)).then_inc(spstored[i % NSP], 16)
            evacuated(sp, last("spv"))
            for q in range(4):
                sp.dma_start(d["vp"][q].rearrange("p (t n) -> p t n", t=NT),
                             vf[:, :, 64 * q:64 * q + 64]).then_inc(vstored, 16)
            sp.wait_ge(vstored, 64)
            for s in wstored:
                sp.wait_ge(s, 16 * (2 + 2 * 4))
            for s in spstored:
                sp.wait_ge(s, 16 * 16 // NSP)
            sp.wait_ge(s_const, 48)

        @block.gpsimd
        def _(pool):
            pool.memset(g["mhalf"][:, :], -0.5).then_inc(pool_own, 1)
            pool.wait_ge(stat, 2 * NT)
            pool.tensor_scalar(rstd[:, :], mv[:, :, 1], 1e-5, None, ALU.add).then_inc(pool_own, 1)
            pool.wait_ge(pool_own, 2)
            pool.tensor_tensor(rstd[:, :], rstd[:, :], g["mhalf"][:, 0:NT], ALU.pow).then_inc(rstd_ready, 1)
            pool.wait_ge(ssq_ready, 2 * NT)
            pool.tensor_scalar(rms[:, :, :], ssq[:, :, :], 1e-6, None, ALU.add).then_inc(pool_own, 1)
            pool.wait_ge(pool_own, 3)
            pool.tensor_tensor(rms[:, :, :], rms[:, :, :], g["mhalf"][:, 0:2 * NT].rearrange("p (a b) -> p a b", a=2),
                               ALU.pow).then_inc(rms_ready, 1)

        @block.tensor
        def _(pe):
            def transposes(n, blocks):
                at = 0
                for src in blocks:
                    k, m = src.shape[0], src.shape[1]
                    mm = pe.transpose(bank[n % 8][0:m, at:at + k], src, ident[0:k, 0:k])
                    at += k
                mm.then_inc(pe_job, 1)

            pe.wait_ge(s_ident, 16)
            for n, job in enumerate(jobs):
                kind, out = job[0], bank[n % 8]
                if n >= 8:
                    evacuated(pe, n - 8)
                if kind == "xT":
                    k, q = job[1:]
                    pe.wait_ge(xn_ready, 4 * q + 4)
                    transposes(n, [xn[:, 4 * q + j, k * P:(k + 1) * P] for j in range(4)])
                elif kind == "w1T":
                    k = slice(job[1] * P, (job[1] + 1) * P)
                    pe.wait_ge(s_w1, 48)
                    transposes(n, [qa_nat[:, 0, k], qa_nat[:, 1, k], lora_nat[:, k], gate_nat[:, k]])
                elif kind == "proj1":
                    t = slice(job[1] * P, (job[1] + 1) * P)
                    evacuated(pe, last("w1T"))
                    for k in range(NK):
                        mm = pe.matmul(out[:, 0:W1], xT[:, k, t], w1T[:, k, :], start=(k == 0), stop=(k == NK - 1))
                    mm.then_inc(pe_job, 1)
                elif kind == "spT":
                    pe.wait_ge(s_sp, 48)
                    transposes(n, [sp_nat[:, job[1], m, k * P:(k + 1) * P] for k in range(NK) for m in range(2)])
                elif kind == "kpT":
                    k, q = job[1:]
                    pe.wait_ge(s_kpe, 16)
                    transposes(n, [kpe_nat[:, 4 * q + j, k * P:(k + 1) * P] for j in range(4)])
                elif kind in ("pe0T", "pe1T"):
                    r = slice(0, P) if kind == "pe0T" else slice(P, 256)
                    pe.wait_ge(s_wq, 96)
                    transposes(n, [wpe[:, 4 * job[1] + j, r] for j in range(4)])
                elif kind == "lat0":
                    for j in range(8):
                        h = 8 * job[1] + j
                        mm = pe.matmul(out[:, 64 * j:64 * j + 64], wqn[:, h, 0:P], wk[:, h, :], start=True, stop=True)
                    mm.then_inc(pe_job, 1)
                elif kind == "lat1":
                    for j in range(8):
                        h = 8 * job[1] + j
                        for r in (0, 64):
                            mm = pe.matmul(out[r:r + 64, 64 * j:64 * j + 64], wqn[:, h, P:QR], wk[:, h, :],
                                           start=True, stop=True)
                    mm.then_inc(pe_job, 1)
                elif kind == "spqk":
                    w, m, h = job[1:]
                    evacuated(pe, last("spT"))
                    for k in range(NK):
                        mm = pe.matmul(out[:, :], spT[:, w, k, m * P:(m + 1) * P], xT[:, k, h * HALF:(h + 1) * HALF],
                                       start=(k == 0), stop=(k == NK - 1))
                    mm.then_inc(pe_job, 1)
                elif kind == "spv":
                    for j in range(2):
                        t = 2 * job[1] + j
                        for k in range(NK):
                            mm = pe.matmul(out[:, j * HID:(j + 1) * HID], xT[:, k, t * P:(t + 1) * P], spT[:, 2, k, :],
                                           start=(k == 0), stop=(k == NK - 1))
                    mm.then_inc(pe_job, 1)
                elif kind in ("qm0T", "qm1T"):
                    r = slice(0, P) if kind == "qm0T" else slice(P, 256)
                    pe.wait_ge(norm_ready, 1)
                    transposes(n, [m1[:, 4 * job[1] + j, r] for j in range(4)])
                elif kind == "cT":
                    pe.wait_ge(norm_ready, 1)
                    transposes(n, [cdup[:, 4 * job[1] + j, :] for j in range(4)])

        def plain(n):
            job = jobs[n]
            kind, out = job[0], bank[n % 8]
            if kind == "xT":
                return xT[:, job[1], job[2] * HALF:(job[2] + 1) * HALF], out[:, :]
            if kind == "w1T":
                return w1T[:, job[1], :], out[:, 0:W1]
            if kind == "proj1":
                return m1[:, job[1], :], out[:, 0:W1]
            if kind == "spT":
                return spT[:, job[1], :, :].rearrange("p k n -> p (k n)"), out[:, :]
            if kind == "kpT":
                return kpT[:, job[1], job[2] * HALF:(job[2] + 1) * HALF], out[:, :]
            if kind in ("pe0T", "pe1T"):
                to = aq[kind == "pe1T"][:, 4 * job[1]:4 * job[1] + 4, :]
                return (to.rearrange("p n (b j) -> p n b j", j=64)[:, :, 0:4:3, :],
                        out[:, :].rearrange("p (n b j) -> p n b j", b=2, j=64))
            if kind in ("lat0", "lat1"):
                to = aq[kind == "lat1"][:, 4 * job[1]:4 * job[1] + 4, 64:192]
                return to, out[:, :].rearrange("p (n j) -> p n j", j=P)
            if kind == "spv":
                return vf[:, 2 * job[1]:2 * job[1] + 2, :].rearrange("p t n -> p (t n)"), out[:, :]
            if kind == "cT":
                return cT[:, job[1] * HALF:(job[1] + 1) * HALF], out[:, :]
            return None

        def hi_of(n):
            job = jobs[n]
            if job[0] == "spqk":
                return sp_hi[:, (n - first_spqk) % NSP, :]
            cols = slice(job[1] * HALF, (job[1] + 1) * HALF)
            return (g["qm0h"] if job[0] == "qm0T" else g["qm1"])[:, cols]

        chunks = [kpT[:, 0, :], kpT[:, 1, :]] + [
            aq[kind][:, 4 * q:4 * q + 4, :].rearrange("p n j -> p (n j)") for kind in range(2) for q in range(2)]
        chunk_jobs = [last("kpT")] * 2 + [last("lat0")] * 2 + [last("lat1")] * 2

        @block.scalar
        def _(act):
            def weight_hi(c):
                evacuated(act, chunk_jobs[c])
                if c >= 2:
                    act.wait_ge(wstored[c % 2], 32 if c < 4 else 96)
                act.activation(split_hi[:, c % 2, :], chunks[c], ACT.Copy).then_inc(wsplit_hi, 1)

            for n, job in enumerate(jobs):
                if job[0] in split:
                    act.wait_ge(pe_job, n + 1)
                    if job[0] == "spqk" and n - first_spqk >= NSP:
                        i = n - first_spqk
                        act.wait_ge(spstored[i % NSP], 32 * (i // NSP))
                    act.activation(hi_of(n), bank[n % 8][:, :], ACT.Copy).then_inc(hi_ready, 1)
                elif by_act[n]:
                    act.wait_ge(pe_job, n + 1)
                    act.activation(*plain(n), ACT.Copy).then_inc(ev_act, 1)
                if n == last("xT") + 2:
                    evacuated(act, last("xT"))
                    act.activation(g["xh"][:, :, :], xT[:, :, :], ACT.Copy).then_inc(hi_ready, 1)
                if n == last("proj1") + 2:
                    evacuated(act, last("proj1"))
                    for t in range(NT):
                        act.activation(junk[:, :], m1[:, t, 0:QR], ACT.Square, scale=float(QR) ** -0.5,
                                       accum_out=ssq[:, 0, t:t + 1]).then_inc(ssq_ready, 1)
                        act.wait_ge(ssq_ready, 2 * t + 1)
                        act.activation(junk[:, 0:LAT], m1[:, t, QR:QR + LAT], ACT.Square, scale=float(LAT) ** -0.5,
                                       accum_out=ssq[:, 1, t:t + 1]).then_inc(ssq_ready, 1)
                        act.wait_ge(ssq_ready, 2 * t + 2)
                if n == last("qm1T"):
                    evacuated(act, last("cT"))
                    for b in range(4):
                        rows = slice(64, P) if b % 2 == 0 else slice(0, 64)
                        act.activation(g["kh"][rows, b, :], cT[rows, :], ACT.Copy).then_inc(kh_ready, 1)
                if n in chunk_after:
                    weight_hi(chunk_after.index(n))
            act.wait_ge(logits, 1)
            act.activation(gl[:, :, :], gl[:, :, :], ACT.Exp).then_inc(gexp, 1)
            act.wait_ge(s_const, 48)
            act.activation(g["sel"][0:64, :], g["sel_f"][0:64, :], ACT.Copy).then_inc(hi_ready, 1)

        @block.vector
        def _(dve):
            own = [0]

            def link(ins):
                own[0] += 1
                ins.then_inc(dve_own, 1)
                dve.wait_ge(dve_own, own[0])

            his = [0]

            def weight_lo(c):
                dve.wait_ge(wsplit_hi, c + 1)
                dve.tensor_tensor(split_lo[:, c % 2, :], chunks[c], split_hi[:, c % 2, :].bitcast(F32),
                                  ALU.subtract).then_inc(wsplit_lo, 1)

            for q in range(2):
                dve.wait_ge(s_x[q], 16)
                for t in range(4 * q, 4 * q + 4):
                    dve.bn_stats(stats[:, t, :], xn[:, t, :]).then_inc(stat, 1)
            dve.wait_ge(stat, NT)
            for t in range(NT):
                dve.bn_aggr(mv[:, t, :], stats[:, t, :]).then_inc(stat, 1)
            dve.wait_ge(rstd_ready, 1)
            for t in range(NT):
                dve.tensor_scalar(xn[:, t, :], xn[:, t, :], mv[:, t, 0:1], rstd[:, t:t + 1],
                                  ALU.subtract, ALU.mult).then_inc(xn_ready, 1)
            for n, job in enumerate(jobs):
                kind = job[0]
                if kind in split:
                    his[0] += 1
                    dve.wait_ge(hi_ready, 1 + his[0])
                    src, hi = bank[n % 8], hi_of(n)
                    if kind == "spqk":
                        lo = sp_lo[:, (n - first_spqk) % NSP, :]
                        dve.tensor_tensor(lo, src[:, :], hi.bitcast(F32), ALU.subtract).then_inc(ev_dve, 1)
                    elif kind == "qm0T":
                        lo = g["qm0l"][:, job[1] * HALF:(job[1] + 1) * HALF]
                        dve.tensor_tensor(lo, src[:, :], hi.bitcast(F32), ALU.subtract).then_inc(ev_dve, 1)
                    else:
                        dve.tensor_tensor(hi[64:P, :], src[64:P, :], hi[64:P, :].bitcast(F32),
                                          ALU.subtract).then_inc(ev_dve, 1)
                elif not by_act[n]:
                    dve.wait_ge(pe_job, n + 1)
                    dve.tensor_copy(*plain(n)).then_inc(ev_dve, 1)
                if n == last("xT") + 4:
                    dve.wait_ge(hi_ready, 1)
                    link(dve.tensor_tensor(g["xl"][:, :, :], xT[:, :, :], g["xh"][:, :, :].bitcast(F32), ALU.subtract))
                if n == last("spqk"):
                    dve.wait_ge(rms_ready, 1)
                    dve.wait_ge(s_ln, 48)
                    for t in range(NT):
                        for r in (0, 64):
                            ins = dve.scalar_tensor_tensor(cdup[:, t, r:r + 64], m1[:, t, QR:QR + LAT],
                                                           rms[:, 1, t:t + 1], lnkv[:, :], ALU.mult, ALU.mult)
                    link(ins)
                    for t in range(NT):
                        ins = dve.scalar_tensor_tensor(m1[:, t, 0:QR], m1[:, t, 0:QR], rms[:, 0, t:t + 1],
                                                       lnq[:, :], ALU.mult, ALU.mult)
                    link(ins)
                    link(dve.tensor_copy(m1[:, :, QR:256], m1[:, :, P:QR]))
                    dve.tensor_tensor(gl[:, :, :], m1[:, :, 256:258],
                                      gate_b[:, :].unsqueeze(1).broadcast_to((P, NT, 2)), ALU.add).then_inc(norm_ready, 1)
                    dve.wait_ge(norm_ready, 1)
                    link(dve.tensor_reduce(gmax[:, :], gl[:, :, :], AX, ALU.max))
                    dve.tensor_tensor(gl[:, :, :], gl[:, :, :], gmax[:, :].unsqueeze(2).broadcast_to((P, NT, 2)),
                                      ALU.subtract).then_inc(logits, 1)
                if n == last("qm1T"):
                    for b in range(4):
                        dve.wait_ge(kh_ready, b + 1)
                        rows = slice(64, P) if b % 2 == 0 else slice(0, 64)
                        ins = dve.tensor_tensor(g["kl"][rows, b, :], cT[rows, :], g["kh"][rows, b, :].bitcast(F32),
                                                ALU.subtract)
                    link(ins)
                if n in chunk_after:
                    weight_lo(chunk_after.index(n))
            dve.wait_ge(gexp, 1)
            link(dve.tensor_reduce(gsum[:, :], gl[:, :, :], AX, ALU.add))
            link(dve.reciprocal(gsum[:, :], gsum[:, :]))
            link(dve.tensor_tensor(gates[:, :, :], gl[:, :, :], gsum[:, :].unsqueeze(2).broadcast_to((P, NT, 2)),
                                   ALU.mult))



X_STEPS = [
    [("mm", 3), ("P", 0)],
    [("S", 1), ("mm", 3), ("P", 1)],
    [("o", 1), ("mm", 3), ("P", 2)],
    [("o", 1), ("mm", 3), ("P", 3)],
    [("o", 1), ("pm", 4)],
    [("o", 1), ("pm", 3), ("P", 4)],
    [("mT", 1), ("pm", 4)],
    [("pm", 4), ("P", 5)],
    [("pm", 5)],
    [("S", 0), ("pm", 4)],
    [("pm", 4)],
    [("pm", 4)],
    [("pT", 0), ("pT", 1), ("mm", 4)],
    [("mm", 6)],
    [("mm", 6)],
    [("mT", 0), ("mm", 4)],
]
X_FIRST = [
    [("P", 0), ("P", 1)],
    [("P", 2), ("P", 3)],
    [("pm", 5)],
    [("pm", 5)],
    [("pm", 5)],
    [("pm", 4), ("P", 4)],
    [("pm", 4)],
    [("pm", 3), ("P", 5)],
    [("oT", 1), ("pm", 1), ("oT", 1), ("pm", 1), ("oT", 1)],
    [("oT", 1), ("pm", 1), ("oT", 1), ("pm", 1), ("oT", 1)],
    [("oT", 1), ("pm", 1), ("oT", 2), ("pm", 1), ("oT", 1)],
    [("pT", 0), ("pT", 1)],
    [("vo", 1), ("mm", 3)],
    [("vo", 1), ("mm", 5)],
    [("vo", 1), ("mm", 6)],
    [("vo", 1), ("mm", 6), ("mT", 0)],
]
MM_LATE = 20
BY_ACT = ("mT", "pT", "S", "oT", "vo", "o")


def x_steps(v):
    count = {"pm": 0, "mm": MM_LATE if v else 0, "oT": 0, "vo": 0, "o": 0}
    steps = []
    for tiles in X_STEPS if v else X_FIRST:
        step = []
        for kind, n in tiles:
            numbers = [n]
            if kind in count:
                numbers = [(count[kind] + i) % 32 for i in range(n)]
                count[kind] += n
            for i in numbers:
                if (kind, i) == ("mT", 1) or kind == "mm" and i >= MM_LATE:
                    here = 1 <= v <= NP
                elif kind == "o":
                    here = v == NP + 1
                elif kind == "S":
                    here = v >= 2 if i else 1 <= v <= NP
                else:
                    here = v < NP
                if here:
                    step.append((kind, i))
        steps.append(step)
    return steps


def attention(nc, a, d, g):
    NS = 16
    slots = range(NP + 2)
    xs = [x_steps(v) for v in slots]
    x_index = {}
    for v in slots:
        for step in xs[v]:
            for tile in step:
                x_index[(v, *tile)] = len(x_index)

    x_tiles = [(t[0], t[1:]) for t in x_index]

    with ExitStack() as ctx:
        def sb(name, shape, dt=F32):
            return ctx.enter_context(nc.sbuf_tensor(name, shape, dt))

        def ps(name):
            return ctx.enter_context(nc.psum_tensor(name, [P, HALF], F32))

        def sem(name):
            return ctx.enter_context(nc.semaphore(name))

        NST, NX = 3, 3
        st = [ps(f"st{i}") for i in range(NST)]
        xb = [ps(f"xb{i}") for i in range(NX)]
        pvm = ps("pvm")
        pvp = ps("pvp")
        kh, kl = g["kh"], g["kl"]
        qh, ql, wst = g["qh"], g["ql"], g["wst"]
        raw, rot, rc = g["raw"], g["rot"], g["rc"]
        em = g["em"]
        ep = sb("ep", [P, 8, HALF])
        acc = sb("acc", [P, 2, HALF])
        pq = sb("pq", [P, 2, 2, HALF], F32R)
        pk = sb("pk", [P, 2, 2, S], F32R)
        vp = sb("vp", [P, 2, NT, 4, 32])
        ones = sb("ones", [P, 64])
        mr = sb("mr", [64, S], F32R)
        mrp = sb("mrp", [4, HALF], F32R)
        m2 = sb("m2", [P, 2, 2, 4, 2])
        ms = sb("ms", [P, 2, 4, 2])
        m2p = sb("m2p", [P, 4, 4, 2])
        msp = sb("msp", [P, 4, 4])
        ctxr = sb("ctxr", [P, HALF])
        sums = sb("sums", [P, HALF])
        rec = sb("rec", [P, HALF])
        pvr = sb("pvr", [P, HALF])
        prec = sb("prec", [P, HALF])
        amax = sb("amax", [P, 32])
        inv = sb("inv", [P, 32])
        ident, sel, cdup = g["ident"], g["sel"], g["cdup"]
        o_nat = em[:, :, :].rearrange("p a b -> p (a b)").rearrange("p (m n) -> p m n", m=2)
        oT = ep[:, :, :].rearrange("p a b -> p (a b)").rearrange("p (h n) -> p h n", n=HID)
        wv = acc[:, :, :].rearrange("p a b -> p (a b)").rearrange("p (h l) -> p h l", l=LAT)
        spo_nat = [t[:, :].rearrange("p (g e) -> p g e", e=32) for t in (ctxr, sums)]
        vo_out = [ctxr, sums, pvr, prec]
        natural = [g["cos"], g["sin"]]
        code, absolute, sign = (g[n + "_f"][:, :] for n in ("qm0h", "qm0l", "qm1"))

        init = sem("init")
        init_odd = sem("init_odd")
        x_ready = sem("x_ready")
        x_dve = sem("x_dve")
        x_act = sem("x_act")
        st_ready = sem("st_ready")
        e_ready = sem("e_ready")
        pvm_done = sem("pvm_done")
        pvp_done = sem("pvp_done")
        added = sem("added")
        raw_ready = sem("raw_ready")
        lat_hi = sem("lat_hi")
        cos_done = sem("cos_done")
        turned = [sem(f"turned{i}") for i in range(2)]
        sin_done = sem("sin_done")
        roped = sem("roped")
        rope_hi = sem("rope_hi")
        rope_lo = sem("rope_lo")
        mm_ready = sem("mm_ready")
        pm_ready = sem("pm_ready")
        mrow_in = sem("mrow_in")
        wst_in = [sem(f"wst_in{i}") for i in range(2)]
        stack_in = [sem(f"stack_in{i}") for i in range(2)]
        vp_in = [sem(f"vp_in{i}") for i in range(2)]
        ctx_out = sem("ctx_out")
        rec_part = sem("rec_part")
        ctx_ready = sem("ctx_ready")
        ctx_stored = sem("ctx_stored")
        pat_out = sem("pat_out")
        pat_part = sem("pat_part")
        pat_ready = sem("pat_ready")
        pat_stored = sem("pat_stored")

        ow_in = sem("ow_in")
        spo_in = sem("spo_in")
        vo_stored = sem("vo_stored")
        ffn_in = [sem(f"ffn_in{i}") for i in range(2)]
        transposed = sem("transposed")
        q_own = sem("q_own")
        ctx_back = sem("ctx_back")

        block = ctx.enter_context(nc.Block())

        DIRECT = 2 * NP - 3
        PDIRECT = NP - 2

        first = sum(v == 0 for v, _ in x_tiles)

        def ring_place(n):
            return n % (NX + NST) if n < first else n % NX

        def x_bank(v, tile):
            return (xb + st)[ring_place(x_index[(v, *tile)])]

        def x_wait(eng, v, tile):
            eng.wait_ge(x_ready, x_index[(v, *tile)] + 1)

        def x_emptied(eng, v, tile):
            kind = tile[0] in BY_ACT
            n = sum((t[1] in BY_ACT) == kind and i <= x_index[(v, *tile)] for t, i in x_index.items())
            eng.wait_ge(x_act if kind else x_dve, n)

        def adds(it, q, kt, h):
            return 28 * it + 14 * q + 2 * (max(kt, 1) - 1) + h + 1

        NSTACK = 12
        UNIT = [(0, 1), (2, 3), (4,), (5,)]

        def unit_at(v, s):
            return {3: 0, 5: 1, 7: 2, 9: 3}.get(s) if v < NP else None


        @block.sync
        def _(sp):
            def load_stacks(v):
                quad, half, b = v // 2, v % 2, v % 2
                for w, to, cols in ((0, pq, slice(half * HALF, (half + 1) * HALF)), (1, pk, slice(0, S))):
                    for j in range(2):
                        for slot in range(3):
                            lo = int(slot == (2 if w == 0 else 1))
                            src = d["spqk"][w, lo, 64 * quad:64 * quad + 64, cols].rearrange(
                                "(t j p) n -> j p t n", j=2, p=PD)[j]
                            at = 64 * j + PD * slot
                            sp.dma_start(to[at:at + PD, b, :, :].bitcast(F32), src).then_inc(stack_in[v % 2], 16)

            def load_vp(v):
                to = vp[:, v % 2, :, :, :].rearrange("p t n e -> p (t n) e")
                sp.dma_start(to[:, :, 0:PD], d["vp"][v // 2].rearrange("p (g e) -> p g e", e=PD)).then_inc(vp_in[v % 2], 16)

            def load_weights(v):
                sp.dma_start(wst[:, v % 2, :, :].rearrange("p c j -> p (c j)").bitcast(F32), d["wst"][v]).then_inc(wst_in[v % 2], 16)

            def turn(v, u):
                n = 4 * v + u
                sp.wait_ge(raw_ready, 6 * v + UNIT[u][-1] + 1)
                if n >= 2:
                    sp.wait_ge(roped, n - 1)
                for b in range(4):
                    o = b ^ 1
                    sp.dma_start(rot[32 * b:32 * b + 32, n % 2, :], raw[32 * o:32 * o + 32, n % 2, :]).then_inc(turned[n % 2], 16)

            def load_ffn(c):
                src = (a["ffn_up"][c * P:(c + 1) * P, :] if c < 2 else
                       a["ffn_down"].rearrange("(k p) n -> p k n", p=P)[:, 4 * (c - 2):4 * (c - 1), :])
                to = natural[c % 2][:, :]
                if c >= 2:
                    to = to.rearrange("p (k n) -> p k n", n=HID)
                sp.dma_start(to, src).then_inc(ffn_in[c % 2], 16)

            def load_epilogue():
                for j in range(4):
                    sp.dma_start((rot if j < 2 else rc)[:, j % 2, :], d["vo"][j]).then_inc(ctx_back, 16)
                sp.wait_ge(pat_stored, 16 * PDIRECT)
                for n in range(PDIRECT):
                    sp.dma_start(pattern_tile(g, n), d["pat"][n]).then_inc(ctx_back, 16)
                sp.wait_ge(st_ready, 64 * (NP - 1))
                sp.wait_ge(ctx_stored, 16 * DIRECT)
                for n in range(DIRECT):
                    half = slice(n % 2 * HALF, (n % 2 + 1) * HALF)
                    sp.dma_start(context_tile(g, n // 2)[:, half], d["ctx"][n // 2, :, half]).then_inc(ctx_back, 16)
                for c in (2, 3):
                    sp.wait_ge(transposed, c - 1)
                    load_ffn(c)
                sp.wait_ge(ctx_back, 16 * (4 + PDIRECT + DIRECT))

            load_weights(0)
            for v in slots:
                if v < NP:
                    if v >= 2:
                        sp.wait_ge(st_ready, 64 * (v - 1))
                    if v == 0:
                        sp.wait_ge(init, 6)
                    if v == 1:
                        sp.wait_ge(init_odd, 2)
                    load_stacks(v)
                    if v + 1 < NP:
                        if v >= 1:
                            x_wait(sp, v - 1, ("P", 5))
                        load_weights(v + 1)
                    turn(v, 0)
                    if v == 0:
                        sp.dma_start(o_nat, a["o_w"].rearrange("(m p) n -> p m n", p=P)).then_inc(ow_in, 16)
                        sp.dma_start(wv, a["kv_b_w"].rearrange("(h d) l -> d h l", d=NOPE + DV)[NOPE:NOPE + DV]
                                     ).then_inc(ow_in, 16)
                        for m in range(2):
                            sp.dma_start(spo_nat[m][:, :, 0:PD], a["sp_o_w"][m * P:(m + 1) * P, :].rearrange(
                                "p (g e) -> p g e", e=PD)).then_inc(spo_in, 16)
                if v == NP:
                    load_epilogue()
                if 2 <= v < NP:
                    sp.wait_ge(ctx_ready, 2 * (v - 2) + 2)
                    sp.dma_start(d["ctx"][v - 2, :, HALF:S], rec[:, :]).then_inc(ctx_stored, 16)
                if v < NP:
                    if v >= 2:
                        sp.wait_ge(pvp_done, NT * (v - 1))
                    load_vp(v)
                    turn(v, 1)
                if 2 <= v < NP:
                    sp.wait_ge(pat_ready, v - 1)
                    sp.dma_start(d["pat"][v - 2], prec[:, :]).then_inc(pat_stored, 16)
                if v < NP:
                    for u in (2, 3):
                        turn(v, u)
                if v == NP - 1:
                    sp.wait_ge(rope_lo, 8 * NP)
                    sp.wait_ge(sin_done, 4 * NP)
                    x_emptied(sp, NP - 1, ("P", 5))
                    load_ffn(0)
                    load_ffn(1)
                if 1 <= v < NP:
                    sp.wait_ge(ctx_ready, 2 * (v - 1) + 1)
                    sp.dma_start(d["ctx"][v - 1, :, 0:HALF], rec[:, :]).then_inc(ctx_stored, 16)
                if v < NP:
                    x_emptied(sp, v, ("pT", 1))
                    for hh in range(4):
                        at = 64 * (hh % 2) + 3 * PD
                        sp.dma_start(pq[at:at + 1, v % 2, hh // 2, :].bitcast(F32),
                                     mrp[hh:hh + 1, :].bitcast(F32)).then_inc(mrow_in, 16)
                if v == 0:
                    for j in range(4):
                        x_emptied(sp, 0, ("vo", j))
                        sp.dma_start(d["vo"][j], vo_out[j][:, :]).then_inc(vo_stored, 16)

        @block.gpsimd
        def _(pool):
            pool.memset(pq[:, 0, :, :].bitcast(F32), 0.0).then_inc(init, 1)
            pool.memset(vp[:, :, :, :, PD:32], 1.0).then_inc(init, 1)
            pool.memset(ones[:, :], 1.0).then_inc(init, 1)
            pool.memset(ctxr[:, :], 0.0).then_inc(init, 1)
            pool.memset(sums[:, :], 0.0).then_inc(init, 1)
            pool.memset(pq[:, 1, :, :].bitcast(F32), 0.0).then_inc(init_odd, 1)

            def turn_sin(v, u):
                n = 4 * v + u
                half = slice((u % 2) * HALF, (u % 2 + 1) * HALF)
                pool.wait_ge(turned[n % 2], 64 * (n // 2 + 1))
                pool.tensor_tensor(rot[:, n % 2, :], rot[:, n % 2, :], g["sin"][:, half], ALU.mult).then_inc(sin_done, 1)

            def rope(v, u):
                n = 4 * v + u
                pool.wait_ge(sin_done, n + 1)
                if u < 2:
                    pool.wait_ge(cos_done, 4 * v + 2 * u + 2)
                else:
                    x_emptied(pool, v, ("P", UNIT[u][0]))
                pool.tensor_tensor(rc[:, n % 2, :], rc[:, n % 2, :], rot[:, n % 2, :], ALU.add).then_inc(roped, 1)

            def rope_lo_of(v, u, s):
                n = 4 * v + u
                if v:
                    it, t = (v - 1, s - 1)
                    pool.wait_ge(added, 28 * it + 14 * (t // NT) + 2 * (t % NT))
                half = slice((u % 2) * HALF, (u % 2 + 1) * HALF)
                hi, lo = (qh, ql) if u < 2 else (kh, kl)
                for h in range(2):
                    rows = slice(64 * h, 64 * h + 64)
                    pool.wait_ge(rope_hi, 2 * n + h + 1)
                    pool.tensor_tensor(lo[rows, 2 * (v % 2) + h, half], rc[rows, n % 2, :],
                                       hi[rows, 2 * (v % 2) + h, half].bitcast(F32),
                                       ALU.subtract).then_inc(rope_lo, 1)
                pool.wait_ge(rope_lo, 2 * n + 2)

            def add(it, q, kt):
                for h in range(2):
                    j = 2 * (NT * q + kt) + h
                    pool.wait_ge(e_ready, 64 * it + 4 * (NT * q + kt) + 2 * h + 1)
                    if kt == 1:
                        if q == 1:
                            x_wait(pool, it + 1, ("S", 0))
                        elif it >= 1:
                            x_wait(pool, it + 1, ("S", 1))
                        else:
                            x_wait(pool, 0, ("vo", 3))
                        first = em[:, (j - 2) % 8, :]
                    else:
                        pool.wait_ge(added, adds(it, q, kt - 1, h))
                        first = acc[:, h, :]
                    pool.tensor_tensor(acc[:, h, :], first, em[:, j % 8, :], ALU.add).then_inc(added, 1)

            for v in slots:
                for s in range(NS):
                    if unit_at(v, s - 1) is not None:
                        rope_lo_of(v, unit_at(v, s - 1), s)
                    if unit_at(v, s) is not None:
                        turn_sin(v, unit_at(v, s))
                        rope(v, unit_at(v, s))
                    if 1 <= v <= NP and s % NT:
                        add(v - 1, s // NT, s % NT)

        @block.scalar
        def _(act):
            def produce(v, i):
                tile, n = x_bank(v, ("P", i)), 6 * v + i
                x_wait(act, v, ("P", i))
                u = next(u for u in range(4) if i in UNIT[u])
                un = 4 * v + u
                if i == UNIT[u][0] and un >= 2:
                    act.wait_ge(turned[un % 2], 64 * (un // 2))
                if i < 4:
                    h, half = i % 2, slice((i // 2) * HALF, (i // 2 + 1) * HALF)
                    pe_rows = slice(64 * h, 64 * h + 64)
                    lat_rows = slice(64 - 64 * h, P - 64 * h)
                    act.activation(raw[pe_rows, un % 2, :], tile[pe_rows, :], ACT.Copy).then_inc(raw_ready, 1)
                    act.activation(qh[lat_rows, 2 * (v % 2) + h, half], tile[lat_rows, :],
                                   ACT.Copy).then_inc(lat_hi, 1)
                else:
                    act.activation(raw[:, un % 2, :], tile[:, :], ACT.Copy).then_inc(raw_ready, 1)

            def x_tile(v, tile):
                kind, i = tile
                if kind == "P":
                    produce(v, i)
                if kind not in BY_ACT:
                    return
                x_wait(act, v, tile)
                src = x_bank(v, tile)
                if kind == "mT":
                    at = 32 * ((v - i) % 2)
                    act.activation(mr[at:at + 2, i * HALF:(i + 1) * HALF], src[0:2, :], ACT.Copy).then_inc(x_act, 1)
                elif kind == "pT":
                    if v:
                        act.wait_ge(mrow_in, 64 * v)
                    act.activation(mrp[:, 256 * i:256 * i + 256], src[0:4, 0:256], ACT.Copy).then_inc(x_act, 1)
                elif kind == "oT":
                    to = oT[:, 2 * i:2 * i + 2, :] if i < 8 else g["spoT"][:, 2 * (i - 8):2 * (i - 8) + 2, :]
                    act.activation(to.rearrange("p h n -> p (h n)"), src[:, :], ACT.Copy).then_inc(x_act, 1)
                elif kind == "o":
                    if i == 0:
                        act.wait_ge(pvm_done, 32 * NP)
                        act.wait_ge(added, 28 * NP)
                    act.activation(em[:, i, :], src[:, :], ACT.Copy).then_inc(x_act, 1)
                elif kind == "vo":
                    act.activation(vo_out[i][:, :], src[:, :], ACT.Copy).then_inc(x_act, 1)
                elif kind == "S":
                    n = 2 * (v - 2) + 1 if i else 2 * (v - 1)
                    if n:
                        act.wait_ge(rec_part, 4 * n)
                    act.activation(sums[:, :], src[:, :], ACT.Copy).then_inc(x_act, 1)

            def rope_hi_of(v, u):
                n = 4 * v + u
                half = slice((u % 2) * HALF, (u % 2 + 1) * HALF)
                act.wait_ge(roped, n + 1)
                for h in range(2):
                    rows = slice(64 * h, 64 * h + 64)
                    to = (qh if u < 2 else kh)[rows, 2 * (v % 2) + h, half]
                    act.activation(to, rc[rows, n % 2, :], ACT.Copy).then_inc(rope_hi, 1)

            for v in slots:
                it = v - 1
                for s in range(NS):
                    if s == 1 and v >= 2 or s == 9 and 1 <= v <= NP:
                        n = 2 * (v - 2) + 1 if s == 1 else 2 * it
                        act.wait_ge(pvm_done, 16 * (n + 1))
                        if n:
                            act.wait_ge(ctx_ready, n)
                        else:
                            act.wait_ge(vo_stored, 64)
                        act.activation(ctxr[:, :], pvm[:, :], ACT.Copy).then_inc(ctx_out, 1)
                    if s == 2 and v >= 2:
                        act.wait_ge(pvp_done, NT * (v - 1))
                        if v > 2:
                            act.wait_ge(pat_ready, v - 2)
                        act.activation(pvr[:, :], pvp[:, :], ACT.Copy).then_inc(pat_out, 1)
                    tiles = iter(xs[v][s])
                    if 0 <= it < NP:
                        for x in range(4):
                            n = 64 * it + 4 * s + x
                            j = 32 * it + 2 * s + x // 2
                            act.wait_ge(st_ready, n + 1)
                            if j >= 8:
                                if x % 2 == 0:
                                    act.wait_ge(pvm_done, j - 7)
                                    o = j - 8
                                    act.wait_ge(added, adds(o // 32, o % 32 // 16, o % 16 // 2, o % 2))
                                else:
                                    act.wait_ge(pvp_done, (j - 8) // 4 + 1)
                            if x % 2 == 0:
                                act.activation(em[:, j % 8, :], st[n % NST][:, :], ACT.Exp,
                                               scale=MAIN_SCALE).then_inc(e_ready, 1)
                            else:
                                act.activation(ep[:, j % 8, :], st[n % NST][:, :], ACT.Exp,
                                               scale=PAT_SCALE).then_inc(e_ready, 1)
                            for tile in islice(tiles, 1):
                                x_tile(v, tile)
                    for tile in tiles:
                        x_tile(v, tile)
                    if unit_at(v, s) is not None:
                        rope_hi_of(v, unit_at(v, s))

        @block.vector
        def _(dve):
            dve.memset(pk[:, 0, :, :].bitcast(F32), -1.0).then_inc(init, 1)
            dve.memset(pk[:, 1, :, :].bitcast(F32), -1.0).then_inc(init_odd, 1)

            def produce(v, i):
                tile, n = x_bank(v, ("P", i)), 6 * v + i
                u = next(u for u in range(4) if i in UNIT[u])
                half = slice((u % 2) * HALF, (u % 2 + 1) * HALF)
                un = 4 * v + u
                if un >= 2:
                    dve.wait_ge(rope_lo, 2 * (un - 1))
                if i < 4:
                    h = i % 2
                    pe_rows = slice(64 * h, 64 * h + 64)
                    lat_rows = slice(64 - 64 * h, P - 64 * h)
                    dve.wait_ge(raw_ready, n + 1)
                    dve.tensor_tensor(rc[pe_rows, un % 2, :], tile[pe_rows, :], g["cos"][pe_rows, half],
                                      ALU.mult).then_inc(cos_done, 1)
                    dve.wait_ge(lat_hi, 4 * v + i + 1)
                    dve.tensor_tensor(ql[lat_rows, 2 * (v % 2) + h, half], tile[lat_rows, :],
                                      qh[lat_rows, 2 * (v % 2) + h, half].bitcast(F32),
                                      ALU.subtract).then_inc(x_dve, 1)
                else:
                    dve.wait_ge(raw_ready, n + 1)
                    dve.tensor_tensor(rc[:, un % 2, :], tile[:, :], g["cos"][:, half], ALU.mult).then_inc(x_dve, 1)

            def x_tile(v, tile):
                kind, i = tile
                if kind == "P":
                    produce(v, i)
                if kind not in ("pm", "mm"):
                    return
                x_wait(dve, v, tile)
                src = x_bank(v, tile)
                if kind == "pm":
                    dve.tensor_reduce(m2p[:, i // 8, i % 4, i // 4 % 2:i // 4 % 2 + 1], src[:, :], AX,
                                      ALU.max).then_inc(x_dve, 1)
                    if i == 31:
                        x_emptied(dve, v, tile)
                        if v:
                            x_wait(dve, v - 1, ("pT", 1))
                        dve.tensor_reduce(msp[:, :, :], m2p[:, :, :, :], AX, ALU.max).then_inc(pm_ready, 1)
                elif kind == "mm":
                    q, h, t, kt = i // 16, i // 8 % 2, i // 2 % 4, i % 2
                    dve.tensor_reduce(m2[:, q, h, t, kt:kt + 1], src[:, :], AX, ALU.max).then_inc(x_dve, 1)
                    if i % 16 == 15:
                        x_emptied(dve, v, tile)
                        dve.tensor_reduce(ms[:, q, :, :].rearrange("p t h -> p h t"), m2[:, q, :, :, :], AX,
                                          ALU.max).then_inc(mm_ready, 1)

            QUARTER = HALF // 4

            def main_reciprocal(v, i, j):
                n = 2 * (v - 2) + 1 if i else 2 * (v - 1)
                cols = slice(j * QUARTER, (j + 1) * QUARTER)
                if j == 0:
                    x_emptied(dve, v, ("S", i))
                    if n:
                        dve.wait_ge(ctx_ready, n)
                        dve.wait_ge(ctx_stored, 16 * min(n, DIRECT))
                    if n == DIRECT:
                        dve.wait_ge(st_ready, 64 * (NP - 1))
                dve.reciprocal(rec[:, cols], sums[:, cols]).then_inc(rec_part, 1)
                if j == 3:
                    dve.wait_ge(rec_part, 4 * (n + 1))
                    dve.wait_ge(ctx_out, n + 1)
                    to = rec[:, :]
                    if n >= DIRECT:
                        to = context_tile(g, n // 2)[:, n % 2 * HALF:(n % 2 + 1) * HALF]
                    dve.tensor_tensor(to, ctxr[:, :], rec[:, :], ALU.mult).then_inc(ctx_ready, 1)

            def pattern_reciprocal(it, j):
                cols = slice(j * QUARTER, (j + 1) * QUARTER)
                if j == 0:
                    dve.wait_ge(pat_out, it + 1)
                    if it:
                        dve.wait_ge(pat_ready, it)
                        dve.wait_ge(pat_stored, 16 * min(it, PDIRECT))
                    else:
                        dve.wait_ge(vo_stored, 64)
                    if it == PDIRECT:
                        for t in turned:
                            dve.wait_ge(t, 128 * NP)
                    dve.stream_shuffle(prec[:, :], pvr[:, :], [i | 16 for i in range(32)]).then_inc(pat_part, 1)
                    dve.wait_ge(pat_part, 5 * it + 1)
                dve.reciprocal(prec[:, cols], prec[:, cols]).then_inc(pat_part, 1)
                if j == 3:
                    dve.wait_ge(pat_part, 5 * it + 5)
                    to = prec[:, :] if it < PDIRECT else pattern_tile(g, it)
                    dve.tensor_tensor(to, pvr[:, :], prec[:, :], ALU.mult).then_inc(pat_ready, 1)

            def between(v, s, j):
                if v >= 2 and s in (2, 3):
                    main_reciprocal(v, 1, 2 * (s - 2) + j)
                if v >= 2 and s in (4, 5):
                    pattern_reciprocal(v - 2, 2 * (s - 4) + j)
                if 1 <= v <= NP and s in (10, 11):
                    main_reciprocal(v, 0, 2 * (s - 10) + j)

            own = [0]

            def link(ins):
                own[0] += 1
                ins.then_inc(q_own, 1)
                dve.wait_ge(q_own, own[0])

            QUANTIZE = 18

            def quantize(c, step):
                spread = lambda t: t[:, :].unsqueeze(2).broadcast_to((P, 32, 32))
                blocks = lambda t: t.rearrange("p (b j) -> p b j", j=32)
                thresholds = {6: 3.5, 7: 2.5, 9: 1.75, 10: 1.25, 11: 0.75, 12: 0.25}

                if step == 0:
                    if c == 0:
                        x_wait(dve, NP - 1, ("P", 5))
                    dve.wait_ge(ffn_in[c % 2], 16 * (c // 2 + 1))
                    link(dve.transpose(sign, natural[c % 2][:, :]))
                    dve.engine_nop().then_inc(transposed, 1)
                elif step == 1:
                    link(dve.tensor_reduce(amax[:, :], blocks(sign), AX, ALU.max, apply_absolute_value=True))
                elif step == 2:
                    link(dve.tensor_scalar(amax[:, :], amax[:, :], 1e-30, None, ALU.max))
                    link(dve.tensor_scalar(amax[:, :].bitcast(I32), amax[:, :].bitcast(I32), 0x7F800000, None,
                                           ALU.bitwise_and))
                    link(dve.reciprocal(inv[:, :], amax[:, :]))
                elif step == 3:
                    link(dve.tensor_scalar(absolute.bitcast(I32), sign.bitcast(I32), 0x7FFFFFFF, None, ALU.bitwise_and))
                elif step == 4:
                    link(dve.scalar_tensor_tensor(blocks(absolute), blocks(absolute), 4.0, spread(inv), ALU.mult,
                                                  ALU.mult))
                elif step == 5:
                    link(dve.tensor_scalar(code, absolute, 5.0, 2.0, ALU.is_ge, ALU.mult))
                elif step in thresholds:
                    link(dve.scalar_tensor_tensor(code, absolute, thresholds[step], code, ALU.is_ge, ALU.add))
                elif step == 8:
                    link(dve.tensor_scalar(code, code, 2.0, None, ALU.mult))
                elif step == 13:
                    link(dve.tensor_scalar(sign.bitcast(I32), sign.bitcast(I32), -2147483648, None, ALU.bitwise_and))
                elif step == 14:
                    link(dve.tensor_tensor(code.bitcast(I32), code.bitcast(I32), sign.bitcast(I32), ALU.bitwise_or))
                elif step == 15:
                    link(dve.scalar_tensor_tensor(blocks(code), blocks(code), 0.125, spread(amax), ALU.mult, ALU.mult))
                elif step == 16:
                    link(dve.transpose(absolute, code))
                elif step == 17:
                    to = g["xh"][:, c, :] if c < 2 else g["xl"][:, c - 2, :]
                    link(dve.tensor_copy(to, absolute))

            def quantized(v, s):
                if (v, s) < (NP - 1, 12) or v > NP:
                    return 0
                return 3 if v < NP or s < 4 else 5

            q_step = 0
            for v in slots:
                for s in range(NS):
                    q_end = min(q_step + quantized(v, s), 4 * QUANTIZE)
                    for n, tile in enumerate(xs[v][s]):
                        x_tile(v, tile)
                        if n in (1, 3):
                            between(v, s, n // 2)
                        if tile[0] == "mm" and q_step < q_end:
                            quantize(*divmod(q_step, QUANTIZE))
                            q_step += 1
                    for j in range(2):
                        if len(xs[v][s]) < 2 * j + 2:
                            between(v, s, j)
                    while q_step < q_end:
                        quantize(*divmod(q_step, QUANTIZE))
                        q_step += 1

        @block.tensor
        def _(pe):

            def passes(out, pairs, sem_):
                for n, (w, x) in enumerate(pairs):
                    mm = pe.matmul(out, w, x, start=(n == 0), stop=(n == len(pairs) - 1))
                mm.then_inc(sem_, 1)

            def main_scores(it, s, h):
                n = 64 * it + 4 * s + 2 * h
                q, kt, b = s // NT, s % NT, 2 * (it % 2) + h
                if n >= NST:
                    pe.wait_ge(e_ready, n - NST + 1)
                keys, queries = slice(kt * P, (kt + 1) * P), slice(q * HALF, (q + 1) * HALF)
                at = 32 * (it % 2)
                passes(st[n % NST][:, :], [
                    (kh[:, b, keys], qh[:, b, queries]), (kh[:, b, keys], ql[:, b, queries]),
                    (kl[:, b, keys], qh[:, b, queries]), (sel[at:at + 2, h * P:(h + 1) * P], mr[at:at + 2, queries]),
                ], st_ready)

            def pattern_scores(it, s, x):
                n = 64 * it + 4 * s + 2 * x + 1
                if n >= NST:
                    pe.wait_ge(e_ready, n - NST + 1)
                hh, kt = 2 * (s % 2) + x, s // 2
                rows = slice(64 * x, 64 * x + 3 * PD + 1)
                passes(st[n % NST][:, :], [(pk[rows, it % 2, hh // 2, kt * P:(kt + 1) * P],
                                          pq[rows, it % 2, hh // 2, :])], st_ready)

            def main_values(it, s):
                q, kt = s // NT, s % NT
                if kt == 0 and (it or q):
                    pe.wait_ge(ctx_out, 2 * it + q)
                for h in range(2):
                    pe.wait_ge(e_ready, 64 * it + 4 * s + 2 * h + 1)
                    pe.matmul(pvm[64 * h:64 * h + 64, :], cdup[:, kt, 0:LAT], em[:, (2 * s + h) % 8, :],
                              start=(kt == 0), stop=(kt == NT - 1)).then_inc(pvm_done, 1)

            def pattern_values(it, kt):
                if kt == 0:
                    pe.wait_ge(vp_in[it % 2], 16 * (it // 2 + 1))
                    if it:
                        pe.wait_ge(pat_out, it)
                pe.wait_ge(e_ready, 64 * it + 4 * (2 * kt + 1) + 4)
                for hh in range(4):
                    mm = pe.matmul(pvp[32 * hh:32 * hh + 32, :], vp[:, it % 2, kt, hh, :], ep[:, (4 * kt + hh) % 8, :],
                                   start=(kt == 0), stop=(kt == NT - 1))
                mm.then_inc(pvp_done, 1)

            def x_tile(v, tile):
                kind, i = tile
                n = x_index[(v, *tile)]
                out, b = x_bank(v, tile), v % 2
                before = max((m for m in range(max(n - NX - NST, 0), n) if ring_place(m) == ring_place(n)), default=None)
                if before is not None:
                    x_emptied(pe, *x_tiles[before])
                if kind == "P":
                    if i == 0:
                        pe.wait_ge(wst_in[v % 2], 16 * (v // 2 + 1))
                    w = [wst[:, b, c, :] for c in range(NW)]
                    if i < 4:
                        half = slice((i // 2) * HALF, (i // 2 + 1) * HALF)
                        o = 4 * (i % 2)
                        qm0h, qm0l, qm1 = g["qm0h"][:, half], g["qm0l"][:, half], g["qm1"]
                        passes(out[:, :], [(w[o], qm0h), (w[o + 1], qm0h), (w[o], qm0l), (w[o + 2], qm1[:, half]),
                                           (w[o + 3][0:64, :], qm1[0:64, half])], x_ready)
                    else:
                        half = slice((i - 4) * HALF, (i - 3) * HALF)
                        pairs = []
                        for k in range(NK):
                            xh, xl = g["xh"][:, k, half], g["xl"][:, k, half]
                            pairs += [(w[8 + 2 * k], xh), (w[9 + 2 * k], xh), (w[8 + 2 * k], xl)]
                        passes(out[:, :], pairs, x_ready)
                elif kind == "pm":
                    if i == 0:
                        if v == 0:
                            pe.wait_ge(init, 6)
                        if v == 1:
                            pe.wait_ge(init_odd, 2)
                        pe.wait_ge(stack_in[v % 2], 16 * NSTACK * (v // 2 + 1))
                    hh, kt, t = i % 4, i // 4 % 2, i // 8
                    rows = slice(64 * (hh % 2), 64 * (hh % 2) + 3 * PD)
                    passes(out[:, :], [(pq[rows, b, hh // 2, t * P:(t + 1) * P],
                                        pk[rows, b, hh // 2, kt * HALF:(kt + 1) * HALF])], x_ready)
                elif kind == "mm":
                    if i == 0:
                        pe.wait_ge(rope_hi, 8 * (v + 1))
                    q, h, t, kt = i // 16, i // 8 % 2, i // 2 % 4, i % 2
                    at = (4 * q + t) * P
                    b = (v - (i >= MM_LATE)) % 2
                    passes(out[:, :], [(qh[:, 2 * b + h, at:at + P],
                                        kh[:, 2 * b + h, kt * HALF:(kt + 1) * HALF])], x_ready)
                elif kind == "oT":
                    pe.wait_ge(ow_in, 32)
                    pe.wait_ge(spo_in, 32)
                    for j in range(4):
                        r, m = 2 * i + j // 2, j % 2
                        if i < 8:
                            src = o_nat[:, m, r * DV:(r + 1) * DV]
                        else:
                            src = spo_nat[m][:, 4 * (r - 16):4 * (r - 15), :].rearrange("p h e -> p (h e)")
                        mm = pe.transpose(out[:, j * P:(j + 1) * P], src, ident[:, :])
                    mm.then_inc(x_ready, 1)
                elif kind == "o":
                    if i == 0:
                        pe.wait_ge(ctx_back, 16 * (4 + PDIRECT + DIRECT))
                        pe.wait_ge(ctx_ready, 2 * NP - 1)
                        pe.wait_ge(pat_ready, NP - 1)
                    output_projection(pe, g, out, i).then_inc(x_ready, 1)
                elif kind == "vo":
                    x_emptied(pe, 0, ("oT", 9))
                    for j in range(2):
                        for h in range(2):
                            hd = 2 * (2 * i + j) + h
                            mm = pe.matmul(out[64 * h:64 * h + 64, j * HID:(j + 1) * HID], wv[:, hd, :], oT[:, hd, :],
                                           start=True, stop=True)
                    mm.then_inc(x_ready, 1)
                elif kind == "mT":
                    pair = v - 1 if i else v
                    pe.wait_ge(mm_ready, 2 * pair + i + 1)
                    for t in range(4):
                        mm = pe.matmul(out[0:2, t * P:(t + 1) * P], ms[:, i, t, :], ident[:, :], start=True, stop=True)
                    mm.then_inc(x_ready, 1)
                elif kind == "pT":
                    pe.wait_ge(pm_ready, v + 1)
                    for t in range(2):
                        mm = pe.matmul(out[0:4, t * P:(t + 1) * P], msp[:, 2 * i + t, :], ident[:, :],
                                       start=True, stop=True)
                    mm.then_inc(x_ready, 1)
                elif kind == "S":
                    it = v - 2 if i else v - 1
                    for h in range(2):
                        pe.wait_ge(added, adds(it, i, NT - 1, h))
                        mm = pe.matmul(out[64 * h:64 * h + 64, :], ones[:, :], acc[:, h, :], start=True, stop=True)
                    mm.then_inc(x_ready, 1)

            for v in slots:
                it = v - 1
                for s in range(NS):
                    tiles = iter(xs[v][s])
                    if 0 <= it < NP:
                        if v == 1 and s == 0:
                            x_emptied(pe, 0, ("mm", 19))
                        if s == 0:
                            pe.wait_ge(rope_lo, 8 * (it + 1))
                            x_emptied(pe, it, ("mT", 0))
                            pe.wait_ge(mrow_in, 64 * (it + 1))
                        if s == NT:
                            x_emptied(pe, v, ("mT", 1))
                        for x in range(2):
                            for scores in (main_scores, pattern_scores):
                                scores(it, s, x)
                                for tile in islice(tiles, 1):
                                    x_tile(v, tile)
                        if s:
                            main_values(it, s - 1)
                        if s >= 3 and s % 2:
                            pattern_values(it, (s - 3) // 2)
                    if v >= 2:
                        if s == 0:
                            main_values(v - 2, NS - 1)
                        if s == 1:
                            pattern_values(v - 2, NT - 1)
                    for tile in tiles:
                        x_tile(v, tile)



def context_tile(g, pair):
    if pair >= 6:
        return g["ql_f"][:, pair % 2, :]
    return g[("kh", "kl", "qh")[pair // 2]][:, pair % 2, :].bitcast(F32)


def pattern_tile(g, n):
    if n < NP - 2:
        return g["wst"][:, n // 3, 4 * (n % 3):4 * (n % 3) + 4, :].rearrange("p c j -> p (c j)").bitcast(F32)
    return g["raw"][:, n - (NP - 2), :]


def output_projection(pe, g, out, t):
    half, tq = divmod(t, 4)
    for j in range(NP):
        vo = g["rot" if j < 4 else "rc"][:, j // 2 % 2, j % 2 * HID:(j % 2 + 1) * HID]
        pe.matmul(out[:, 0:HID], context_tile(g, j)[:, t * P:(t + 1) * P], vo, start=(j == 0), stop=(j == NP - 1))
    for j in range(4):
        mm = pe.matmul(out[:, HID:2 * HID], pattern_tile(g, 2 * j + half)[:, tq * P:(tq + 1) * P],
                       g["spoT"][:, j, :], start=(j == 0), stop=(j == 3))
    return mm


def epilogue(nc, a, d, g, out):
    order = [(0, 0), (1, 0), (0, 1), (1, 1), (2, 0), (2, 1)]
    jobs = [("o", t) for t in range(4, NT - 1)] + [("xT", k, 0) for k in range(NK)] + [("o", NT - 1)]
    jobs += [("up", 0, m) for m in range(8)] + [("down", 0, m) for m in range(2)]
    jobs += [("xT", k, 1) for k in range(NK)] + [("up", 1, m) for m in range(8)]
    jobs += [("yT", j) for j in range(2)] + [("down", 1, m) for m in range(2)]
    jobs += [("yT", 2 + j) for j in range(2)]
    index = {j: n for n, j in enumerate(jobs)}
    by_act = [j[0] in ("up", "down") for j in jobs]

    with ExitStack() as ctx:
        def sb(name, shape, dt=F32):
            return ctx.enter_context(nc.sbuf_tensor(name, shape, dt))

        def sem(name):
            return ctx.enter_context(nc.semaphore(name))

        bank = [ctx.enter_context(nc.psum_tensor(f"c_bank{i}", [P, HALF], F32)) for i in range(8)]
        wup, wdn = g["xh"], g["xl"][:, :, :].rearrange("p a b -> p (a b)").rearrange("p (k n) -> p k n", n=HID)
        hhi = [g[t][:, 2 + i, h * HALF:(h + 1) * HALF] for t in ("kh", "kl") for i in range(2) for h in range(2)]
        hlo = [g[t][:, 2 + i, h * HALF:(h + 1) * HALF] for t in ("qh", "ql") for i in range(2) for h in range(2)]
        res = sb("res", [P, NT, HID])
        x2h = sb("x2h", [P, NK, S], F32R)
        x2l = sb("x2l", [P, NK, S], F32R)
        NHF = 4
        hf = sb("hf", [P, NHF, HALF])
        yT = sb("yT", [P, 2, HALF])
        ya = sb("ya", [P, 4, HID])
        yf = sb("yf", [P, 4, HID])
        x2 = sb("x2", [P, NT, HID])
        ub = sb("ub", [P, 8])
        db = sb("db", [P, 2])
        stats = sb("c_stats", [P, NT, 6])
        mv = sb("c_mv", [P, 3, NT, 2])
        rstd = sb("c_rstd", [P, 3, NT])
        ident, gates, stash = g["ident"], g["gates"], g["em"]

        res_in = sem("res_in")
        bias_in = sem("bias_in")
        pe_job = sem("c_pe_job")
        ev_act = sem("c_ev_act")
        ev_dve = sem("c_ev_dve")
        own = sem("c_own")
        var_ready = sem("var_ready")
        rstd_ready = sem("c_rstd_ready")
        x2_ready = sem("x2_ready")
        pool_own = sem("c_pool_own")
        x2_hi = sem("x2_hi")
        h_hi = sem("h_hi")
        h_lo = [sem(f"h_lo{i}") for i in range(2)]
        y_ready = sem("y_ready")
        stored = sem("stored")

        def evacuated(eng, n):
            for s, flag in ((ev_act, True), (ev_dve, False)):
                count = sum(b == flag for b in by_act[:n + 1])
                if count:
                    eng.wait_ge(s, count)

        block = ctx.enter_context(nc.Block())

        @block.sync
        def _(sp):
            sp.dma_start(res[:, :, :], a["x"].rearrange("b (t p) n -> p (b t) n", p=P)).then_inc(res_in, 16)
            sp.dma_start(ub[:, :], a["up_bias"]).then_inc(bias_in, 16)
            sp.dma_start(db[:, :], a["down_bias"]).then_inc(bias_in, 16)
            o = out.rearrange("b (t p) n -> p (b t) n", p=P)
            for t in range(NT):
                sp.wait_ge(y_ready, t + 1)
                sp.dma_start(o[:, t, :], x2[:, t, :]).then_inc(stored, 16)
            sp.wait_ge(stored, 16 * NT)

        @block.gpsimd
        def _(pool):
            def root(n):
                kind, q = order[n]
                four = rstd[:, kind, 4 * q:4 * q + 4]
                pool.wait_ge(var_ready, n + 1)
                pool.tensor_scalar(four, mv[:, kind, 4 * q:4 * q + 4, 1], 1e-5, None, ALU.add).then_inc(pool_own, 1)
                pool.wait_ge(pool_own, n + 1)
                pool.tensor_tensor(four, four, g["mhalf"][:, 0:4], ALU.pow).then_inc(rstd_ready, 1)

            def lo_of_gelu(q, m):
                pool.wait_ge(h_hi, 8 * q + m + 1)
                pool.tensor_tensor(hlo[m], hf[:, m % NHF, :], hhi[m].bitcast(F32), ALU.subtract).then_inc(h_lo[1], 1)

            root(0)
            root(1)
            lo_of_gelu(0, 1)
            root(2)
            lo_of_gelu(0, 3)
            lo_of_gelu(0, 5)
            root(3)
            lo_of_gelu(0, 7)
            for m in (1, 3, 5, 7):
                lo_of_gelu(1, m)
            root(4)
            root(5)

        @block.tensor
        def _(pe):
            def transposes(n, blocks):
                for j, src in enumerate(blocks):
                    mm = pe.transpose(bank[n % 8][:, j * P:(j + 1) * P], src, ident[:, :])
                mm.then_inc(pe_job, 1)

            for n, job in enumerate(jobs):
                kind, o = job[0], bank[n % 8]
                if n >= 8:
                    evacuated(pe, n - 8)
                if kind == "o":
                    output_projection(pe, g, o, job[1]).then_inc(pe_job, 1)
                elif kind == "xT":
                    k, q = job[1:]
                    pe.wait_ge(x2_ready, q + 1)
                    transposes(n, [x2[:, 4 * q + j, k * P:(k + 1) * P] for j in range(4)])
                elif kind == "up":
                    q, m = job[1:]
                    half = slice(q * HALF, (q + 1) * HALF)
                    evacuated(pe, index[("xT", 1, q)])
                    for i, (k, x) in enumerate([(k, x) for k in range(NK) for x in (x2h, x2l)]):
                        mm = pe.matmul(o[:, :], wup[:, k, m * P:(m + 1) * P], x[:, k, half], start=(i == 0), stop=(i == 3))
                    mm.then_inc(pe_job, 1)
                elif kind == "down":
                    q, m = job[1:]
                    for k in range(8):
                        if m == 0:
                            pe.wait_ge(h_lo[k % 2], 4 * q + k // 2 + 1)
                        pe.matmul(o[:, :], wdn[:, k, m * P:(m + 1) * P], hhi[k], start=(k == 0), stop=False)
                        mm = pe.matmul(o[:, :], wdn[:, k, m * P:(m + 1) * P], hlo[k], start=False, stop=(k == 7))
                    mm.then_inc(pe_job, 1)
                elif kind == "yT":
                    q, j = divmod(job[1], 2)
                    pe.wait_ge(ev_act, sum(by_act[:index[("down", q, 1)] + 1]))
                    transposes(n, [yT[:, m, (2 * j + t) * P:(2 * j + t + 1) * P] for t in range(2) for m in range(2)])

        @block.scalar
        def _(act):
            ups = 0
            act.wait_ge(bias_in, 32)
            for n, job in enumerate(jobs):
                kind, o = job[0], bank[n % 8]
                if kind in ("o", "yT"):
                    continue
                act.wait_ge(pe_job, n + 1)
                if kind == "xT":
                    k, q = job[1:]
                    act.activation(x2h[:, k, q * HALF:(q + 1) * HALF], o[:, :], ACT.Copy).then_inc(x2_hi, 1)
                elif kind == "up":
                    q, m = job[1:]
                    if ups >= NHF:
                        t = ups - NHF
                        act.wait_ge(h_hi, t + 1)
                        act.wait_ge(h_lo[t % 2], t // 2 + 1)
                    act.activation(hf[:, m % NHF, :], o[:, :], ACT.Gelu_apprx_tanh, bias=ub[:, m:m + 1]).then_inc(ev_act, 1)
                    ups += 1
                elif kind == "down":
                    q, m = job[1:]
                    if q:
                        act.wait_ge(pe_job, index[("yT", 1)] + 1)
                    act.activation(yT[:, m, :], o[:, :], ACT.Identity, bias=db[:, m:m + 1]).then_inc(ev_act, 1)

        @block.vector
        def _(dve):
            count = [0]

            def link(ins):
                count[0] += 1
                ins.then_inc(own, 1)
                dve.wait_ge(own, count[0])

            def statistics(kind, q, srcs):
                for t in range(4):
                    ins = dve.bn_stats(stats[:, 4 * q + t, :], srcs[t])
                link(ins)
                for t in range(4):
                    ins = dve.bn_aggr(mv[:, kind, 4 * q + t, :], stats[:, 4 * q + t, :])
                ins.then_inc(var_ready, 1)

            def normalise(kind, q, dsts, srcs):
                dve.wait_ge(rstd_ready, order.index((kind, q)) + 1)
                for t in range(4):
                    ins = dve.tensor_scalar(dsts[t], srcs[t], mv[:, kind, 4 * q + t, 0:1],
                                            rstd[:, kind, 4 * q + t:4 * q + t + 1], ALU.subtract, ALU.mult)
                return ins

            def tiles(t, q):
                return [t[:, 4 * q + i, :] for i in range(4)]

            def mix(tiles):
                for stage in range(2):
                    for t in tiles:
                        n = index.get(("o", t))
                        o = stash[:, t, :] if n is None else bank[n % 8]
                        if stage == 0:
                            if n is not None:
                                dve.wait_ge(pe_job, n + 1)
                            ins = dve.tensor_scalar(ya[:, t % 4, :], o[:, HID:2 * HID], gates[:, t, 1:2], None, ALU.mult)
                            continue
                        ins = dve.scalar_tensor_tensor(ya[:, t % 4, :], o[:, 0:HID], gates[:, t, 0:1], ya[:, t % 4, :],
                                                       ALU.mult, ALU.add)
                        if n is not None:
                            ins.then_inc(ev_dve, 1)
                    if stage == 0:
                        link(ins)
                if n is None:
                    link(dve.engine_nop())
                else:
                    dve.wait_ge(ev_dve, sum(not b for b in by_act[:n + 1]))

            def attention_norm(q, stage):
                if stage == 0:
                    statistics(0, q, tiles(ya, 0))
                elif stage == 1:
                    link(normalise(0, q, tiles(ya, 0), tiles(ya, 0)))
                elif stage == 2:
                    if q == 0:
                        dve.wait_ge(res_in, 16)
                    r = res[:, 4 * q:4 * q + 4, :]
                    link(dve.tensor_tensor(r, r, ya[:, :, :], ALU.add))
                elif stage == 3:
                    statistics(1, q, tiles(res, q))
                elif stage == 4:
                    normalise(1, q, tiles(x2, q), tiles(res, q)).then_inc(x2_ready, 1)

            def final_norm(q, stage):
                banks = [bank[index[("yT", 2 * q + j)] % 8] for j in range(2)]
                srcs = [banks[t // 2][:, t % 2 * HID:(t % 2 + 1) * HID] for t in range(4)]
                if stage == 0:
                    dve.wait_ge(pe_job, index[("yT", 2 * q + 1)] + 1)
                    statistics(2, q, srcs)
                elif stage == 1:
                    normalise(2, q, tiles(yf, 0), srcs).then_inc(ev_dve, 1)
                    evacuated(dve, index[("yT", 2 * q)])
                    dve.engine_nop().then_inc(ev_dve, 1)
                elif stage == 2:
                    for t in range(4):
                        dve.tensor_tensor(x2[:, 4 * q + t, :], res[:, 4 * q + t, :], yf[:, t, :],
                                          ALU.add).then_inc(y_ready, 1)

            def lo_of_input(q):
                for k in range(NK):
                    n = index[("xT", k, q)]
                    half = slice(q * HALF, (q + 1) * HALF)
                    dve.wait_ge(x2_hi, 2 * q + k + 1)
                    dve.tensor_tensor(x2l[:, k, half], bank[n % 8][:, :], x2h[:, k, half].bitcast(F32),
                                      ALU.subtract).then_inc(ev_dve, 1)

            def split_gelu(q, m):
                n = 8 * q + m + 1
                dve.wait_ge(ev_act, sum(by_act[:index[("up", q, m)] + 1]))
                if q and m == 0:
                    dve.wait_ge(pe_job, index[("down", 0, 1)] + 1)
                dve.tensor_copy(hhi[m], hf[:, m % NHF, :]).then_inc(h_hi, 1)
                if m % 2 == 0:
                    dve.wait_ge(h_hi, n)
                    dve.tensor_tensor(hlo[m], hf[:, m % NHF, :], hhi[m].bitcast(F32), ALU.subtract).then_inc(h_lo[0], 1)

            mix(range(4))
            for stage in range(5):
                attention_norm(0, stage)
            for t in range(4, NT - 1):
                mix([t])
            lo_of_input(0)
            mix([NT - 1])
            for m in range(8):
                split_gelu(0, m)
                if m in (1, 2, 3, 5, 7):
                    attention_norm(1, (1, 2, 3, 5, 7).index(m))
            lo_of_input(1)
            for m in range(8):
                split_gelu(1, m)
            for q in range(2):
                for stage in range(3):
                    final_norm(q, stage)


NAMES = {
    "x": "L0_attn_hidden_states", "q_a_w": "L0_attn_q_a_w", "q_a_ln_w": "L0_attn_q_a_ln_w",
    "q_b_w": "L0_attn_q_b_w", "kv_a_w": "L0_attn_kv_a_w", "kv_a_ln_w": "L0_attn_kv_a_ln_w",
    "kv_b_w": "L0_attn_kv_b_w", "o_w": "L0_attn_o_w", "sp_q_w": "L0_attn_sp_q_w",
    "sp_k_w": "L0_attn_sp_k_w", "sp_v_w": "L0_attn_sp_v_w", "sp_o_w": "L0_attn_sp_o_w",
    "gate_w": "L0_attn_gate_w", "gate_b": "L0_attn_gate_b", "ffn_up": "L0_ffn_up_kernel",
    "up_bias": "L0_ffn_up_bias", "ffn_down": "L0_ffn_down_kernel", "down_bias": "L0_ffn_down_bias",
}


def build(nc, a, out):
    def scratch(name, shape, dt=F32):
        return nc.dram_tensor(name, shape, dt, kind="Internal").ap()

    d = {
        "wst": scratch("wst_d", (NP, P, NW * P)),
        "spqk": scratch("spqk_d", (2, 2, HID, S)),
        "vp": scratch("vp_d", (4, P, NT * 64)),
        "ctx": scratch("ctx_d", (NP, P, S)),
        "pat": scratch("pat_d", (NP, P, HALF)),
        "vo": scratch("vo_d", (4, P, HALF)),
    }
    with ExitStack() as ctx:
        def sb(name, shape, dt=F32):
            return ctx.enter_context(nc.sbuf_tensor(name, shape, dt))

        g = {"ident": sb("ident", [P, P]), "gates": sb("gates", [P, NT, 2]), "mhalf": sb("mhalf", [P, 2 * NT])}
        with ExitStack() as inner:
            def sbi(name, shape, dt=F32):
                return inner.enter_context(nc.sbuf_tensor(name, shape, dt))

            def two_types(shapes):
                with ExitStack() as before:
                    plain = {n + "_f": before.enter_context(nc.sbuf_tensor(n + "_f", shape, F32))
                             for n, shape in shapes.items()}
                return plain | {n: sbi(n, shape, F32R) for n, shape in shapes.items()}

            g |= two_types({"qm0h": [P, S], "qm0l": [P, S], "qm1": [P, S]})
            g |= {
                "sel_f": sbi("sel_f", [64, 256]), "sel": sbi("sel", [64, 256], F32R),
                "cos": sbi("cos", [P, S]), "sin": sbi("sin", [P, S]),
                "cdup": sbi("cdup", [P, NT, P]),
                "xh": sbi("xh", [P, NK, S], F32R), "xl": sbi("xl", [P, NK, S], F32R),
                "kh": sbi("kh", [P, 4, S], F32R), "kl": sbi("kl", [P, 4, S], F32R),
            }
            prologue(nc, a, d, g)
            g |= two_types({"ql": [P, 4, S]})
            g |= {
                "qh": sbi("qh", [P, 4, S], F32R), "wst": sbi("wst", [P, 2, NW, P], F32R),
                "raw": sbi("raw", [P, 2, HALF]), "rot": sbi("rot", [P, 2, HALF]), "rc": sbi("rc", [P, 2, HALF]),
                "em": sbi("em", [P, 8, HALF]), "spoT": sbi("spoT", [P, 4, HID]),
            }
            attention(nc, a, d, g)
            epilogue(nc, a, d, g, out)



def constants():
    consts = np.zeros((P, P + 256), np.float32)
    consts[:, 0:P] = np.eye(P, dtype=np.float32)
    for b in (0, 32):
        for h in range(2):
            consts[b + h, P + h * P:P + (h + 1) * P] = -1.0
    f32 = np.float32
    inv_freq = f32(1.0) / np.power(f32(10000.0), np.arange(0, ROPE, 2, dtype=f32) / f32(ROPE))
    angle = np.outer(inv_freq, np.arange(S, dtype=f32)).astype(f32)
    c, s = np.cos(angle), np.sin(angle)
    rope = np.stack([np.concatenate([c] * 4), np.concatenate([-s, s] * 2)]).astype(f32)
    return consts, rope


def kernel(**inputs):
    import concourse.bacc as bacc
    from concourse.bass_utils import run_bass_kernel_spmd

    nc = bacc.Bacc("TRN2", target_bir_lowering=False, num_devices=1, dynamic_dma_scratch_size=1024)
    arrays, aps = {}, {}
    for short, name in NAMES.items():
        v = np.ascontiguousarray(inputs[name])
        if short in ("up_bias", "down_bias"):
            v = np.ascontiguousarray(v.reshape(-1, P).T)
        arrays[f"in_{short}"] = v
    arrays["in_consts"], arrays["in_rope"] = constants()
    for key, v in arrays.items():
        aps[key[3:]] = nc.dram_tensor(key, v.shape, F32, kind="ExternalInput").ap()
    out = nc.dram_tensor("out_0", (1, S, HID), F32, kind="ExternalOutput").ap()
    build(nc, aps, out)
    r = run_bass_kernel_spmd(nc, [arrays], core_ids=[0])
    return r.results[0]["out_0"]
```
